# Optimizing a Trainium2 kernel written in Bass

```python
import numpy as np
import jax
import jax.numpy as jnp

def _softmax(x, axis=-1):
    return jax.nn.softmax(x, axis=axis)

def _gelu(x):
    return jax.nn.gelu(x, approximate=True)

def _silu(x):
    return jax.nn.silu(x)

def _sigmoid(x):
    return jax.nn.sigmoid(x)

def _layernorm(x, axis=-1, eps=1e-05):
    m = jnp.mean(x, axis=axis, keepdims=True)
    v = jnp.var(x, axis=axis, keepdims=True)
    return (x - m) / jnp.sqrt(v + eps)

def _scatter_add(tgt, idx, src, axis=0):
    return tgt.at[idx].add(src)

def _segment_sum(src, seg, n):
    return jax.ops.segment_sum(src, seg, n)
kernel_name = 'mk_recurrent_d2_jaxref_r8_09fd78'

def setup_inputs(seed: int=0):
    np.random.seed(seed)
    _w = jnp.asarray

    def _L0_attn_setup():
        import jax, jax.numpy as jnp
        import numpy as np
        B, T, D = (2, 256, 256)
        H, G = (32, 8)
        HD = D // H
        GROUP = H // G
        ROPE_BASE = 10000.0

        def _apply_rope(x):
            t = x.shape[2]
            half = HD // 2
            inv_freq = 1.0 / ROPE_BASE ** (jnp.arange(half, dtype=jnp.float32) * 2.0 / HD)
            ang = jnp.arange(t, dtype=jnp.float32)[:, None] * inv_freq[None, :]
            cos, sin = (jnp.cos(ang), jnp.sin(ang))
            x1, x2 = (x[..., :half], x[..., half:])
            out = jnp.concatenate([x1 * cos - x2 * sin, x2 * cos + x1 * sin], axis=-1)
            return out.astype(x.dtype)
        key = jax.random.key(seed)
        kx, kq, kk, kv, ko = jax.random.split(key, 5)
        scale = 0.02
        x = jax.random.normal(kx, (B, T, D), dtype=jnp.float32)
        Wq = jax.random.normal(kq, (D, D), dtype=jnp.float32) * scale
        Wk = jax.random.normal(kk, (D, G * HD), dtype=jnp.float32) * scale
        Wv = jax.random.normal(kv, (D, G * HD), dtype=jnp.float32) * scale
        Wo = jax.random.normal(ko, (D, D), dtype=jnp.float32) * scale
        return {'x': x, 'Wq': Wq, 'Wk': Wk, 'Wv': Wv, 'Wo': Wo}
    _L0_attn_in = _L0_attn_setup()

    def _L0_ffn_setup():
        import jax, jax.numpy as jnp
        import numpy as np
        ALPHA = 1.702
        LIMIT = 7.0
        EPS = 1e-05
        TOP_K = 4
        key = jax.random.key(seed)
        ks = jax.random.split(key, 8)
        B, S, H, I, E = (2, 64, 256, 256, 16)
        return {'x': jax.random.normal(ks[0], (B, S, H), jnp.float32), 'norm_w': jnp.ones((H,), jnp.float32), 'gate_w': jax.random.normal(ks[1], (E, H), jnp.float32) * 0.02, 'gate_b': jax.random.normal(ks[2], (E,), jnp.float32) * 0.02, 'w1': jax.random.normal(ks[3], (E, 2 * I, H), jnp.float32) * 0.02, 'b1': jax.random.normal(ks[4], (E, 2 * I), jnp.float32) * 0.02, 'w2': jax.random.normal(ks[5], (E, H, I), jnp.float32) * 0.02, 'b2': jax.random.normal(ks[6], (E, H), jnp.float32) * 0.02}
    _L0_ffn_in = _L0_ffn_setup()

    def _L1_attn_setup():
        import jax, jax.numpy as jnp
        import numpy as np
        B, S, D = (4, 256, 256)
        H = 16
        HD = D // H
        key = jax.random.key(seed)
        ks = jax.random.split(key, 5)
        scale = 1.0 / np.sqrt(D)
        return {'x': jax.random.normal(ks[0], (B, S, D), dtype=jnp.float32), 'wq': jax.random.normal(ks[1], (D, D), dtype=jnp.float32) * scale, 'wk': jax.random.normal(ks[2], (D, D), dtype=jnp.float32) * scale, 'wv': jax.random.normal(ks[3], (D, D), dtype=jnp.float32) * scale, 'wo': jax.random.normal(ks[4], (D, D), dtype=jnp.float32) * scale}
    _L1_attn_in = _L1_attn_setup()

    def _L1_ffn_setup():
        import jax, jax.numpy as jnp
        import numpy as np
        DIM = 256
        HID = 704
        ZERO_POINT = 128.0

        def _qlinear(x, wq, scale):
            W = (wq.astype(jnp.float32) - ZERO_POINT) * scale[:, None]
            return jnp.einsum('bsd,hd->bsh', x, W)
        key = jax.random.key(seed)
        ks = jax.random.split(key, 7)
        B, S = (4, 256)
        sg = jax.random.uniform(ks[1], (HID,)) * (0.02 / np.sqrt(DIM)) + 0.0001
        su = jax.random.uniform(ks[3], (HID,)) * (0.02 / np.sqrt(DIM)) + 0.0001
        sd = jax.random.uniform(ks[5], (DIM,)) * (0.02 / np.sqrt(HID)) + 0.0001
        return {'x': jax.random.normal(ks[0], (B, S, DIM), dtype=jnp.float32), 'wq_gate': jax.random.randint(ks[2], (HID, DIM), 0, 32, dtype=jnp.int32), 's_gate': sg, 'wq_up': jax.random.randint(ks[4], (HID, DIM), 0, 32, dtype=jnp.int32), 's_up': su, 'wq_down': jax.random.randint(ks[6], (DIM, HID), 0, 32, dtype=jnp.int32), 's_down': sd}
    _L1_ffn_in = _L1_ffn_setup()
    _d = {'L0_attn_x': _L0_attn_in['x'], 'L0_attn_Wq': _L0_attn_in['Wq'], 'L0_attn_Wk': _L0_attn_in['Wk'], 'L0_attn_Wv': _L0_attn_in['Wv'], 'L0_attn_Wo': _L0_attn_in['Wo'], 'L0_ffn_norm_w': _L0_ffn_in['norm_w'], 'L0_ffn_gate_w': _L0_ffn_in['gate_w'], 'L0_ffn_gate_b': _L0_ffn_in['gate_b'], 'L0_ffn_w1': _L0_ffn_in['w1'], 'L0_ffn_b1': _L0_ffn_in['b1'], 'L0_ffn_w2': _L0_ffn_in['w2'], 'L0_ffn_b2': _L0_ffn_in['b2'], 'L1_attn_wq': _L1_attn_in['wq'], 'L1_attn_wk': _L1_attn_in['wk'], 'L1_attn_wv': _L1_attn_in['wv'], 'L1_attn_wo': _L1_attn_in['wo'], 'L1_ffn_wq_gate': _L1_ffn_in['wq_gate'], 'L1_ffn_s_gate': _L1_ffn_in['s_gate'], 'L1_ffn_wq_up': _L1_ffn_in['wq_up'], 'L1_ffn_s_up': _L1_ffn_in['s_up'], 'L1_ffn_wq_down': _L1_ffn_in['wq_down'], 'L1_ffn_s_down': _L1_ffn_in['s_down']}
    _x0 = _d['L0_attn_x']
    _d['L0_attn_x'] = jax.random.normal(jax.random.fold_in(jax.random.key(seed), 1), (8, 256, 256), dtype=_x0.dtype)
    del _x0
    return _d

def reference(L0_attn_x, L0_attn_Wq, L0_attn_Wk, L0_attn_Wv, L0_attn_Wo, L0_ffn_norm_w, L0_ffn_gate_w, L0_ffn_gate_b, L0_ffn_w1, L0_ffn_b1, L0_ffn_w2, L0_ffn_b2, L1_attn_wq, L1_attn_wk, L1_attn_wv, L1_attn_wo, L1_ffn_wq_gate, L1_ffn_s_gate, L1_ffn_wq_up, L1_ffn_s_up, L1_ffn_wq_down, L1_ffn_s_down):

    def _L0_attn_ref(x, Wq, Wk, Wv, Wo):
        import jax, jax.numpy as jnp
        import numpy as np
        B, T, D = (2, 256, 256)
        H, G = (32, 8)
        HD = D // H
        GROUP = H // G
        ROPE_BASE = 10000.0

        def _apply_rope(x):
            t = x.shape[2]
            half = HD // 2
            inv_freq = 1.0 / ROPE_BASE ** (jnp.arange(half, dtype=jnp.float32) * 2.0 / HD)
            ang = jnp.arange(t, dtype=jnp.float32)[:, None] * inv_freq[None, :]
            cos, sin = (jnp.cos(ang), jnp.sin(ang))
            x1, x2 = (x[..., :half], x[..., half:])
            out = jnp.concatenate([x1 * cos - x2 * sin, x2 * cos + x1 * sin], axis=-1)
            return out.astype(x.dtype)
        b, t, _ = x.shape
        q = (x @ Wq).reshape(b, t, H, HD).transpose(0, 2, 1, 3)
        k = (x @ Wk).reshape(b, t, G, HD).transpose(0, 2, 1, 3)
        v = (x @ Wv).reshape(b, t, G, HD).transpose(0, 2, 1, 3)
        q = _apply_rope(q)
        k = _apply_rope(k)
        k = jnp.repeat(k, GROUP, axis=1)
        v = jnp.repeat(v, GROUP, axis=1)
        scores = jnp.einsum('bhqd,bhkd->bhqk', q, k)
        causal = jnp.triu(jnp.ones((t, t), dtype=bool), k=1)
        scores = jnp.where(causal, -jnp.inf, scores)
        attn = jax.nn.softmax(scores / jnp.sqrt(jnp.float32(HD)), axis=-1)
        ctx = jnp.einsum('bhqk,bhkd->bhqd', attn, v)
        ctx = jnp.swapaxes(ctx, -2, -1).reshape(b, t, D)
        return ctx @ Wo

    def _L0_ffn_ref(x, norm_w, gate_w, gate_b, w1, b1, w2, b2):
        import jax, jax.numpy as jnp
        import numpy as np
        ALPHA = 1.702
        LIMIT = 7.0
        EPS = 1e-05
        TOP_K = 4
        B, S, H = x.shape
        M = B * S
        E = gate_w.shape[0]
        xf = x.reshape(M, H)
        t = xf * jax.lax.rsqrt(jnp.mean(xf * xf, axis=-1, keepdims=True) + EPS) * norm_w
        logits = t @ gate_w.T + gate_b
        vals, idx = jax.lax.top_k(logits, TOP_K)
        gates_k = jax.nn.softmax(vals, axis=-1)
        G = jnp.zeros((M, E), x.dtype).at[jnp.arange(M)[:, None], idx].set(gates_k)
        h = jnp.einsum('mh,eoh->emo', t, w1) + b1[:, None, :]
        a = jnp.minimum(h[..., ::2], LIMIT)
        b = jnp.clip(h[..., 1::2], -LIMIT, LIMIT)
        act = a * jax.nn.sigmoid(ALPHA * a) * (b + 1.0)
        y = jnp.einsum('emi,edi->emd', act, w2) + b2[:, None, :]
        delta = jnp.einsum('me,emd->md', G, y)
        return x + delta.reshape(B, S, H)

    def _L1_attn_ref(x, wq, wk, wv, wo):
        import jax, jax.numpy as jnp
        import numpy as np
        B, S, D = (4, 256, 256)
        H = 16
        HD = D // H
        b, s, d = x.shape
        q = (x @ wq.T).reshape(b, s, H, HD).transpose(0, 2, 1, 3)
        k = (x @ wk.T).reshape(b, s, H, HD).transpose(0, 2, 1, 3)
        v = (x @ wv.T).reshape(b, s, H, HD).transpose(0, 2, 1, 3)
        scores = jnp.einsum('bhqd,bhkd->bhqk', q, k) / np.sqrt(HD)
        causal = jnp.tril(jnp.ones((s, s), dtype=bool))
        scores = jnp.where(causal, scores, -jnp.inf)
        prob = jax.nn.softmax(scores, axis=-1)
        out = jnp.einsum('bhqk,bhkd->bhqd', prob, v)
        out = out.transpose(0, 2, 1, 3).reshape(b, s, d)
        return out @ wo.T

    def _L1_ffn_ref(x, wq_gate, s_gate, wq_up, s_up, wq_down, s_down):
        import jax, jax.numpy as jnp
        import numpy as np
        DIM = 256
        HID = 704
        ZERO_POINT = 128.0

        def _qlinear(x, wq, scale):
            W = (wq.astype(jnp.float32) - ZERO_POINT) * scale[:, None]
            return jnp.einsum('bsd,hd->bsh', x, W)
        gate = _qlinear(x, wq_gate, s_gate)
        gate = jax.nn.silu(gate)
        up = _qlinear(x, wq_up, s_up)
        return _qlinear(gate * up, wq_down, s_down)
    x = L0_attn_x
    xn = _layernorm(x, axis=-1)
    s = _L0_attn_ref(xn, L0_attn_Wq, L0_attn_Wk, L0_attn_Wv, L0_attn_Wo)
    g = _silu(_L0_ffn_ref(xn, L0_ffn_norm_w, L0_ffn_gate_w, L0_ffn_gate_b, L0_ffn_w1, L0_ffn_b1, L0_ffn_w2, L0_ffn_b2))
    x = x + s * g
    xn = _layernorm(x, axis=-1)
    s = _L1_attn_ref(xn, L1_attn_wq, L1_attn_wk, L1_attn_wv, L1_attn_wo)
    g = _silu(_L1_ffn_ref(xn, L1_ffn_wq_gate, L1_ffn_s_gate, L1_ffn_wq_up, L1_ffn_s_up, L1_ffn_wq_down, L1_ffn_s_down))
    x = x + s * g
    return x

_drawn_inputs = setup_inputs


def setup_inputs(seed=0):
    import zlib

    import numpy as np

    out = dict(_drawn_inputs(seed))
    spreads = {'L0_ffn_norm_w': (1.0, 0.6)}
    factors = {'L0_attn_Wq': 8.0,
     'L0_attn_Wk': 8.0,
     'L0_attn_Wv': 5.838,
     'L0_attn_Wo': 6.106,
     'L0_ffn_gate_w': 8.0,
     'L0_ffn_gate_b': 8.0,
     'L0_ffn_w1': 8.0,
     'L0_ffn_b1': 8.0,
     'L0_ffn_w2': 8.0,
     'L0_ffn_b2': 8.0,
     'L1_attn_wq': 8.0,
     'L1_attn_wk': 8.0,
     'L1_attn_wv': 8.0,
     'L1_attn_wo': 8.0,
     'L1_ffn_s_gate': 8.0,
     'L1_ffn_s_up': 8.0,
     'L1_ffn_s_down': 8.0}
    for name, (base, spread) in spreads.items():
        noise = np.random.default_rng([zlib.crc32(name.encode()), seed]).standard_normal(out[name].shape)
        drawn = base * np.exp(spread * noise) if base else spread * noise
        out[name] = jnp.asarray(drawn.astype(out[name].dtype))
    for name, factor in factors.items():
        out[name] = (out[name] * factor).astype(out[name].dtype)
    return out
```

```python
from contextlib import ExitStack

import numpy as np

import concourse.bass as bass
from concourse import mybir

ALU = mybir.AluOpType
ACT = mybir.ActivationFunctionType
AX = mybir.AxisListType
F32 = mybir.dt.float32
F32R = mybir.dt.float32r
BF16 = mybir.dt.bfloat16
I32 = mybir.dt.int32
U32 = mybir.dt.uint32

P = 128
B, T, D = 8, 256, 256
QT = T // P
KC = D // P
NT = B * QT
H0, G0, HD0 = 32, 8, 8
H1, HD1 = 16, 16
E, TOPK, I = 16, 4, 256
BLOCKS = 80
BPB = BLOCKS // B
HID = 704
HC = (HID + P - 1) // P
ROWS = [min(P, HID - c * P) for c in range(HC)]
EPS = 1e-5
BIG = float(2.0 ** 100)
ALPHA, LIMIT = 1.702, 7.0
NOT_A_LOGIT = -3.0e38
CHOSEN = 3.0e38


def build(nc, a, out):
    tokens = nc.dram_tensor("expert_tokens", [BLOCKS * P, 1], U32).ap()
    t_rows = nc.dram_tensor("normed_rows", [NT * P, D], F32).ap()
    y_rows = nc.dram_tensor("expert_rows", [BLOCKS * P, D], F32).ap()
    s_rows = nc.dram_tensor("attention_rows", [(NT + QT) * P, D], F32).ap()
    with ExitStack() as ctx:
        def sb(name, shape, dt=F32):
            return ctx.enter_context(nc.sbuf_tensor(name, shape, dt))

        m = {}
        m["x"] = sb("x", [P, NT, D])
        m["mean_rstd"] = sb("mean_rstd", [P, 2, NT])
        m["ident"] = sb("ident", [P, P])
        m["ident_bf"] = sb("ident_bf", [P, P], BF16)
        m["row_mask"] = sb("row_mask", [P, P], BF16)
        m["step"] = sb("step", [P, P], F32R)
        m["shift"] = sb("shift", [P, 2, 4, 3 * P], F32R)
        m["slots"] = sb("slots", [P, NT + QT, TOPK], U32)
        m["gates"] = sb("gates", [P, NT, TOPK])
        m["block_expert"] = sb("block_expert", [1, BLOCKS], I32)
        m["block_tokens"] = sb("block_tokens", [P, BLOCKS + 2], U32)
        m["bank"] = [ctx.enter_context(nc.psum_tensor(f"bank{i}", [P, 512], F32)) for i in range(8)]
        route(nc, a, m, tokens, t_rows)
        layer0(nc, a, m, t_rows, y_rows, s_rows)
        layer1(nc, a, m, y_rows, s_rows, out)


def sems(nc, ctx, names):
    return {n: ctx.enter_context(nc.semaphore(n)) for n in names}


class Chain:

    def __init__(self, eng, sem, base=0):
        self.eng, self.sem, self.base, self.n = eng, sem, base, 0

    def then(self, ins):
        self.n += 1
        ins.then_inc(self.sem, 1)
        return ins

    def wait(self):
        self.eng.wait_ge(self.sem, self.base + self.n)

    def link(self, ins):
        self.then(ins)
        self.wait()


RSQRT_STEPS = 14


def rsqrt(nc, c, v, y, w):
    c.link(nc.vector.tensor_single_scalar(w.bitcast(I32), v.bitcast(I32), 1, ALU.logical_shift_right))
    c.link(nc.vector.tensor_scalar(y.bitcast(I32), w.bitcast(I32), -1.0, float(0x5F3759DF), ALU.mult, ALU.add))
    for _ in range(4):
        c.link(nc.vector.tensor_tensor(w, y, y, ALU.mult))
        c.link(nc.vector.scalar_tensor_tensor(out=w, in0=w, scalar=-0.5, in1=v, op0=ALU.mult, op1=ALU.mult))
        c.link(nc.vector.scalar_tensor_tensor(out=y, in0=w, scalar=1.5, in1=y, op0=ALU.add, op1=ALU.mult))


def route(nc, a, m, tokens, t_rows):
    x, mr, bank = m["x"], m["mean_rstd"], m["bank"]
    CH = 4
    with ExitStack() as ctx:
        def sb(name, shape, dt=F32):
            return ctx.enter_context(nc.sbuf_tensor(name, shape, dt))

        s = sems(nc, ctx, "x_in consts_in vec t_made t_stored t_turned t_cols logit_psum logits "
                          "exp_in exp_out mask_bf counted zeroed scattered tokens_back tokens_f tokens_turned "
                          "pool_set dma_zero".split())
        stats = sb("stats", [P, NT, 6])
        rms = sb("rms", [P, NT])
        ve = sb("ve", [P, NT])
        w16 = sb("w16", [P, NT])
        eps = sb("eps", [P, NT])
        norm_w = sb("norm_w", [P, D])
        gate_w = sb("gate_w", [P, KC, E])
        gate_b = sb("gate_b", [P, E])
        xn = sb("xn_r", [P, QT, D])
        t = sb("t_r", [P, QT, D])
        tT = sb("tT_r", [P, KC, QT * P])
        lg = sb("lg", [P, NT, E + 4])
        top = sb("top", [P, NT, 8])
        marks = sb("marks", [P, NT, 8])
        repl = sb("repl", [P, NT, E + 4])
        mk = sb("mk", [P, NT, E])
        mk_bf = sb("mk_bf", [P, NT, E], BF16)
        ex = sb("ex", [P, NT, E])
        ge = sb("ge", [P, NT, E])
        den = sb("den", [P, NT])
        tot = sb("tot", [P, NT, E])
        cum = sb("cum", [P, NT + 1, E])
        cmp = sb("cmp", [P, E, NT])
        need = sb("need", [P, E])
        end = sb("end", [P, E])
        start = sb("start", [P, E])
        where = sb("where", [P, NT, E])
        best = sb("best", [P, NT, 8])
        cmp_n = sb("cmp_n", [1, BLOCKS, E])
        exp_n = sb("exp_n", [1, BLOCKS])
        before = sb("before", [P, P], BF16)
        ones = sb("ones", [P, P], BF16)
        multiples = sb("multiples", [P, NT])
        upto = sb("upto", [P, E, E])
        block_no = sb("block_no", [1, BLOCKS])
        step_f = sb("step_f", [P, P])
        shift_f = sb("shift_f", [P, 3 * P])
        token_no = sb("token_no", [P, NT], U32)
        zeros = sb("zeros", [BLOCKS, P], U32)
        back = sb("back", [BLOCKS, P], U32)
        back_f = sb("back_f", [BLOCKS, P])

        block = ctx.enter_context(nc.Block())

        @block.sync
        def _(sp):
            for name in ("t_made", "t_stored", "t_turned", "t_cols", "logit_psum", "logits", "vec"):
                sp.sem_inc(s[name], 1)
            xv = a["x"].rearrange("b (i p) d -> p (b i) d", p=P)
            for c in range(NT // CH):
                sp.dma_start(x[:, c * CH:(c + 1) * CH, :], xv[:, c * CH:(c + 1) * CH, :]).then_inc(s["x_in"], 16)
                if c == 0:
                    n = 0
                    for dst, src in ((m["ident"][:], a["ident"]), (m["ident_bf"][:], a["ident_bf"]),
                                     (m["row_mask"][:], a["row_mask"]), (step_f[:], a["step"]),
                                     (shift_f[:], a["shift"]), (before[:], a["before"]),
                                     (multiples[:], a["multiples"]), (upto[:], a["upto"]),
                                     (block_no[:], a["block_no"]), (token_no[:], a["token_no"]),
                                     (gate_w[:], a["gate_w"].rearrange("(c p) e -> p c e", p=P)),
                                     (gate_b[:], a["gate_b"].partition_broadcast(P)),
                                     (norm_w[:], a["norm_w"].partition_broadcast(P))):
                        sp.dma_start(dst, src).then_inc(s["consts_in"], 16)
                        n += 1
                    assert n == CONSTS
                sp.wait_ge(s["x_in"], 16 * (c + 1))
            with sp.Fori(0, B) as b:
                sp.wait_ge(s["t_made"], 1 + QT * b + QT)
                sp.dma_start(t_rows.rearrange("(i p) d -> p i d", p=P)[:, bass.ds(b * QT, QT), :],
                             t[:]).then_inc(s["t_stored"], 16)
            sp.wait_ge(s["t_stored"], 1 + 16 * B)
            sp.wait_ge(s["pool_set"], 1)
            sp.dma_start(tokens.rearrange("(n p) o -> n (p o)", p=P), zeros[:]).then_inc(s["dma_zero"], 16)
            sp.wait_ge(s["scattered"], 16 * NT * TOPK)
            sp.dma_start(back[:], tokens.rearrange("(n p) o -> n (p o)", p=P)).then_inc(s["tokens_back"], 16)

        @block.gpsimd
        def _(pool):
            pool.memset(zeros[:], 0).then_inc(s["pool_set"], 1)
            pool.wait_ge(s["dma_zero"], 16)
            pool.wait_ge(s["counted"], 3)
            for n in range(NT):
                for k in range(TOPK):
                    pool.indirect_dma_start(tokens, bass.IndirectOffsetOnAxis(m["slots"][:, n, k:k + 1], 0),
                                            token_no[:, n:n + 1], None).then_inc(s["scattered"], 16)

        @block.tensor
        def _(pe):
            pe.wait_ge(s["consts_in"], 16 * CONSTS)
            with pe.Fori(0, B) as b:
                pe.wait_ge(s["t_made"], 1 + QT * b + QT)
                for k in range(KC):
                    for i in range(QT):
                        ins = pe.transpose(bank[0][:, (k * QT + i) * P:(k * QT + i + 1) * P],
                                           t[:, i, k * P:(k + 1) * P], m["ident"][:])
                ins.then_inc(s["t_turned"], 1)
                pe.wait_ge(s["t_cols"], 1 + b + 1)
                pe.wait_ge(s["logits"], 1 + b)
                for i in range(QT):
                    for k in range(KC):
                        ins = pe.matmul(bank[1][:, i * E:(i + 1) * E], tT[:, k, i * P:(i + 1) * P],
                                        gate_w[:, k, :], start=(k == 0), stop=(k == KC - 1))
                ins.then_inc(s["logit_psum"], 1)
            pe.wait_ge(s["mask_bf"], 1)
            pe.matmul(bank[2][:, 0:NT * E], before[:], mk_bf[:].rearrange("p n e -> p (n e)"), start=True, stop=True)
            pe.matmul(bank[3][:, 0:NT * E], ones[:], mk_bf[:].rearrange("p n e -> p (n e)"),
                      start=True, stop=True).then_inc(s["counted"], 1)
            pe.wait_ge(s["tokens_f"], 1)
            pe.transpose(bank[0][:, 0:BLOCKS], back_f[:], m["ident"][0:BLOCKS, 0:BLOCKS]).then_inc(s["tokens_turned"], 1)

        @block.scalar
        def _(act):
            with act.Fori(0, B) as b:
                act.wait_ge(s["t_turned"], 1 + b + 1)
                act.activation(tT[:].rearrange("p k t -> p (k t)"), bank[0][:], ACT.Copy).then_inc(s["t_cols"], 1)
            act.wait_ge(s["exp_in"], 1)
            act.activation(ex[:], ex[:], ACT.Exp).then_inc(s["exp_out"], 1)

        @block.vector
        def _(dve):
            c = Chain(dve, s["vec"], 1)
            c.then(dve.memset(ones[:], 1.0))
            c.then(dve.memset(lg[:, :, E:], NOT_A_LOGIT))
            c.then(dve.memset(marks[:, :, TOPK:], NOT_A_LOGIT))
            c.then(dve.memset(cum[:, 0, :], 0.0))
            c.then(dve.memset(m["slots"][:, NT:, :], 0))
            c.then(dve.memset(m["block_tokens"][:, BLOCKS:], 0))
            dve.wait_ge(s["consts_in"], 16 * CONSTS)
            c.then(dve.tensor_copy(m["step"][:], step_f[:]))
            for n in range(2):
                for j in range(4):
                    c.then(dve.tensor_copy(m["shift"][:, n, j, :], shift_f[:]))
            for n in range(NT):
                if n % CH == 0:
                    dve.wait_ge(s["x_in"], 16 * (n // CH + 1))
                c.then(dve.bn_stats(stats[:, n, :], x[:, n, :]))
            c.wait()
            for n in range(NT):
                c.then(dve.bn_aggr(mr[:, :, n], stats[:, n, :]))
            c.wait()
            c.link(dve.tensor_scalar(ve[:], mr[:, 1, :], EPS, None, ALU.add))
            c.link(dve.tensor_copy(den[:], mr[:, 1, :]))
            rsqrt(nc, c, ve[:], mr[:, 1, :], w16[:])
            c.link(dve.tensor_tensor(w16[:], mr[:, 1, :], mr[:, 1, :], ALU.mult))
            c.link(dve.tensor_tensor(ve[:], w16[:], den[:], ALU.mult))
            c.link(dve.tensor_scalar(ve[:], ve[:], EPS, None, ALU.add))
            rsqrt(nc, c, ve[:], rms[:], w16[:])
            base = c.n
            with dve.Fori(0, B) as b:
                dve.wait_ge(s["t_turned"], 1 + b)
                dve.wait_ge(s["t_stored"], 1 + 16 * b)
                for i in range(QT):
                    n = b * QT + i
                    dve.tensor_scalar(xn[:, i, :], x[:, bass.ds(n, 1), :].rearrange("p o d -> p (o d)"),
                                      mr[:, 0, bass.ds(n, 1)], mr[:, 1, bass.ds(n, 1)],
                                      ALU.subtract, ALU.mult).then_inc(s["vec"], 1)
                dve.wait_ge(s["vec"], 1 + b * QT + (base + QT))
                for i in range(QT):
                    dve.scalar_tensor_tensor(out=t[:, i, :], in0=xn[:, i, :], scalar=rms[:, bass.ds(b * QT + i, 1)],
                                             in1=norm_w[:], op0=ALU.mult, op1=ALU.mult).then_inc(s["t_made"], 1)
                dve.wait_ge(s["logit_psum"], 1 + b + 1)
                dve.tensor_tensor(lg[:, bass.ds(b * QT, QT), 0:E], bank[1][:, 0:QT * E].rearrange("p (i e) -> p i e", i=QT),
                                  gate_b[:].unsqueeze(1).broadcast_to([P, QT, E]), ALU.add).then_inc(s["logits"], 1)
            c.n += B * QT
            dve.wait_ge(s["logits"], 1 + B)
            for n in range(NT):
                c.then(dve.max(top[:, n, :], lg[:, n, 0:E]))
            c.wait()
            c.link(dve.tensor_copy(marks[:, :, 0:TOPK], top[:, :, 0:TOPK]))
            for n in range(NT):
                c.then(dve.match_replace(repl[:, n, :], marks[:, n, :], lg[:, n, :], CHOSEN))
            c.wait()
            c.link(dve.tensor_tensor(mk[:], repl[:, :, 0:E], lg[:, :, 0:E], ALU.not_equal))
            dve.tensor_copy(mk_bf[:], mk[:]).then_inc(s["mask_bf"], 1)
            dve.tensor_tensor(ex[:], lg[:, :, 0:E], top[:, :, 0:1].broadcast_to([P, NT, E]),
                              ALU.subtract).then_inc(s["exp_in"], 1)
            dve.wait_ge(s["exp_out"], 1)
            c.link(dve.tensor_tensor(ge[:], ex[:], mk[:], ALU.mult))
            c.link(dve.tensor_reduce(den[:], ge[:], AX.X, ALU.add))
            c.link(dve.reciprocal(w16[:], den[:]))
            c.then(dve.tensor_tensor(ge[:], ge[:], w16[:].unsqueeze(2).broadcast_to([P, NT, E]), ALU.mult))
            dve.wait_ge(s["counted"], 1)
            c.link(dve.tensor_copy(tot[:].rearrange("p n e -> p (n e)"), bank[3][:, 0:NT * E]))
            for n in range(NT):
                c.link(dve.tensor_tensor(cum[:, n + 1, :], cum[:, n, :], tot[:, n, :], ALU.add))
            c.link(dve.tensor_tensor(cmp[:], cum[:, NT, :].unsqueeze(2).broadcast_to([P, E, NT]),
                                     multiples[:].unsqueeze(1).broadcast_to([P, E, NT]), ALU.is_gt))
            c.link(dve.tensor_reduce(need[:], cmp[:], AX.X, ALU.add))
            c.link(dve.tensor_tensor(cmp[:], need[:].unsqueeze(1).broadcast_to([P, E, E]), upto[:], ALU.mult))
            c.link(dve.tensor_reduce(end[:], cmp[:], AX.X, ALU.add))
            c.link(dve.tensor_tensor(start[:], end[:], need[:], ALU.subtract))
            c.link(dve.tensor_scalar(start[:], start[:], float(P), 1.0, ALU.mult, ALU.add))
            c.link(dve.tensor_tensor(where[:].rearrange("p n e -> p (n e)"), bank[2][:, 0:NT * E],
                                     cum[:, 0:NT, :].rearrange("p n e -> p (n e)"), ALU.add))
            c.link(dve.tensor_tensor(where[:], where[:], start[:].unsqueeze(1).broadcast_to([P, NT, E]), ALU.add))
            c.link(dve.tensor_tensor(where[:], where[:], mk[:], ALU.mult))
            for n in range(NT):
                c.then(dve.max(best[:, n, :], where[:, n, :]))
            c.wait()
            dve.tensor_scalar(m["slots"][:, 0:NT, :], best[:, :, 0:TOPK], -1.0, None, ALU.add).then_inc(s["counted"], 2)
            for k in range(TOPK):
                c.link(dve.tensor_tensor(ex[:], where[:], best[:, :, k:k + 1].broadcast_to([P, NT, E]), ALU.is_equal))
                c.link(dve.tensor_tensor(ex[:], ex[:], ge[:], ALU.mult))
                c.link(dve.tensor_reduce(m["gates"][:, :, k], ex[:], AX.X, ALU.add))
            c.link(dve.tensor_tensor(cmp_n[:], end[0:1, :].unsqueeze(1).broadcast_to([1, BLOCKS, E]),
                                     block_no[:].unsqueeze(2).broadcast_to([1, BLOCKS, E]), ALU.is_le))
            c.link(dve.tensor_reduce(exp_n[:], cmp_n[:], AX.X, ALU.add))
            c.link(dve.tensor_scalar(m["block_expert"][:], exp_n[:], float(E - 1), None, ALU.min))
            dve.wait_ge(s["tokens_back"], 16)
            dve.tensor_copy(back_f[:], back[:]).then_inc(s["tokens_f"], 1)
            dve.wait_ge(s["tokens_turned"], 1)
            c.link(dve.tensor_copy(m["block_tokens"][:, 0:BLOCKS], bank[0][:, 0:BLOCKS]))


CONSTS = 13


def weave(attention, other, steps):
    tick, attending, beside = 0, True, True
    while attending or beside:
        if attending:
            attending = next(attention, "end") != "end"
        for _ in range(steps.get(tick, 0) if attending else 1):
            beside = beside and next(other, "end") != "end"
        tick += 1


def layer0(nc, a, m, t_rows, y_rows, s_rows):
    x, mr, bank = m["x"], m["mean_rstd"], m["bank"]
    S, C, MISC, HB, TB, YB = bank[0:2], bank[2:4], bank[4], bank[5], bank[6], bank[7]
    HJ = H0 // 4
    QKV = D + 2 * G0 * HD0
    ROT = D + G0 * HD0
    ROW_FILLS, KEY_FILLS = 3 * HJ, 3 * G0
    with ExitStack() as ctx:
        def sb(name, shape, dt=F32):
            return ctx.enter_context(nc.sbuf_tensor(name, shape, dt))

        counts = ("xn_made xn_turned xn_cols qkv_psum rot v_made stacked q_turned q_cols k_turned k_cols "
                          "row_scores row_max max_turned max_rows shift_even shift_odd key_scores probs ctx_psum ctx_out "
                          "ctx_turned ctx_norm norm_steps s_psum s_made s_stored "
                          "picked rows_turned rows_cols hidden gate_in lin_in tanh_done lin_scaled mid acted "
                          "act_turned act_cols y_psum y_made y_stored").split()
        s = sems(nc, ctx, ["weights_in", "experts_in", "parts", "set", "gathered_even", "gathered_odd"] + counts)
        gathered = [s["gathered_even"], s["gathered_odd"]]
        shift_in = [s["shift_even"], s["shift_odd"]]
        w_qkv = sb("w_qkv", [P, KC, QKV])
        w_o = sb("w_o", [P, QT, D])
        w1 = sb("w1", [P, KC, E * 2 * I])
        w2 = sb("w2", [P, KC, E * D])
        pick = sb("pick", [P, E * P], BF16)
        bias = sb("bias", [P, 2 * I + D], BF16)
        cos = sb("cos", [P, QT, HD0])
        sin = sb("sin", [P, QT, HD0])
        xn = sb("xn", [P, QT, D])
        xnT = sb("xnT", [P, KC, T])
        t1 = sb("rot_a", [P, ROT])
        t2 = sb("rot_b", [P, ROT])
        qT = sb("qT", [P, HJ, T], F32R)
        kT = sb("kT", [P, 2, 4, T], F32R)
        v = sb("v", [P, QT, G0, 32])
        nmax = sb("nmax", [P, QT, H0])
        nmaxT = sb("nmaxT", [H0, 3 * P], F32R)
        shared = sb("shared", [P, 3072])
        qs = shared[:, 0:2048].rearrange("p (i n) -> p i n", i=QT)
        ks = shared[:, 2048:2560].rearrange("p (i n) -> p i n", i=QT)
        p0 = shared[:, 0:2048].rearrange("p (u j q) -> p u j q", u=2, j=4)
        p1 = shared[:, 2048:3072].rearrange("p (u j q) -> p u j q", u=2, j=4)
        ctx_sb = sb("ctx_sb", [P, QT, 4 * P])
        rec = sb("rec", [P, 4, 4])
        cx = sb("cx", [P, QT, D])
        s_sb = sb("s_sb", [P, QT, D])
        rows_in = sb("rows_in", [P, 2, D])
        rows_no = sb("rows_no", [P, 2], U32)
        carrier = sb("carrier0", [P, 2])
        rowsT = sb("rowsT", [P, KC * P])
        gate = sb("gate", [P, I])
        lin = sb("lin", [P, I])
        tanh = sb("tanh", [P, I])
        actd = sb("actd", [P, I])
        actT = sb("actT", [P, KC * P])
        y = sb("y", [P, D])
        block = ctx.enter_context(nc.Block())


        @block.sync
        def _(sp):
            for name in counts:
                sp.sem_inc(s[name], 1)
            for n, (dst, src) in enumerate((
                    (w_qkv[:], a["wqkv0"].rearrange("(c p) n -> p c n", p=P)),
                    (w_o[:], a["wo0"].rearrange("(c p) n -> p c n", p=P)),
                    (cos[:], a["cos"]), (sin[:], a["sin"]),
                    (pick[:], a["pick"].rearrange("p e m -> p (e m)")))):
                sp.dma_start(dst, src).then_inc(s["weights_in"], 16)
            sp.wait_ge(s["set"], 1)
            for part in range(3):
                sp.dma_start(w2[32 * part:32 * part + E, 0, 0:768], a["b12"]).then_inc(s["weights_in"], 16)
            sp.wait_ge(s["parts"], 6)
            for k in range(KC):
                sp.dma_start(w1[:, k, :], a["w1"][k * P:(k + 1) * P, :]).then_inc(s["experts_in"], 16)
                sp.dma_start(w2[:, k, :], a["w2"][k * P:(k + 1) * P, :]).then_inc(s["experts_in"], 16)
            with sp.Fori(0, B) as b:
                def attention():
                    for _ in range(34):
                        yield
                    for g in range(G0):
                        sp.wait_ge(s["key_scores"], 1 + KEY_FILLS * b + 3 * max(g - 1, 0))
                        if g == 0:
                            sp.wait_ge(s["max_rows"], 1 + 2 * b + 2)
                        sp.dma_start(m["shift"][0:1, g % 2, :, :].bitcast(F32),
                                     nmaxT[4 * g:4 * g + 4, :].bitcast(F32)).then_inc(shift_in[g % 2], 16)
                        for _ in range(4):
                            yield
                    for _ in range(5):
                        yield
                    sp.wait_ge(s["s_made"], 1 + b + 1)
                    sp.dma_start(s_rows.rearrange("(n p) d -> p n d", p=P)[:, bass.ds(b * QT, QT), :],
                                 s_sb[:]).then_inc(s["s_stored"], 16)
                    yield

                def experts():
                    for k in range(BPB):
                        for _ in range(3):
                            yield
                        sp.wait_ge(s["y_made"], 1 + BPB * b + k + 1)
                        sp.dma_start(y_rows[bass.ds((b * BPB + k) * P, P), :], y[:]).then_inc(s["y_stored"], 16)
                        yield

                weave(attention(), experts(), {t: 1 for t in range(0, 90, 2)})
            sp.wait_ge(s["s_made"], 1 + B)
            sp.dma_start(s_rows.rearrange("(n p) d -> p n d", p=P)[:, NT:NT + QT, :], s_sb[:]).then_inc(s["s_stored"], 16)
            sp.wait_ge(s["s_stored"], 1 + 16 * (B + 1))
            sp.wait_ge(s["y_stored"], 1 + 16 * BLOCKS)

        @block.gpsimd
        def _(pool):
            def gather(n, u):
                nc.gpsimd.tensor_copy(rows_no[:, u:u + 1], m["block_tokens"][:, bass.ds(n, 1)]).then_inc(s["picked"], 1)
                pool.wait_ge(s["picked"], 1 + 2 * n + 2)
                nc.gpsimd.tensor_tensor(carrier[:, 1:2], carrier[:, 0:1], carrier[:, 0:1], ALU.add).then_inc(s["picked"], 1)
                nc.gpsimd.indirect_dma_start(rows_in[:, u, :], None, t_rows,
                                             bass.IndirectOffsetOnAxis(rows_no[:, u:u + 1], 0)).then_inc(gathered[u], 16)

            pool.memset(carrier[:], 0.0).then_inc(s["picked"], 1)
            pool.wait_ge(s["picked"], 1 + 1)
            gather(0, 0)
            gather(1, 1)
            with pool.Fori(0, B) as b:
                for k in range(BPB):
                    n = b * BPB + k
                    pool.wait_ge(s["rows_turned"], 1 + n + 1)
                    pool.wait_ge(gathered[k % 2], 16 * (b * (BPB // 2) + k // 2 + 1))
                    gather(n + 2, k % 2)
            for u in range(2):
                pool.wait_ge(gathered[u], 16 * (BLOCKS // 2 + 1))

        @block.tensor
        def _(pe):
            pe.wait_ge(s["weights_in"], 16 * 8)
            with pe.Fori(0, B) as b:
                def attention():
                    yield
                    pe.wait_ge(s["xn_made"], 1 + QT * b + QT)
                    pe.wait_ge(s["s_made"], 1 + b)
                    for k in range(KC):
                        for i in range(QT):
                            ins = pe.transpose(MISC[:, (k * QT + i) * P:(k * QT + i + 1) * P],
                                               xn[:, i, k * P:(k + 1) * P], m["ident"][:])
                    ins.then_inc(s["xn_turned"], 1)
                    yield
                    pe.wait_ge(s["xn_cols"], 1 + b + 1)
                    pe.wait_ge(s["ctx_out"], 1 + 4 * b)
                    for i in range(QT):
                        for k in range(KC):
                            ins = pe.matmul(C[i][:, 0:QKV], xnT[:, k, i * P:(i + 1) * P], w_qkv[:, k, :],
                                            start=(k == 0), stop=(k == KC - 1))
                        ins.then_inc(s["qkv_psum"], 1)
                    yield
                    yield
                    pe.wait_ge(s["probs"], 1 + KEY_FILLS * b)
                    for f in range(4):
                        if f == 0:
                            pe.wait_ge(s["stacked"], 1 + 2 * b + 2)
                        if f >= 2:
                            pe.wait_ge(s["q_cols"], 1 + 4 * b + f - 1)
                        for c in range(2):
                            for i in range(QT):
                                ins = pe.transpose(S[f % 2][:, (c * QT + i) * P:(c * QT + i + 1) * P],
                                                   qs[:, i, (2 * f + c) * P:(2 * f + c + 1) * P], m["ident"][:])
                        ins.then_inc(s["q_turned"], 1)
                        yield
                    pe.wait_ge(s["xn_cols"], 1 + b + 1)
                    for h in range(2):
                        for i in range(QT):
                            ins = pe.transpose(MISC[:, (h * QT + i) * P:(h * QT + i + 1) * P],
                                               ks[:, i, h * P:(h + 1) * P], m["ident"][:])
                    ins.then_inc(s["k_turned"], 1)
                    yield
                    pe.wait_ge(s["k_cols"], 1 + 4 * b + 4)
                    pe.wait_ge(s["q_cols"], 1 + 4 * b + 4)
                    for f in range(ROW_FILLS):
                        hj, u = f // 3, f % 3
                        if f >= 2:
                            pe.wait_ge(s["row_max"], 1 + ROW_FILLS * b + f - 1)
                        o = S[f % 2]
                        if u == 0:
                            pe.matmul(o[:], qT[:, hj, 0:P], kT[:, hj // 4, :, 0:P], start=True, stop=False)
                            ins = pe.matmul(o[:], m["ident_bf"][:], m["row_mask"][:].unsqueeze(1).broadcast_to([P, 4, P]),
                                            start=False, stop=True)
                        else:
                            pe.matmul(o[:], qT[:, hj, P:T], kT[:, hj // 4, 2 * u - 2:2 * u, :], start=True, stop=False)
                            ins = pe.matmul(o[:].rearrange("p (g t) -> p g t", g=2)[:, :, P:T], m["ident_bf"][:],
                                            m["row_mask"][:].unsqueeze(1).broadcast_to([P, 2, P]), start=False, stop=True)
                        ins.then_inc(s["row_scores"], 1)
                        yield
                    pe.wait_ge(s["row_max"], 1 + ROW_FILLS * b + ROW_FILLS)
                    for i in range(QT):
                        ins = pe.transpose(MISC[0:H0, i * P:(i + 1) * P], nmax[:, i, :], m["ident"][:])
                    ins.then_inc(s["max_turned"], 1)
                    yield

                    def context(g):
                        h, o = g // 4, 32 * (g % 4)
                        pe.wait_ge(s["probs"], 1 + KEY_FILLS * b + 3 * g + 3)
                        if g == 4:
                            pe.wait_ge(s["ctx_out"], 1 + 4 * b + 2)
                        pe.matmul(C[0][o:o + 32, :], v[:, 0, g, :], p0[:, g % 2, :, 0:P], start=True, stop=True)
                        pe.matmul(C[1][o:o + 32, :], v[:, 0, g, :], p0[:, g % 2, :, P:T], start=True, stop=False)
                        pe.matmul(C[1][o:o + 32, :], v[:, 1, g, :], p1[:, g % 2, :, :],
                                  start=False, stop=True).then_inc(s["ctx_psum"], 1)

                    def turn_context(n):
                        pe.wait_ge(s["ctx_out"], 1 + 4 * b + 2 * (n // 2) + 2)
                        if n == 0:
                            pe.wait_ge(s["max_rows"], 1 + 2 * b + 2)
                        else:
                            pe.wait_ge(s["ctx_norm"], 1 + 4 * b + n)
                        for j in range(4):
                            ins = pe.transpose(MISC[:, j * P:(j + 1) * P], ctx_sb[:, n % 2, j * P:(j + 1) * P], m["ident"][:])
                        ins.then_inc(s["ctx_turned"], 1)

                    for g in range(G0):
                        pe.wait_ge(shift_in[g % 2], 1 + 16 * (G0 // 2 * b + g // 2 + 1))
                        for u in range(3):
                            f = 3 * g + u
                            if f >= 2:
                                pe.wait_ge(s["probs"], 1 + KEY_FILLS * b + f - 1)
                            o = S[f % 2]
                            h = g // 4
                            if u < 2:
                                pe.matmul(o[:], kT[:, h, g % 4, 0:P], qT[:, 4 * h + 2 * u:4 * h + 2 * u + 2, :],
                                          start=True, stop=False)
                                ins = pe.matmul(o[:], m["step"][:], m["shift"][:, g % 2, 2 * u:2 * u + 2, 0:T],
                                                start=False, stop=True)
                            else:
                                pe.matmul(o[:], kT[:, h, g % 4, P:T], qT[:, 4 * h:4 * h + 4, P:T],
                                          start=True, stop=False)
                                ins = pe.matmul(o[:], m["step"][:], m["shift"][:, g % 2, :, T:3 * P],
                                                start=False, stop=True)
                            ins.then_inc(s["key_scores"], 1)
                            yield
                        if g >= 1:
                            context(g - 1)
                        if g == 5:
                            turn_context(0)
                        if g == 6:
                            turn_context(1)
                        yield
                    context(G0 - 1)
                    yield
                    turn_context(2)
                    yield
                    turn_context(3)
                    yield
                    pe.wait_ge(s["ctx_norm"], 1 + 4 * b + 4)
                    for r in range(QT):
                        for i in range(QT):
                            ins = pe.matmul(MISC[:, r * D:(r + 1) * D], cx[:, i, r * P:(r + 1) * P], w_o[:, i, :],
                                            start=(i == 0), stop=(i == QT - 1))
                    ins.then_inc(s["s_psum"], 1)
                    yield

                def experts():
                    for k in range(BPB):
                        n = b * BPB + k
                        pe.wait_ge(gathered[k % 2], 16 * (b * (BPB // 2) + k // 2 + 1))
                        pe.wait_ge(s["act_cols"], 1 + n)
                        for c in range(KC):
                            ins = pe.transpose(TB[:, c * P:(c + 1) * P], rows_in[:, k % 2, c * P:(c + 1) * P], m["ident"][:])
                        ins.then_inc(s["rows_turned"], 1)
                        yield
                        if k == 0:
                            pe.wait_ge(s["experts_in"], 64)
                        e = pe.value_load(m["block_expert"][0:1, bass.ds(n, 1)], min_val=0, max_val=E - 1)
                        pe.wait_ge(s["rows_cols"], 1 + n + 1)
                        pe.wait_ge(s["lin_in"], 1 + n)
                        pe.matmul(HB[:], pick[:, bass.ds(e * P, P)], bias[:, 0:2 * I], start=True, stop=False)
                        for c in range(KC):
                            ins = pe.matmul(HB[:], rowsT[:, c * P:(c + 1) * P], w1[:, c, bass.ds(e * 2 * I, 2 * I)],
                                            start=False, stop=(c == KC - 1))
                        ins.then_inc(s["hidden"], 1)
                        yield
                        pe.wait_ge(s["acted"], 1 + n + 1)
                        for c in range(KC):
                            ins = pe.transpose(TB[:, c * P:(c + 1) * P], actd[:, c * P:(c + 1) * P], m["ident"][:])
                        ins.then_inc(s["act_turned"], 1)
                        yield
                        pe.wait_ge(s["act_cols"], 1 + n + 1)
                        pe.wait_ge(s["y_made"], 1 + n)
                        pe.matmul(YB[:, 0:D], pick[:, bass.ds(e * P, P)], bias[:, 2 * I:], start=True, stop=False)
                        for c in range(KC):
                            ins = pe.matmul(YB[:, 0:D], actT[:, c * P:(c + 1) * P], w2[:, c, bass.ds(e * D, D)],
                                            start=False, stop=(c == KC - 1))
                        ins.then_inc(s["y_psum"], 1)
                        yield

                weave(attention(), experts(), {t: 1 for t in range(0, 90, 2)})

        @block.scalar
        def _(act):
            with act.Fori(0, B) as b:
                def attention():
                    yield
                    act.wait_ge(s["xn_turned"], 1 + b + 1)
                    act.activation(xnT[:].rearrange("p k t -> p (k t)"), MISC[:], ACT.Copy).then_inc(s["xn_cols"], 1)
                    yield
                    yield
                    yield
                    for f in range(4):
                        act.wait_ge(s["q_turned"], 1 + 4 * b + f + 1)
                        act.activation(qT[:, 2 * f:2 * f + 2, :].rearrange("p c t -> p (c t)"), S[f % 2][:],
                                       ACT.Copy).then_inc(s["q_cols"], 1)
                        yield
                    for _ in range(1 + ROW_FILLS + 1):
                        yield
                    for g in range(G0):
                        for u in range(3):
                            f = 3 * g + u
                            act.wait_ge(s["key_scores"], 1 + KEY_FILLS * b + f + 1)
                            if u == 0 and g >= 2:
                                act.wait_ge(s["ctx_psum"], 1 + G0 * b + g - 1)
                            if u < 2:
                                dst = p0[:, g % 2, 2 * u:2 * u + 2, :].rearrange("p j q -> p (j q)")
                            else:
                                dst = p1[:, g % 2, :, :].rearrange("p j q -> p (j q)")
                            act.activation(dst, S[f % 2][:], ACT.Exp, scale=float(HD0) ** -0.5).then_inc(s["probs"], 1)
                            yield
                        if g == 4:
                            evacuate(0)
                        yield
                    evacuate(1)
                    yield
                    yield
                    yield
                    act.wait_ge(s["s_psum"], 1 + b + 1)
                    act.wait_ge(s["s_stored"], 1 + 16 * b)
                    act.activation(s_sb[:].rearrange("p i d -> p (i d)"), MISC[:], ACT.Copy).then_inc(s["s_made"], 1)
                    yield

                def evacuate(h):
                    act.wait_ge(s["ctx_psum"], 1 + G0 * b + 4 * h + 4)
                    act.wait_ge(s["ctx_turned"], 1 + 4 * b + 2 * h)
                    for i in range(QT):
                        act.activation(ctx_sb[:, i, :], C[i][:], ACT.Copy).then_inc(s["ctx_out"], 1)

                def experts():
                    for k in range(BPB):
                        n = b * BPB + k
                        act.wait_ge(s["rows_turned"], 1 + n + 1)
                        act.wait_ge(s["hidden"], 1 + n)
                        act.activation(rowsT[:], TB[:, 0:KC * P], ACT.Copy).then_inc(s["rows_cols"], 1)
                        yield
                        act.wait_ge(s["gate_in"], 1 + n + 1)
                        act.wait_ge(s["mid"], 1 + n)
                        act.activation(tanh[:], gate[:], ACT.Tanh, scale=ALPHA / 2).then_inc(s["tanh_done"], 1)
                        yield
                        act.wait_ge(s["act_turned"], 1 + n + 1)
                        act.wait_ge(s["y_psum"], 1 + n)
                        act.activation(actT[:], TB[:, 0:KC * P], ACT.Copy).then_inc(s["act_cols"], 1)
                        yield
                        act.wait_ge(s["y_psum"], 1 + n + 1)
                        act.wait_ge(s["y_stored"], 1 + 16 * n)
                        act.activation(y[:], YB[:, 0:D], ACT.Copy).then_inc(s["y_made"], 1)
                        yield

                weave(attention(), experts(), {t: 1 for t in range(0, 90, 2)})

        @block.vector
        def _(dve):
            V = nc.vector
            V.memset(w2[:, 0, 0:768], 0.0).then_inc(s["set"], 1)
            V.memset(kT[:].rearrange("p h g t -> p (h g t)").bitcast(F32), 0.0).then_inc(s["parts"], 1)
            V.memset(v[:], 0.0).then_inc(s["parts"], 1)
            dve.wait_ge(s["parts"], 2)
            V.memset(v[:, :, :, HD0:HD0 + 1], 1.0).then_inc(s["parts"], 1)
            dve.wait_ge(s["weights_in"], 16 * 8)
            b12, left, half = w2[:, 0, 0:768], w2[:, 0, 768:1536], w2[:, 0, 1536:1920].bitcast(BF16)
            V.tensor_copy(bias[:], b12).then_inc(s["parts"], 1)
            dve.wait_ge(s["parts"], 4)
            V.tensor_tensor(left, b12, bias[:], ALU.subtract).then_inc(s["norm_steps"], 1)
            dve.wait_ge(s["norm_steps"], 1 + 1)
            V.tensor_copy(half, left).then_inc(s["norm_steps"], 1)
            dve.wait_ge(s["norm_steps"], 1 + 2)
            V.tensor_copy(bias[32:64, :], half[32:64, :]).then_inc(s["parts"], 1)
            V.tensor_tensor(bias[64:96, :], left[64:96, :], half[64:96, :], ALU.subtract).then_inc(s["parts"], 1)
            BASE = 2
            STEPS = 5 * QT + 4
            with dve.Fori(0, B) as b:
                c = Chain(dve, s["norm_steps"], 1 + b * STEPS + BASE)

                def rotate(i):
                    dve.wait_ge(s["qkv_psum"], 1 + QT * b + i + 1)
                    if i == 0:
                        dve.wait_ge(s["ctx_psum"], 1 + G0 * b)
                    V.tensor_copy(v[:, i, :, 0:HD0],
                                  C[i][:, ROT:QKV].rearrange("p (g d) -> p g d", d=HD0)).then_inc(s["v_made"], 1)
                    qk = C[i][:, 0:ROT].rearrange("p (h d) -> p h d", d=HD0)
                    t1v = t1[:].rearrange("p (h d) -> p h d", d=HD0)
                    t2v = t2[:].rearrange("p (h d) -> p h d", d=HD0)
                    n, hd = ROT // HD0, HD0 // 2
                    c.then(V.tensor_tensor(t1v, qk, cos[:, i:i + 1, :].broadcast_to([P, n, HD0]), ALU.mult))
                    c.then(V.tensor_tensor(t2v[:, :, 0:hd], qk[:, :, hd:], sin[:, i:i + 1, 0:hd].broadcast_to([P, n, hd]), ALU.mult))
                    c.link(V.tensor_tensor(t2v[:, :, hd:], qk[:, :, 0:hd], sin[:, i:i + 1, hd:].broadcast_to([P, n, hd]), ALU.mult))
                    c.link(V.tensor_tensor(t1[:], t1[:], t2[:], ALU.add))
                    q = t1[:, 0:D].rearrange("p (n o d) -> p n o d", o=1, d=HD0).broadcast_to([P, 32, 2, HD0])
                    k = t1[:, D:ROT].rearrange("p (n o d) -> p n o d", o=1, d=HD0).broadcast_to([P, 8, 2, HD0])
                    q4 = qs[:, i, :].rearrange("p (n r c d) -> p n r c d", r=2, c=2, d=HD0)
                    k4 = ks[:, i, :].rearrange("p (n r c d) -> p n r c d", r=2, c=2, d=HD0)
                    V.tensor_copy(q4[:, :, 0, :, :].bitcast(F32R), q).then_inc(s["v_made"], 1)
                    c.link(V.tensor_copy(k4[:, :, :, 0, :].bitcast(F32R), k))
                    dve.wait_ge(s["v_made"], 1 + 4 * b + 2 * i + 2)
                    V.tensor_tensor(k4[:, :, :, 1, :].bitcast(F32R), k, k4[:, :, :, 0, :], ALU.subtract).then_inc(s["rot"], 1)
                    V.tensor_tensor(q4[:, :, 1, :, :].bitcast(F32R), q, q4[:, :, 0, :, :],
                                    ALU.subtract).then_inc(s["stacked"], 1)
                    dve.wait_ge(s["stacked"], 1 + 2 * b + i + 1)
                    dve.wait_ge(s["rot"], 1 + 2 * b + i + 1)

                def normalise(n):
                    h, i = n // 2, n % 2
                    dve.wait_ge(s["ctx_turned"], 1 + 4 * b + n + 1)
                    o = MISC[:].rearrange("p (j g r) -> p j g r", j=4, g=4)
                    c.link(V.reciprocal(rec[:], o[:, :, :, HD0]))
                    dst = cx[:, i, h * P:(h + 1) * P].rearrange("p (g j d) -> p j g d", g=4, j=4)
                    V.tensor_tensor(dst, o[:, :, :, 0:HD0], rec[:].unsqueeze(3).broadcast_to([P, 4, 4, HD0]),
                                    ALU.mult).then_inc(s["ctx_norm"], 1)

                def attention():
                    dve.wait_ge(s["xn_turned"], 1 + b)
                    for i in range(QT):
                        n = b * QT + i
                        V.tensor_scalar(xn[:, i, :], x[:, bass.ds(n, 1), :].rearrange("p o d -> p (o d)"),
                                        mr[:, 0, bass.ds(n, 1)], mr[:, 1, bass.ds(n, 1)],
                                        ALU.subtract, ALU.mult).then_inc(s["xn_made"], 1)
                    yield
                    yield
                    rotate(0)
                    yield
                    rotate(1)
                    yield
                    for _ in range(4):
                        yield
                    dve.wait_ge(s["k_turned"], 1 + b + 1)
                    for g in range(4):
                        r = slice(32 * g, 32 * g + 32)
                        V.tensor_copy(kT[r, :, g, :], MISC[r, :].rearrange("p (h t) -> p h t", h=2)).then_inc(s["k_cols"], 1)
                    yield
                    for f in range(ROW_FILLS):
                        hj, u = f // 3, f % 3
                        h, j = hj // 4, hj % 4
                        o = S[f % 2]
                        dve.wait_ge(s["row_scores"], 1 + ROW_FILLS * b + f + 1)
                        heads = nmax[:].rearrange("p i (h g j) -> p i h g j", h=2, g=4)
                        if u == 0:
                            dst, src = heads[:, 0, h, :, j], o[:].rearrange("p (g t) -> p g t", g=4)
                        else:
                            dst, src = heads[:, 1, h, 2 * u - 2:2 * u, j], o[:].rearrange("p (g t) -> p g t", g=2)
                        V.tensor_reduce(dst, src, AX.X, ALU.max, negate=True).then_inc(s["row_max"], 1)
                        yield
                    dve.wait_ge(s["max_turned"], 1 + b + 1)
                    for u in range(2):
                        dve.wait_ge(shift_in[u], 1 + 16 * (G0 // 2) * b)
                    V.tensor_copy(nmaxT[:, 0:T], MISC[0:H0, 0:T]).then_inc(s["max_rows"], 1)
                    V.tensor_copy(nmaxT[:, T:], MISC[0:H0, P:T]).then_inc(s["max_rows"], 1)
                    yield
                    for g in range(G0):
                        for _ in range(3):
                            yield
                        if g == 5:
                            normalise(0)
                        if g == 6:
                            normalise(1)
                        yield
                    yield
                    normalise(2)
                    yield
                    normalise(3)
                    yield
                    yield

                def experts():
                    for k in range(BPB):
                        n = b * BPB + k
                        yield
                        dve.wait_ge(s["hidden"], 1 + n + 1)
                        dve.wait_ge(s["tanh_done"], 1 + n)
                        V.tensor_scalar(gate[:], HB[:, 0:I], LIMIT, None, ALU.min).then_inc(s["gate_in"], 1)
                        V.tensor_scalar(lin[:], HB[:, I:2 * I], LIMIT, -LIMIT, ALU.min, ALU.max).then_inc(s["lin_in"], 1)
                        dve.wait_ge(s["lin_in"], 1 + n + 1)
                        V.tensor_scalar(lin[:], lin[:], 1.0, 0.5, ALU.add, ALU.mult).then_inc(s["lin_scaled"], 1)
                        dve.wait_ge(s["tanh_done"], 1 + n + 1)
                        dve.wait_ge(s["act_turned"], 1 + n)
                        V.scalar_tensor_tensor(out=actd[:], in0=tanh[:], scalar=1.0, in1=gate[:],
                                               op0=ALU.add, op1=ALU.mult).then_inc(s["mid"], 1)
                        dve.wait_ge(s["mid"], 1 + n + 1)
                        dve.wait_ge(s["lin_scaled"], 1 + n + 1)
                        V.tensor_tensor(actd[:], actd[:], lin[:], ALU.mult).then_inc(s["acted"], 1)
                        yield
                        yield
                        yield

                weave(attention(), experts(), {t: 1 for t in range(0, 90, 2)})
                assert c.n == STEPS, c.n


def layer1(nc, a, m, y_rows, s_rows, out):
    x, mr, bank = m["x"], m["mean_rstd"], m["bank"]
    S, C, MISC, HB, TB, YB = bank[0:2], bank[2:4], bank[4], bank[5], bank[6], bank[7]
    PAIRS, GROUPS = H1 // 2, H1 // 4
    HEAD_AT = 20
    FFN_AT = {4: 1, 5: 1, 6: 1, 12: 1, 18: 1, 24: 1, 26: 1, 27: 1, 38: 1}
    ROW_FILLS, KEY_FILLS = GROUPS + PAIRS, 3 * GROUPS
    CHOICES = QT * TOPK
    with ExitStack() as ctx:
        def sb(name, shape, dt=F32):
            return ctx.enter_context(nc.sbuf_tensor(name, shape, dt))

        counts = ("s_in picked1 head_steps steps1 f_made f_tanh x_made xn_made1 xn_turned1 xn_cols1 qk_psum v_psum "
                          "v_cols stacked1 q_turned1 q_cols1 k_turned1 k_low k_high row_scores1 row_max1 max_turned1 "
                          "max_rows1 shift_even1 shift_odd1 key_scores1 probs1 ctx_psum1 ctx_out1 ctx_turned1 ctx_norm1 "
                          "cx_turned cx_cols s_psum1 s_made1 "
                          "hid_psum hid_tanh hid_mid hid_made down_psum down_made out_tanh out_mid out_made stored").split()
        s = sems(nc, ctx, ["attn_in", "ffn_in", "prep", "rows_in1"] + counts)
        shift_in = [s["shift_even1"], s["shift_odd1"]]
        w_qkv = sb("w_qkv1", [P, KC, 3 * D])
        w_o = sb("w_o1", [P, KC, D])
        raw = sb("raw", [P, KC, HID], I32)
        w_gate = sb("w_gate1", [P, KC, HID])
        w_up = sb("w_up1", [P, KC, HID])
        w_down = sb("w_down1", [P, HC, D])
        s_gate = sb("s_gate", [P, HC])
        s_up = sb("s_up", [P, HC])
        s_both = sb("s_both", [P, HC])
        s_down = sb("s_down", [P, D])
        s0 = sb("s0", [P, QT, D])
        rows_no = sb("rows_no1", [P, CHOICES], U32)
        rows = sb("rows1", [P, CHOICES, D])
        f = sb("f", [P, QT, D])
        ft = sb("ft", [P, QT, D])
        stats = sb("stats1", [P, QT, 6])
        mv = sb("mv", [P, 2, QT])
        ve = sb("ve1", [P, QT])
        carrier = sb("carrier", [P, 2])
        ready = sb("ready", [P, 2])
        w2 = sb("w_2", [P, QT])
        xn = sb("xn1", [P, QT, D])
        xnT = sb("xnT1", [P, KC, T])
        qs = sb("qs1", [P, QT, 4 * D])
        ks = sb("ks1", [P, QT, 4 * D])
        qT = sb("qT1", [P, PAIRS, T], F32R)
        kT = sb("kT1", [P, PAIRS, 2, T], F32R)
        v = sb("v1", [P, QT, H1, 32])
        nmax = sb("nmax1", [P, QT, H1])
        nmaxT = sb("nmaxT1", [H1, 3 * P], F32R)
        p0 = sb("p0_1", [P, 2, 4, T])
        p1 = sb("p1_1", [P, 2, 4, P])
        ctx_sb = sb("ctx_sb1", [P, 2, T])
        rec = sb("rec1", [P, QT, 4])
        cx = sb("cx1", [P, QT, D])
        cxT = sb("cxT1", [P, KC, T])
        s1 = sb("s1", [P, QT, D])
        htanh = sb("htanh", [P, T])
        hmid = sb("hmid", [P, T])
        hid = sb("hid", [P, 2, T])
        down = sb("down", [P, QT, D])
        dtanh = sb("dtanh", [P, QT, D])
        dout = sb("dout", [P, QT, D])
        block = ctx.enter_context(nc.Block())


        @block.sync
        def _(sp):
            for name in counts:
                sp.sem_inc(s[name], 1)
            sp.dma_start(w_qkv[:], a["wqkv1"].rearrange("(c p) n -> p c n", p=P)).then_inc(s["attn_in"], 16)
            sp.dma_start(w_o[:], a["wo1"].rearrange("(c p) n -> p c n", p=P)).then_inc(s["attn_in"], 16)
            full = HID // P
            for name, dst in (("s_gate", s_gate), ("s_up", s_up)):
                sp.dma_start(dst[:, 0:full], a[name]).then_inc(s["ffn_in"], 16)
                sp.dma_start(dst[0:ROWS[-1], full:], a[name + "_rest"]).then_inc(s["ffn_in"], 16)
            sp.dma_start(s_down[:], a["s_down"].partition_broadcast(P)).then_inc(s["ffn_in"], 16)
            sp.dma_start(raw[:], a["w_gate"].rearrange("(c p) n -> p c n", p=P)).then_inc(s["ffn_in"], 16)
            sp.wait_ge(s["prep"], 3)
            sp.dma_start(raw[:], a["w_up"].rearrange("(c p) n -> p c n", p=P)).then_inc(s["ffn_in"], 16)
            sp.wait_ge(s["prep"], 4)
            rd = raw[:].rearrange("p c n -> p (c n)")
            for c in range(HC - 1):
                sp.dma_start(rd[:, c * D:(c + 1) * D], a["w_down"][c * P:(c + 1) * P, :]).then_inc(s["ffn_in"], 16)
            sp.wait_ge(s["prep"], 5)
            sp.dma_start(rd[0:ROWS[-1], 0:D], a["w_down"][(HC - 1) * P:, :]).then_inc(s["ffn_in"], 16)
            sv = s_rows.rearrange("(n p) d -> p n d", p=P)
            ov = out.rearrange("b (i p) d -> p (b i) d", p=P)
            sp.dma_start(s0[:], sv[:, 0:QT, :]).then_inc(s["s_in"], 16)
            def next_rows(b):
                sp.wait_ge(s["x_made"], 1 + QT * b + QT)
                sp.dma_start(s0[:], sv[:, bass.ds(b * QT + QT, QT), :]).then_inc(s["s_in"], 16)

            def batch(b, last):
                def attention():
                    for t in range(27):
                        if t == HEAD_AT + 2 and not last:
                            next_rows(b + 1)
                        yield
                    for g in range(GROUPS):
                        sp.wait_ge(s["key_scores1"], 1 + KEY_FILLS * b + 3 * max(g - 1, 0))
                        if g == 0:
                            sp.wait_ge(s["max_rows1"], 1 + 2 * b + 2)
                        sp.dma_start(m["shift"][0:1, g % 2, :, :].bitcast(F32),
                                     nmaxT[4 * g:4 * g + 4, :].bitcast(F32)).then_inc(shift_in[g % 2], 16)
                        for _ in range(4):
                            yield
                    for _ in range(5):
                        yield
                    sp.wait_ge(s["out_made"], 1 + QT * b + QT)
                    sp.dma_start(ov[:, bass.ds(b * QT, QT), :], dout[:]).then_inc(s["stored"], 16)
                    yield

                for _ in attention():
                    pass

            next_rows(0)
            with sp.Fori(0, B - 1) as b:
                batch(b, False)
            batch(B - 1, True)
            sp.wait_ge(s["stored"], 1 + 16 * B)
            sp.wait_ge(s["s_in"], 1 + 16 * (B + 1))

        @block.gpsimd
        def _(pool):
            pool.memset(ready[:], 0.0).then_inc(s["picked1"], 1)
            pool.wait_ge(s["picked1"], 1 + 1)
            with pool.Fori(0, B) as b:
                pool.wait_ge(s["f_made"], 1 + QT * b)
                nc.gpsimd.tensor_copy(rows_no[:], m["slots"][:, bass.ds(b * QT, QT), :].rearrange("p i k -> p (i k)")
                                      ).then_inc(s["picked1"], 1)
                pool.wait_ge(s["picked1"], 1 + 2 * b + 2)
                nc.gpsimd.tensor_tensor(ready[:, 1:2], ready[:, 0:1], ready[:, 0:1], ALU.add).then_inc(s["picked1"], 1)
                for c in range(CHOICES):
                    nc.gpsimd.indirect_dma_start(rows[:, c, :], None, y_rows,
                                                 bass.IndirectOffsetOnAxis(rows_no[:, c:c + 1], 0)).then_inc(s["rows_in1"], 16)
                pool.wait_ge(s["rows_in1"], 16 * CHOICES * (b + 1))

        @block.tensor
        def _(pe):
            pe.wait_ge(s["attn_in"], 32)
            pe.wait_ge(s["prep"], 9)
            def batch(b, last):
                def attention():
                    yield
                    yield
                    pe.wait_ge(s["xn_made1"], 1 + QT * b + QT)
                    pe.wait_ge(s["s_made1"], 1 + b)
                    for k in range(KC):
                        for i in range(QT):
                            ins = pe.transpose(MISC[:, (k * QT + i) * P:(k * QT + i + 1) * P],
                                               xn[:, i, k * P:(k + 1) * P], m["ident"][:])
                    ins.then_inc(s["xn_turned1"], 1)
                    yield
                    pe.wait_ge(s["xn_cols1"], 1 + b + 1)
                    pe.wait_ge(s["ctx_out1"], 1 + GROUPS * b)
                    for i in range(QT):
                        for k in range(KC):
                            ins = pe.matmul(C[i][:], xnT[:, k, i * P:(i + 1) * P], w_qkv[:, k, 0:2 * D],
                                            start=(k == 0), stop=(k == KC - 1))
                        ins.then_inc(s["qk_psum"], 1)
                    for i in range(QT):
                        for k in range(KC):
                            ins = pe.matmul(MISC[:, i * D:(i + 1) * D], xnT[:, k, i * P:(i + 1) * P], w_qkv[:, k, 2 * D:],
                                            start=(k == 0), stop=(k == KC - 1))
                    ins.then_inc(s["v_psum"], 1)
                    yield
                    yield
                    yield
                    pe.wait_ge(s["probs1"], 1 + KEY_FILLS * b)
                    for f_ in range(8):
                        src = qs if f_ < 4 else ks
                        if f_ == 0:
                            pe.wait_ge(s["stacked1"], 1 + 2 * QT * b + 2 * QT)
                        if 2 <= f_ < 6:
                            pe.wait_ge(s["q_cols1"], 1 + 4 * b + f_ - 1)
                        if f_ >= 6:
                            pe.wait_ge(s["k_low"], 1 + 4 * b + f_ - 5)
                            pe.wait_ge(s["k_high"], 1 + 4 * b + f_ - 5)
                        for c in range(2):
                            for i in range(QT):
                                j = 2 * (f_ % 4) + c
                                ins = pe.transpose(S[f_ % 2][:, (c * QT + i) * P:(c * QT + i + 1) * P],
                                                   src[:, i, j * P:(j + 1) * P], m["ident"][:])
                        ins.then_inc(s["q_turned1" if f_ < 4 else "k_turned1"], 1)
                        yield
                    pe.wait_ge(s["k_low"], 1 + 4 * b + 4)
                    pe.wait_ge(s["k_high"], 1 + 4 * b + 4)
                    for f_ in range(ROW_FILLS):
                        if f_ >= 2:
                            pe.wait_ge(s["row_max1"], 1 + ROW_FILLS * b + f_ - 1)
                        o = S[f_ % 2]
                        if f_ < GROUPS:
                            for c in range(2):
                                j = 2 * f_ + c
                                pe.matmul(o[:, c * T:(c + 1) * T], qT[:, j, 0:P], kT[:, j, :, 0:P], start=True, stop=False)
                                ins = pe.matmul(o[:, c * T:(c + 1) * T], m["ident_bf"][:],
                                                m["row_mask"][:].unsqueeze(1).broadcast_to([P, 2, P]), start=False, stop=True)
                        else:
                            j = f_ - GROUPS
                            pe.matmul(o[:], qT[:, j, P:T], kT[:, j, :, :], start=True, stop=False)
                            ins = pe.matmul(o[:].rearrange("p (g t) -> p g t", g=2)[:, :, P:T], m["ident_bf"][:],
                                            m["row_mask"][:].unsqueeze(1).broadcast_to([P, 2, P]), start=False, stop=True)
                        ins.then_inc(s["row_scores1"], 1)
                        yield
                    pe.wait_ge(s["row_max1"], 1 + ROW_FILLS * b + ROW_FILLS)
                    pe.wait_ge(s["v_cols"], 1 + b + 1)
                    for i in range(QT):
                        ins = pe.transpose(MISC[0:H1, i * P:(i + 1) * P], nmax[:, i, :], m["ident"][:])
                    ins.then_inc(s["max_turned1"], 1)
                    yield

                    def context(g):
                        pe.wait_ge(s["probs1"], 1 + KEY_FILLS * b + 3 * g + 3)
                        if g >= 2:
                            pe.wait_ge(s["ctx_out1"], 1 + GROUPS * b + g - 1)
                        for j in range(4):
                            o, h = C[g % 2][32 * j:32 * j + 32, :], 4 * g + j
                            pe.matmul(o[:, 0:T], v[:, 0, h, :], p0[:, g % 2, j, :], start=True, stop=False)
                            ins = pe.matmul(o[:, P:T], v[:, 1, h, :], p1[:, g % 2, j, :], start=False, stop=True)
                        ins.then_inc(s["ctx_psum1"], 1)

                    def turn_context(g):
                        pe.wait_ge(s["ctx_out1"], 1 + GROUPS * b + g + 1)
                        if g == 0:
                            pe.wait_ge(s["max_rows1"], 1 + 2 * b + 2)
                        else:
                            pe.wait_ge(s["ctx_norm1"], 1 + GROUPS * b + g)
                        for i in range(QT):
                            ins = pe.transpose(MISC[:, i * P:(i + 1) * P], ctx_sb[:, g % 2, i * P:(i + 1) * P], m["ident"][:])
                        ins.then_inc(s["ctx_turned1"], 1)

                    for g in range(GROUPS):
                        pe.wait_ge(shift_in[g % 2], 1 + 16 * (GROUPS // 2 * b + g // 2 + 1))
                        for u in range(3):
                            f_ = 3 * g + u
                            if f_ >= 2:
                                pe.wait_ge(s["probs1"], 1 + KEY_FILLS * b + f_ - 1)
                            o = S[f_ % 2]
                            if u < 2:
                                j = 2 * g + u
                                for c in range(2):
                                    pe.matmul(o[:, c * T:(c + 1) * T], kT[:, j, c, 0:P], qT[:, j, :],
                                              start=(c == 0), stop=False, skip_group_check=True)
                                ins = pe.matmul(o[:], m["step"][:], m["shift"][:, g % 2, 2 * u:2 * u + 2, 0:T],
                                                start=False, stop=True, skip_group_check=True)
                            else:
                                for c in range(4):
                                    j = 2 * g + c // 2
                                    pe.matmul(o[:, c * P:(c + 1) * P], kT[:, j, c % 2, P:T], qT[:, j, P:T],
                                              start=(c == 0), stop=False, skip_group_check=True)
                                ins = pe.matmul(o[:], m["step"][:], m["shift"][:, g % 2, :, T:3 * P],
                                                start=False, stop=True, skip_group_check=True)
                            ins.then_inc(s["key_scores1"], 1)
                            yield
                        if g >= 1:
                            context(g - 1)
                        if g >= 2:
                            turn_context(g - 2)
                        yield
                    context(GROUPS - 1)
                    turn_context(GROUPS - 2)
                    yield
                    turn_context(GROUPS - 1)
                    yield
                    pe.wait_ge(s["ctx_norm1"], 1 + GROUPS * b + GROUPS)
                    for k in range(KC):
                        for i in range(QT):
                            ins = pe.transpose(MISC[:, (k * QT + i) * P:(k * QT + i + 1) * P],
                                               cx[:, i, k * P:(k + 1) * P], m["ident"][:])
                    ins.then_inc(s["cx_turned"], 1)
                    yield
                    pe.wait_ge(s["cx_cols"], 1 + b + 1)
                    for i in range(QT):
                        for k in range(KC):
                            ins = pe.matmul(MISC[:, i * D:(i + 1) * D], cxT[:, k, i * P:(i + 1) * P], w_o[:, k, :],
                                            start=(k == 0), stop=(k == KC - 1))
                    ins.then_inc(s["s_psum1"], 1)
                    yield
                    yield

                def feed_forward():
                    for c in range(HC + 1):
                        if c < HC:
                            r = ROWS[c]
                            if c == 0:
                                pe.wait_ge(s["xn_cols1"], 1 + b + 1)
                            pe.wait_ge(s["hid_made"], 1 + HC * b + c)
                            for n, w in enumerate((w_gate, w_up)):
                                for k in range(KC):
                                    ins = pe.matmul(HB[0:r, n * T:(n + 1) * T], w[:, k, c * P:c * P + r], xnT[:, k, :],
                                                    start=(k == 0), stop=(k == KC - 1))
                            ins.then_inc(s["hid_psum"], 1)
                        if c >= 1:
                            d_ = c - 1
                            r = ROWS[d_]
                            pe.wait_ge(s["hid_made"], 1 + HC * b + d_ + 1)
                            if d_ == 0:
                                pe.wait_ge(s["down_made"], 1 + QT * b)
                            for i, o in enumerate((TB, YB)):
                                ins = pe.matmul(o[:, 0:D], hid[0:r, d_ % 2, i * P:(i + 1) * P], w_down[0:r, d_, :],
                                                start=(d_ == 0), stop=(d_ == HC - 1))
                            ins.then_inc(s["down_psum"], 1)
                        yield

                weave(attention(), feed_forward(), FFN_AT)

            with pe.Fori(0, B - 1) as b:
                batch(b, False)
            batch(B - 1, True)

        @block.scalar
        def _(act):
            def head(b):
                for i in range(QT):
                    act.wait_ge(s["f_made"], 1 + QT * b + i + 1)
                    act.activation(ft[:, i, :], f[:, i, :], ACT.Tanh, scale=0.5).then_inc(s["f_tanh"], 1)

            def batch(b, last):
                def attention():
                    yield
                    yield
                    act.wait_ge(s["xn_turned1"], 1 + b + 1)
                    act.activation(xnT[:].rearrange("p k t -> p (k t)"), MISC[:], ACT.Copy).then_inc(s["xn_cols1"], 1)
                    yield
                    act.wait_ge(s["v_psum"], 1 + b + 1)
                    act.activation(v[:, :, :, 0:HD1], MISC[:].rearrange("p (i h d) -> p i h d", i=QT, d=HD1),
                                   ACT.Copy).then_inc(s["v_cols"], 1)
                    yield
                    yield
                    yield
                    for f_ in range(4):
                        act.wait_ge(s["q_turned1"], 1 + 4 * b + f_ + 1)
                        act.activation(qT[:, 2 * f_:2 * f_ + 2, :].rearrange("p c t -> p (c t)"), S[f_ % 2][:],
                                       ACT.Copy).then_inc(s["q_cols1"], 1)
                        yield
                    for f_ in range(4):
                        act.wait_ge(s["k_turned1"], 1 + 4 * b + f_ + 1)
                        act.activation(kT[0:64, 2 * f_:2 * f_ + 2, 0, :], S[f_ % 2][0:64, :].rearrange("p (c t) -> p c t", c=2),
                                       ACT.Copy).then_inc(s["k_low"], 1)
                        yield
                    for t in range(14, 14 + ROW_FILLS + 1):
                        if t == HEAD_AT and not last:
                            head(b + 1)
                        yield

                    def evacuate(g):
                        act.wait_ge(s["ctx_psum1"], 1 + GROUPS * b + g + 1)
                        act.wait_ge(s["ctx_turned1"], 1 + GROUPS * b + max(g - 1, 0))
                        act.activation(ctx_sb[:, g % 2, :], C[g % 2][:, 0:T], ACT.Copy).then_inc(s["ctx_out1"], 1)

                    for g in range(GROUPS):
                        for u in range(3):
                            f_ = 3 * g + u
                            act.wait_ge(s["key_scores1"], 1 + KEY_FILLS * b + f_ + 1)
                            if u == 0 and g >= 2:
                                act.wait_ge(s["ctx_psum1"], 1 + GROUPS * b + g - 1)
                            dst = (p0[:, g % 2, 2 * u:2 * u + 2, :] if u < 2 else p1[:, g % 2, :, :])
                            act.activation(dst.rearrange("p j q -> p (j q)"), S[f_ % 2][:], ACT.Exp,
                                           scale=float(HD1) ** -0.5).then_inc(s["probs1"], 1)
                            yield
                        if g >= 1:
                            evacuate(g - 1)
                        yield
                    evacuate(GROUPS - 1)
                    yield
                    yield
                    act.wait_ge(s["cx_turned"], 1 + b + 1)
                    act.activation(cxT[:].rearrange("p k t -> p (k t)"), MISC[:], ACT.Copy).then_inc(s["cx_cols"], 1)
                    yield
                    act.wait_ge(s["s_psum1"], 1 + b + 1)
                    act.wait_ge(s["out_mid"], 1 + 2 * QT * b)
                    act.activation(s1[:].rearrange("p i d -> p (i d)"), MISC[:], ACT.Copy).then_inc(s["s_made1"], 1)
                    yield
                    for i in range(QT):
                        act.wait_ge(s["down_made"], 1 + QT * b + i + 1)
                        act.activation(dtanh[:, i, :], down[:, i, :], ACT.Tanh, scale=0.5).then_inc(s["out_tanh"], 1)
                    yield

                def feed_forward():
                    for c in range(HC):
                        r = ROWS[c]
                        if c == 0:
                            act.wait_ge(s["prep"], 9)
                        act.wait_ge(s["hid_psum"], 1 + HC * b + c + 1)
                        act.wait_ge(s["hid_mid"], 1 + HC * b + c)
                        act.activation(htanh[0:r, :], HB[0:r, 0:T], ACT.Tanh,
                                       scale=s_gate[0:r, c:c + 1]).then_inc(s["hid_tanh"], 1)
                        yield
                    yield

                weave(attention(), feed_forward(), FFN_AT)

            head(0)
            with act.Fori(0, B - 1) as b:
                batch(b, False)
            batch(B - 1, True)

        @block.vector
        def _(dve):
            V = nc.vector
            full = HID // P
            V.memset(kT[:].rearrange("p h g t -> p (h g t)").bitcast(F32), 0.0).then_inc(s["prep"], 1)
            V.memset(v[:], 0.0).then_inc(s["prep"], 1)
            dve.wait_ge(s["ffn_in"], 16 * 6)
            V.tensor_scalar(w_gate[:], raw[:], -128.0, None, ALU.add).then_inc(s["prep"], 1)
            dve.wait_ge(s["ffn_in"], 16 * 7)
            V.tensor_scalar(w_up[:], raw[:], -128.0, None, ALU.add).then_inc(s["prep"], 1)
            rd = raw[:].rearrange("p c n -> p (c n)")
            dve.wait_ge(s["ffn_in"], 16 * (7 + full))
            V.tensor_scalar(w_down[:, 0:full, :].rearrange("p c n -> p (c n)"), rd[:, 0:full * D], -128.0, None,
                            ALU.add).then_inc(s["prep"], 1)
            dve.wait_ge(s["ffn_in"], 16 * (8 + full))
            V.tensor_scalar(w_down[0:ROWS[-1], full, :], rd[0:ROWS[-1], 0:D], -128.0, None, ALU.add).then_inc(s["prep"], 1)
            dve.wait_ge(s["prep"], 2)
            V.memset(v[:, :, :, HD1:HD1 + 1], 1.0).then_inc(s["prep"], 1)
            V.scalar_tensor_tensor(out=s_both[:, 0:full], in0=s_gate[:, 0:full], scalar=0.5, in1=s_up[:, 0:full],
                                   op0=ALU.mult, op1=ALU.mult).then_inc(s["steps1"], 1)
            V.scalar_tensor_tensor(out=s_both[0:ROWS[-1], full:], in0=s_gate[0:ROWS[-1], full:], scalar=0.5,
                                   in1=s_up[0:ROWS[-1], full:], op0=ALU.mult, op1=ALU.mult).then_inc(s["steps1"], 1)
            dve.wait_ge(s["steps1"], 1 + 2)
            V.tensor_scalar(s_gate[:, 0:full], s_gate[:, 0:full], 0.5, None, ALU.mult).then_inc(s["prep"], 1)
            V.tensor_scalar(s_gate[0:ROWS[-1], full:], s_gate[0:ROWS[-1], full:], 0.5, None, ALU.mult).then_inc(s["prep"], 1)
            BASE = 2
            HEAD = QT * (TOPK + 2 + 2) + 3 + RSQRT_STEPS
            STEPS = 2 * QT + GROUPS
            def head(b):
                c = Chain(dve, s["head_steps"], 1 + b * HEAD)
                xs = [x[:, bass.ds(b * QT + i, 1), :].rearrange("p o d -> p (o d)") for i in range(QT)]
                dve.wait_ge(s["rows_in1"], 16 * CHOICES * (b + 1))
                dve.wait_ge(s["s_in"], 1 + 16 * (b + 1))
                for i in range(QT):
                    n = b * QT + i
                    c.then(V.tensor_scalar(f[:, i, :], xs[i], mr[:, 0, bass.ds(n, 1)], mr[:, 1, bass.ds(n, 1)],
                                           ALU.subtract, ALU.mult))
                for k in range(TOPK):
                    c.wait()
                    for i in range(QT):
                        ins = V.scalar_tensor_tensor(out=f[:, i, :], in0=rows[:, i * TOPK + k, :],
                                                     scalar=m["gates"][:, bass.ds(b * QT + i, 1), k], in1=f[:, i, :],
                                                     op0=ALU.mult, op1=ALU.add)
                        if k < TOPK - 1:
                            c.then(ins)
                        else:
                            ins.then_inc(s["f_made"], 1)
                yield
                for i in range(QT):
                    dve.wait_ge(s["f_tanh"], 1 + QT * b + i + 1)
                    c.then(V.scalar_tensor_tensor(out=ft[:, i, :], in0=ft[:, i, :], scalar=1.0, in1=f[:, i, :],
                                                  op0=ALU.add, op1=ALU.mult))
                c.wait()
                for i in range(QT):
                    c.then(V.scalar_tensor_tensor(out=ft[:, i, :], in0=ft[:, i, :], scalar=0.5, in1=s0[:, i, :],
                                                  op0=ALU.mult, op1=ALU.mult))
                c.wait()
                for i in range(QT):
                    V.tensor_tensor(xs[i], xs[i], ft[:, i, :], ALU.add).then_inc(s["x_made"], 1)
                yield
                dve.wait_ge(s["x_made"], 1 + QT * b + QT)
                c.then(V.memset(carrier[:, 0:1], 0.0))
                for i in range(QT):
                    c.then(V.bn_stats(stats[:, i, :], xs[i]))
                c.wait()
                c.then(V.memset(carrier[:, 1:2], 0.0))
                for i in range(QT):
                    c.then(V.bn_aggr(mv[:, :, i], stats[:, i, :]))
                c.wait()
                c.link(V.tensor_scalar(ve[:], mv[:, 1, :], EPS, None, ALU.add))
                rsqrt(nc, c, ve[:], mv[:, 1, :], w2[:])
                dve.wait_ge(s["xn_turned1"], 1 + b)
                for i in range(QT):
                    V.tensor_scalar(xn[:, i, :], xs[i], mv[:, 0, i:i + 1], mv[:, 1, i:i + 1],
                                    ALU.subtract, ALU.mult).then_inc(s["xn_made1"], 1)
                assert c.n == HEAD, c.n
            def batch(b, last):
                c = Chain(dve, s["steps1"], 1 + b * STEPS + BASE)
                xs = [x[:, bass.ds(b * QT + i, 1), :].rearrange("p o d -> p (o d)") for i in range(QT)]

                def normalise(g):
                    dve.wait_ge(s["ctx_turned1"], 1 + GROUPS * b + g + 1)
                    o = MISC[:, 0:T].rearrange("p (i j r) -> p i j r", i=QT, j=4)
                    c.link(V.reciprocal(rec[:], o[:, :, :, HD1]))
                    V.tensor_tensor(cx[:, :, 64 * g:64 * g + 64].rearrange("p i (j d) -> p i j d", j=4), o[:, :, :, 0:HD1],
                                    rec[:].unsqueeze(3).broadcast_to([P, QT, 4, HD1]), ALU.mult).then_inc(s["ctx_norm1"], 1)

                def attention():
                    coming = iter(()) if last else head(b + 1)
                    for _ in range(4):
                        yield
                    for i in range(QT):
                        dve.wait_ge(s["qk_psum"], 1 + QT * b + i + 1)
                        q = C[i][:, 0:D].rearrange("p (n o d) -> p n o d", o=1, d=HD1).broadcast_to([P, H1, 2, HD1])
                        k = C[i][:, D:2 * D].rearrange("p (n o d) -> p n o d", o=1, d=HD1).broadcast_to([P, H1, 2, HD1])
                        q4 = qs[:, i, :].rearrange("p (n r c d) -> p n r c d", r=2, c=2, d=HD1)
                        k4 = ks[:, i, :].rearrange("p (n r c d) -> p n r c d", r=2, c=2, d=HD1)
                        c.then(V.tensor_copy(q4[:, :, 0, :, :].bitcast(F32R), q))
                        c.link(V.tensor_copy(k4[:, :, :, 0, :].bitcast(F32R), k))
                        V.tensor_tensor(q4[:, :, 1, :, :].bitcast(F32R), q, q4[:, :, 0, :, :],
                                        ALU.subtract).then_inc(s["stacked1"], 1)
                        V.tensor_tensor(k4[:, :, :, 1, :].bitcast(F32R), k, k4[:, :, :, 0, :],
                                        ALU.subtract).then_inc(s["stacked1"], 1)
                        yield
                    for _ in range(4):
                        yield
                    for f_ in range(4):
                        dve.wait_ge(s["k_turned1"], 1 + 4 * b + f_ + 1)
                        V.tensor_copy(kT[64:P, 2 * f_:2 * f_ + 2, 1, :],
                                      S[f_ % 2][64:P, :].rearrange("p (c t) -> p c t", c=2)).then_inc(s["k_high"], 1)
                        yield
                    for f_ in range(ROW_FILLS):
                        dve.wait_ge(s["row_scores1"], 1 + ROW_FILLS * b + f_ + 1)
                        o = S[f_ % 2]
                        if f_ < GROUPS:
                            dst, src = nmax[:, 0, 4 * f_:4 * f_ + 4], o[:].rearrange("p (g t) -> p g t", g=4)
                        else:
                            j = f_ - GROUPS
                            dst, src = nmax[:, 1, 2 * j:2 * j + 2], o[:].rearrange("p (g t) -> p g t", g=2)
                        V.tensor_reduce(dst, src, AX.X, ALU.max, negate=True).then_inc(s["row_max1"], 1)
                        if 14 + f_ in (HEAD_AT, HEAD_AT + 1, HEAD_AT + 2):
                            next(coming, None)
                        yield
                    dve.wait_ge(s["max_turned1"], 1 + b + 1)
                    for u in range(2):
                        dve.wait_ge(shift_in[u], 1 + 16 * (GROUPS // 2) * b)
                    V.tensor_copy(nmaxT[:, 0:T], MISC[0:H1, 0:T]).then_inc(s["max_rows1"], 1)
                    V.tensor_copy(nmaxT[:, T:], MISC[0:H1, P:T]).then_inc(s["max_rows1"], 1)
                    yield
                    for g in range(GROUPS):
                        for _ in range(3):
                            yield
                        if g >= 2:
                            normalise(g - 2)
                        yield
                    normalise(GROUPS - 2)
                    yield
                    normalise(GROUPS - 1)
                    yield
                    yield
                    yield
                    for i, o in enumerate((TB, YB)):
                        if i == 0:
                            dve.wait_ge(s["down_psum"], 1 + HC * b + HC)
                        V.tensor_tensor(down[:, i, :], o[:, 0:D], s_down[:], ALU.mult).then_inc(s["down_made"], 1)
                    yield
                    for i in range(QT):
                        dve.wait_ge(s["out_tanh"], 1 + QT * b + i + 1)
                        V.scalar_tensor_tensor(out=dtanh[:, i, :], in0=dtanh[:, i, :], scalar=1.0, in1=down[:, i, :],
                                               op0=ALU.add, op1=ALU.mult).then_inc(s["out_mid"], 1)
                    dve.wait_ge(s["s_made1"], 1 + b + 1)
                    dve.wait_ge(s["out_mid"], 1 + 2 * QT * b + QT)
                    for i in range(QT):
                        V.scalar_tensor_tensor(out=dtanh[:, i, :], in0=dtanh[:, i, :], scalar=0.5, in1=s1[:, i, :],
                                               op0=ALU.mult, op1=ALU.mult).then_inc(s["out_mid"], 1)
                    dve.wait_ge(s["out_mid"], 1 + 2 * QT * b + 2 * QT)
                    dve.wait_ge(s["stored"], 1 + 16 * b)
                    for i in range(QT):
                        V.tensor_tensor(dout[:, i, :], xs[i], dtanh[:, i, :], ALU.add).then_inc(s["out_made"], 1)

                def feed_forward():
                    for c_ in range(HC):
                        r = ROWS[c_]
                        dve.wait_ge(s["hid_tanh"], 1 + HC * b + c_ + 1)
                        V.scalar_tensor_tensor(out=hmid[0:r, :], in0=htanh[0:r, :], scalar=1.0, in1=HB[0:r, 0:T],
                                               op0=ALU.add, op1=ALU.mult).then_inc(s["hid_mid"], 1)
                        dve.wait_ge(s["hid_mid"], 1 + HC * b + c_ + 1)
                        if c_ >= 2:
                            dve.wait_ge(s["down_psum"], 1 + HC * b + c_ - 1)
                        else:
                            dve.wait_ge(s["down_psum"], 1 + HC * b)
                        V.scalar_tensor_tensor(out=hid[0:r, c_ % 2, :], in0=HB[0:r, T:2 * T], scalar=s_both[0:r, c_:c_ + 1],
                                               in1=hmid[0:r, :], op0=ALU.mult, op1=ALU.mult).then_inc(s["hid_made"], 1)
                        yield
                    yield

                weave(attention(), feed_forward(), FFN_AT)
                assert c.n == STEPS, (c.n, STEPS)

            for _ in head(0):
                pass
            with dve.Fori(0, B - 1) as b:
                batch(b, False)
            batch(B - 1, True)


def constants():
    bf16 = mybir.dt.np(BF16)
    r, c = np.arange(P)[:, None], np.arange(P)[None, :]
    step = np.where((r == 0) | (r - 1 < c), 1.0, 0.0).astype(np.float32)
    beyond = np.where((r > 0) & (r - 1 >= c), -BIG, 0.0).astype(np.float32)
    half = HD0 // 2
    freq = (1.0 / 10000.0 ** (np.arange(half, dtype=np.float32) * 2.0 / HD0)).astype(np.float32)
    ang = np.arange(T, dtype=np.float32)[:, None] * freq[None, :]
    cos, sin = np.cos(ang).astype(np.float32), np.sin(ang).astype(np.float32)
    e = np.arange(E)
    pick = np.zeros((P, E, P), np.float32)
    for part in range(3):
        for n in range(E):
            pick[32 * part + n, n, :] = 1.0
    return {
        "ident": np.eye(P, dtype=np.float32), "ident_bf": np.eye(P).astype(bf16),
        "row_mask": np.where(c > r, -BIG, 0.0).astype(bf16),
        "step": step, "shift": np.concatenate([beyond, 0 * beyond, beyond], 1),
        "before": np.where(r < c, 1.0, 0.0).astype(bf16),
        "multiples": np.broadcast_to(np.arange(NT, dtype=np.float32) * P, (P, NT)).copy(),
        "upto": np.broadcast_to((e[None, :] <= e[:, None]).astype(np.float32), (P, E, E)).copy(),
        "block_no": np.arange(BLOCKS, dtype=np.float32)[None],
        "token_no": (np.arange(NT)[None] * P + np.arange(P)[:, None]).astype(np.uint32),
        "pick": pick.astype(bf16),
        "cos": np.concatenate([cos, cos], 1).reshape(QT, P, HD0).transpose(1, 0, 2).copy(),
        "sin": np.concatenate([-sin, sin], 1).reshape(QT, P, HD0).transpose(1, 0, 2).copy(),
    }


def layout(inputs):
    g = {k: np.asarray(v) for k, v in inputs.items()}
    wq = g["L0_attn_Wq"].reshape(D, 2, 4, 4, HD0).transpose(0, 1, 3, 2, 4).reshape(D, D)
    full = HID // P * P
    w1 = g["L0_ffn_w1"]
    return {
        "x": g["L0_attn_x"],
        "wqkv0": np.concatenate([wq, g["L0_attn_Wk"], g["L0_attn_Wv"]], 1),
        "wo0": g["L0_attn_Wo"],
        "norm_w": g["L0_ffn_norm_w"][None], "gate_w": g["L0_ffn_gate_w"].T, "gate_b": g["L0_ffn_gate_b"][None],
        "w1": w1.reshape(E, I, 2, D).transpose(3, 0, 2, 1).reshape(D, E * 2 * I),
        "w2": g["L0_ffn_w2"].transpose(2, 0, 1).reshape(I, E * D),
        "b12": np.concatenate([g["L0_ffn_b1"].reshape(E, I, 2).transpose(0, 2, 1).reshape(E, 2 * I),
                               g["L0_ffn_b2"]], 1),
        "wqkv1": np.concatenate([g["L1_attn_wq"].T, g["L1_attn_wk"].T, g["L1_attn_wv"].T], 1),
        "wo1": g["L1_attn_wo"].T,
        "w_gate": g["L1_ffn_wq_gate"].T, "w_up": g["L1_ffn_wq_up"].T, "w_down": g["L1_ffn_wq_down"].T,
        **{name + end: part for name in ("s_gate", "s_up") for end, part in (
            ("", g["L1_ffn_" + name][:full].reshape(-1, P).T), ("_rest", g["L1_ffn_" + name][full:, None]))},
        "s_down": g["L1_ffn_s_down"][None],
    }


def kernel(**inputs):
    import concourse.bacc as bacc
    from concourse.bass_utils import run_bass_kernel_spmd

    nc = bacc.Bacc("TRN2", target_bir_lowering=False, num_devices=1)
    arrays, a = {}, {}
    for name, v in {**layout(inputs), **constants()}.items():
        v = np.ascontiguousarray(v)
        arrays[f"in_{name}"] = v
        a[name] = nc.dram_tensor(f"in_{name}", v.shape, mybir.dt.from_np(v.dtype), kind="ExternalInput").ap()
    out = nc.dram_tensor("out_x", [B, T, D], F32, kind="ExternalOutput").ap()
    build(nc, a, out)
    r = run_bass_kernel_spmd(nc, [arrays], core_ids=[0])
    return r.results[0]["out_x"]
```

```python
from contextlib import ExitStack

import numpy as np

import concourse.bass as bass
from concourse import mybir

ALU = mybir.AluOpType
ACT = mybir.ActivationFunctionType
AX = mybir.AxisListType
F32 = mybir.dt.float32
F32R = mybir.dt.float32r
BF16 = mybir.dt.bfloat16
I32 = mybir.dt.int32
U32 = mybir.dt.uint32

P = 128
B, T, D = 8, 256, 256
QT = T // P
KC = D // P
NT = B * QT
H0, G0, HD0 = 32, 8, 8
H1, HD1 = 16, 16
E, TOPK, I = 16, 4, 256
BLOCKS = NT * TOPK + E - 1
BPB = 12
HID = 704
HC = (HID + P - 1) // P
ROWS = [min(P, HID - c * P) for c in range(HC)]
EPS = 1e-5
BIG = float(2.0 ** 100)
ALPHA, LIMIT = 1.702, 7.0
NOT_A_LOGIT = -3.0e38
CHOSEN = 3.0e38


def build(nc, a, out):
    tokens = nc.dram_tensor("expert_tokens", [BLOCKS * P, 1], U32).ap()
    t_rows = nc.dram_tensor("normed_rows", [NT * P, D], F32).ap()
    y_rows = nc.dram_tensor("expert_rows", [BLOCKS * P, D], F32).ap()
    s_rows = nc.dram_tensor("attention_rows", [(NT + QT) * P, D], F32).ap()
    with ExitStack() as ctx:
        def sb(name, shape, dt=F32):
            return ctx.enter_context(nc.sbuf_tensor(name, shape, dt))

        m = {}
        m["x"] = sb("x", [P, NT, D])
        m["mean_rstd"] = sb("mean_rstd", [P, 2, NT])
        m["ident"] = sb("ident", [P, P])
        m["ident_bf"] = sb("ident_bf", [P, P], BF16)
        m["row_mask"] = sb("row_mask", [P, P], BF16)
        m["step"] = sb("step", [P, P], F32R)
        m["shift"] = sb("shift", [P, 2, 4, 3 * P], F32R)
        m["slots"] = sb("slots", [P, NT + QT, TOPK], U32)
        m["gates"] = sb("gates", [P, NT, TOPK])
        m["block_expert"] = sb("block_expert", [1, BLOCKS], I32)
        m["block_tokens"] = sb("block_tokens", [P, BLOCKS], U32)
        m["token_no"] = sb("token_no", [P, NT], U32)
        m["w_qkv"] = sb("w_qkv", [P, KC, D + 2 * G0 * HD0])
        m["w_o"] = sb("w_o", [P, QT, D])
        m["cos"] = sb("cos", [P, QT, HD0])
        m["sin"] = sb("sin", [P, QT, HD0])
        m["bank"] = [ctx.enter_context(nc.psum_tensor(f"bank{i}", [P, 512], F32)) for i in range(8)]
        route(nc, a, m, tokens, t_rows)
        layer0(nc, a, m, tokens, t_rows, y_rows, s_rows)
        layer1(nc, a, m, y_rows, s_rows, out)


def sems(nc, ctx, names):
    return {n: ctx.enter_context(nc.semaphore(n)) for n in names}


class Chain:

    def __init__(self, eng, sem, base=0):
        self.eng, self.sem, self.base, self.n = eng, sem, base, 0

    def then(self, ins):
        self.n += 1
        ins.then_inc(self.sem, 1)
        return ins

    def wait(self):
        self.eng.wait_ge(self.sem, self.base + self.n)

    def link(self, ins):
        self.then(ins)
        self.wait()


RSQRT_STEPS = 14


def rsqrt(nc, c, v, y, w):
    c.link(nc.vector.tensor_single_scalar(w.bitcast(I32), v.bitcast(I32), 1, ALU.logical_shift_right))
    c.link(nc.vector.tensor_scalar(y.bitcast(I32), w.bitcast(I32), -1.0, float(0x5F3759DF), ALU.mult, ALU.add))
    for _ in range(4):
        c.link(nc.vector.tensor_tensor(w, y, y, ALU.mult))
        c.link(nc.vector.scalar_tensor_tensor(out=w, in0=w, scalar=-0.5, in1=v, op0=ALU.mult, op1=ALU.mult))
        c.link(nc.vector.scalar_tensor_tensor(out=y, in0=w, scalar=1.5, in1=y, op0=ALU.add, op1=ALU.mult))


def route(nc, a, m, tokens, t_rows):
    x, mr, bank = m["x"], m["mean_rstd"], m["bank"]
    CH = 4
    with ExitStack() as ctx:
        def sb(name, shape, dt=F32):
            return ctx.enter_context(nc.sbuf_tensor(name, shape, dt))

        s = sems(nc, ctx, "x_in consts_in vec t_made t_stored t_turned t_cols logit_psum logits "
                          "exp_in exp_out mask_bf counted attention_in "
                          "pool_set dma_zero".split())
        stats = sb("stats", [P, NT, 6])
        rms = sb("rms", [P, NT])
        ve = sb("ve", [P, NT])
        w16 = sb("w16", [P, NT])
        eps = sb("eps", [P, NT])
        norm_w = sb("norm_w", [P, D])
        gate_w = sb("gate_w", [P, KC, E])
        gate_b = sb("gate_b", [P, E])
        xn = sb("xn_r", [P, QT, D])
        t = sb("t_r", [P, QT, D])
        tT = sb("tT_r", [P, KC, QT * P])
        lg = sb("lg", [P, NT, E + 4])
        top = sb("top", [P, NT, 8])
        marks = sb("marks", [P, NT, 8])
        repl = sb("repl", [P, NT, E + 4])
        mk = sb("mk", [P, NT, E])
        mk_bf = sb("mk_bf", [P, NT, E], BF16)
        ex = sb("ex", [P, NT, E])
        ge = sb("ge", [P, NT, E])
        den = sb("den", [P, NT])
        tot = sb("tot", [P, NT, E])
        cum = sb("cum", [P, NT + 1, E])
        cmp = sb("cmp", [P, E, NT])
        need = sb("need", [P, E])
        end = sb("end", [P, E])
        start = sb("start", [P, E])
        where = sb("where", [P, NT, E])
        best = sb("best", [P, NT, 8])
        cmp_n = sb("cmp_n", [1, BLOCKS, E])
        exp_n = sb("exp_n", [1, BLOCKS])
        before = sb("before", [P, P], BF16)
        ones = sb("ones", [P, P], BF16)
        multiples = sb("multiples", [P, NT])
        upto = sb("upto", [P, E, E])
        block_no = sb("block_no", [1, BLOCKS])
        step_f = sb("step_f", [P, P])
        shift_f = sb("shift_f", [P, 3 * P])
        zeros = sb("zeros", [BLOCKS, P], U32)

        block = ctx.enter_context(nc.Block())

        @block.sync
        def _(sp):
            for name in ("t_made", "t_stored", "t_turned", "t_cols", "logit_psum", "logits", "vec"):
                sp.sem_inc(s[name], 1)
            xv = a["x"].rearrange("b (i p) d -> p (b i) d", p=P)
            for c in range(NT // CH):
                sp.dma_start(x[:, c * CH:(c + 1) * CH, :], xv[:, c * CH:(c + 1) * CH, :]).then_inc(s["x_in"], 16)
                if c == 0:
                    n = 0
                    for dst, src in ((m["ident"][:], a["ident"]), (m["ident_bf"][:], a["ident_bf"]),
                                     (m["row_mask"][:], a["row_mask"]), (step_f[:], a["step"]),
                                     (shift_f[:], a["shift"]), (before[:], a["before"]),
                                     (multiples[:], a["multiples"]), (upto[:], a["upto"]),
                                     (block_no[:], a["block_no"]), (m["token_no"][:], a["token_no"]),
                                     (gate_w[:], a["gate_w"].rearrange("(c p) e -> p c e", p=P)),
                                     (gate_b[:], a["gate_b"].partition_broadcast(P)),
                                     (norm_w[:], a["norm_w"].partition_broadcast(P))):
                        sp.dma_start(dst, src).then_inc(s["consts_in"], 16)
                        n += 1
                    assert n == CONSTS
                sp.wait_ge(s["x_in"], 16 * (c + 1))
            for dst, src in ((m["w_qkv"][:], a["wqkv0"].rearrange("(c p) n -> p c n", p=P)),
                             (m["w_o"][:], a["wo0"].rearrange("(c p) n -> p c n", p=P)),
                             (m["cos"][:], a["cos"]), (m["sin"][:], a["sin"])):
                sp.dma_start(dst, src).then_inc(s["attention_in"], 16)
            with sp.Fori(0, B) as b:
                sp.wait_ge(s["t_made"], 1 + QT * b + QT)
                sp.dma_start(t_rows.rearrange("(i p) d -> p i d", p=P)[:, bass.ds(b * QT, QT), :],
                             t[:]).then_inc(s["t_stored"], 16)
            sp.wait_ge(s["t_stored"], 1 + 16 * B)
            sp.wait_ge(s["pool_set"], 1)
            sp.dma_start(tokens.rearrange("(n p) o -> n (p o)", p=P), zeros[:]).then_inc(s["dma_zero"], 16)
            sp.wait_ge(s["dma_zero"], 16)
            sp.wait_ge(s["attention_in"], 16 * 4)

        @block.gpsimd
        def _(pool):
            pool.memset(zeros[:], 0).then_inc(s["pool_set"], 1)

        @block.tensor
        def _(pe):
            pe.wait_ge(s["consts_in"], 16 * CONSTS)
            with pe.Fori(0, B) as b:
                pe.wait_ge(s["t_made"], 1 + QT * b + QT)
                for k in range(KC):
                    for i in range(QT):
                        ins = pe.transpose(bank[0][:, (k * QT + i) * P:(k * QT + i + 1) * P],
                                           t[:, i, k * P:(k + 1) * P], m["ident"][:])
                ins.then_inc(s["t_turned"], 1)
                pe.wait_ge(s["t_cols"], 1 + b + 1)
                pe.wait_ge(s["logits"], 1 + b)
                for i in range(QT):
                    for k in range(KC):
                        ins = pe.matmul(bank[1][:, i * E:(i + 1) * E], tT[:, k, i * P:(i + 1) * P],
                                        gate_w[:, k, :], start=(k == 0), stop=(k == KC - 1))
                ins.then_inc(s["logit_psum"], 1)
            pe.wait_ge(s["mask_bf"], 1)
            pe.matmul(bank[2][:, 0:NT * E], before[:], mk_bf[:].rearrange("p n e -> p (n e)"), start=True, stop=True)
            pe.matmul(bank[3][:, 0:NT * E], ones[:], mk_bf[:].rearrange("p n e -> p (n e)"),
                      start=True, stop=True).then_inc(s["counted"], 1)

        @block.scalar
        def _(act):
            with act.Fori(0, B) as b:
                act.wait_ge(s["t_turned"], 1 + b + 1)
                act.activation(tT[:].rearrange("p k t -> p (k t)"), bank[0][:], ACT.Copy).then_inc(s["t_cols"], 1)
            act.wait_ge(s["exp_in"], 1)
            act.activation(ex[:], ex[:], ACT.Exp).then_inc(s["exp_out"], 1)

        @block.vector
        def _(dve):
            c = Chain(dve, s["vec"], 1)
            c.then(dve.memset(ones[:], 1.0))
            c.then(dve.memset(lg[:, :, E:], NOT_A_LOGIT))
            c.then(dve.memset(marks[:, :, TOPK:], NOT_A_LOGIT))
            c.then(dve.memset(cum[:, 0, :], 0.0))
            c.then(dve.memset(m["slots"][:, NT:, :], 0))
            dve.wait_ge(s["consts_in"], 16 * CONSTS)
            c.then(dve.tensor_copy(m["step"][:], step_f[:]))
            for n in range(2):
                for j in range(4):
                    c.then(dve.tensor_copy(m["shift"][:, n, j, :], shift_f[:]))
            for n in range(NT):
                if n % CH == 0:
                    dve.wait_ge(s["x_in"], 16 * (n // CH + 1))
                c.then(dve.bn_stats(stats[:, n, :], x[:, n, :]))
            c.wait()
            for n in range(NT):
                c.then(dve.bn_aggr(mr[:, :, n], stats[:, n, :]))
            c.wait()
            c.link(dve.tensor_scalar(ve[:], mr[:, 1, :], EPS, None, ALU.add))
            c.link(dve.tensor_copy(den[:], mr[:, 1, :]))
            rsqrt(nc, c, ve[:], mr[:, 1, :], w16[:])
            c.link(dve.tensor_tensor(w16[:], mr[:, 1, :], mr[:, 1, :], ALU.mult))
            c.link(dve.tensor_tensor(ve[:], w16[:], den[:], ALU.mult))
            c.link(dve.tensor_scalar(ve[:], ve[:], EPS, None, ALU.add))
            rsqrt(nc, c, ve[:], rms[:], w16[:])
            base = c.n
            with dve.Fori(0, B) as b:
                dve.wait_ge(s["t_turned"], 1 + b)
                dve.wait_ge(s["t_stored"], 1 + 16 * b)
                for i in range(QT):
                    n = b * QT + i
                    dve.tensor_scalar(xn[:, i, :], x[:, bass.ds(n, 1), :].rearrange("p o d -> p (o d)"),
                                      mr[:, 0, bass.ds(n, 1)], mr[:, 1, bass.ds(n, 1)],
                                      ALU.subtract, ALU.mult).then_inc(s["vec"], 1)
                dve.wait_ge(s["vec"], 1 + b * QT + (base + QT))
                for i in range(QT):
                    dve.scalar_tensor_tensor(out=t[:, i, :], in0=xn[:, i, :], scalar=rms[:, bass.ds(b * QT + i, 1)],
                                             in1=norm_w[:], op0=ALU.mult, op1=ALU.mult).then_inc(s["t_made"], 1)
                dve.wait_ge(s["logit_psum"], 1 + b + 1)
                dve.tensor_tensor(lg[:, bass.ds(b * QT, QT), 0:E], bank[1][:, 0:QT * E].rearrange("p (i e) -> p i e", i=QT),
                                  gate_b[:].unsqueeze(1).broadcast_to([P, QT, E]), ALU.add).then_inc(s["logits"], 1)
            c.n += B * QT
            dve.wait_ge(s["logits"], 1 + B)
            for n in range(NT):
                c.then(dve.max(top[:, n, :], lg[:, n, 0:E]))
            c.wait()
            c.link(dve.tensor_copy(marks[:, :, 0:TOPK], top[:, :, 0:TOPK]))
            for n in range(NT):
                c.then(dve.match_replace(repl[:, n, :], marks[:, n, :], lg[:, n, :], CHOSEN))
            c.wait()
            c.link(dve.tensor_tensor(mk[:], repl[:, :, 0:E], lg[:, :, 0:E], ALU.not_equal))
            dve.tensor_copy(mk_bf[:], mk[:]).then_inc(s["mask_bf"], 1)
            dve.tensor_tensor(ex[:], lg[:, :, 0:E], top[:, :, 0:1].broadcast_to([P, NT, E]),
                              ALU.subtract).then_inc(s["exp_in"], 1)
            dve.wait_ge(s["exp_out"], 1)
            c.link(dve.tensor_tensor(ge[:], ex[:], mk[:], ALU.mult))
            c.link(dve.tensor_reduce(den[:], ge[:], AX.X, ALU.add))
            c.link(dve.reciprocal(w16[:], den[:]))
            c.then(dve.tensor_tensor(ge[:], ge[:], w16[:].unsqueeze(2).broadcast_to([P, NT, E]), ALU.mult))
            dve.wait_ge(s["counted"], 1)
            c.link(dve.tensor_copy(tot[:].rearrange("p n e -> p (n e)"), bank[3][:, 0:NT * E]))
            for n in range(NT):
                c.link(dve.tensor_tensor(cum[:, n + 1, :], cum[:, n, :], tot[:, n, :], ALU.add))
            c.link(dve.tensor_tensor(cmp[:], cum[:, NT, :].unsqueeze(2).broadcast_to([P, E, NT]),
                                     multiples[:].unsqueeze(1).broadcast_to([P, E, NT]), ALU.is_gt))
            c.link(dve.tensor_reduce(need[:], cmp[:], AX.X, ALU.add))
            c.link(dve.tensor_tensor(cmp[:], need[:].unsqueeze(1).broadcast_to([P, E, E]), upto[:], ALU.mult))
            c.link(dve.tensor_reduce(end[:], cmp[:], AX.X, ALU.add))
            c.link(dve.tensor_tensor(start[:], end[:], need[:], ALU.subtract))
            c.link(dve.tensor_scalar(start[:], start[:], float(P), 1.0, ALU.mult, ALU.add))
            c.link(dve.tensor_tensor(where[:].rearrange("p n e -> p (n e)"), bank[2][:, 0:NT * E],
                                     cum[:, 0:NT, :].rearrange("p n e -> p (n e)"), ALU.add))
            c.link(dve.tensor_tensor(where[:], where[:], start[:].unsqueeze(1).broadcast_to([P, NT, E]), ALU.add))
            c.link(dve.tensor_tensor(where[:], where[:], mk[:], ALU.mult))
            for n in range(NT):
                c.then(dve.max(best[:, n, :], where[:, n, :]))
            c.wait()
            dve.tensor_scalar(m["slots"][:, 0:NT, :], best[:, :, 0:TOPK], -1.0, None, ALU.add).then_inc(s["counted"], 2)
            for k in range(TOPK):
                c.link(dve.tensor_tensor(ex[:], where[:], best[:, :, k:k + 1].broadcast_to([P, NT, E]), ALU.is_equal))
                c.link(dve.tensor_tensor(ex[:], ex[:], ge[:], ALU.mult))
                c.link(dve.tensor_reduce(m["gates"][:, :, k], ex[:], AX.X, ALU.add))
            c.link(dve.tensor_tensor(cmp_n[:], end[0:1, :].unsqueeze(1).broadcast_to([1, BLOCKS, E]),
                                     block_no[:].unsqueeze(2).broadcast_to([1, BLOCKS, E]), ALU.is_le))
            c.link(dve.tensor_reduce(exp_n[:], cmp_n[:], AX.X, ALU.add))
            c.link(dve.tensor_scalar(m["block_expert"][:], exp_n[:], float(E - 1), None, ALU.min))


CONSTS = 13


def weave(attention, other, steps):
    tick, attending, beside = 0, True, True
    while attending or beside:
        if attending:
            attending = next(attention, "end") != "end"
        for _ in range(steps.get(tick, 0) if attending else 1):
            beside = beside and next(other, "end") != "end"
        tick += 1


def batches(eng, batch):
    batch(0, 0, 0, 0)
    with eng.Fori(1, B - 1) as b:
        batch(b, b * BPB - BPB, b * (BPB // 2) - BPB // 2, BPB)
    done = (B - 2) * BPB
    batch(B - 1, done, done // 2, BLOCKS - done)


def layer0(nc, a, m, tokens, t_rows, y_rows, s_rows):
    x, mr, bank = m["x"], m["mean_rstd"], m["bank"]
    S, C, MISC, HB, TB, YB = bank[0:2], bank[2:4], bank[4], bank[5], bank[6], bank[7]
    RING = bank[0:4]
    HJ = H0 // 4
    QKV = D + 2 * G0 * HD0
    ROT = D + G0 * HD0
    ROW_FILLS, KEY_FILLS = 3 * HJ, 3 * G0
    EXPERTS_AT = {1: 1, 2: 3, 3: 4, 33: 4, 66: 1, 67: 2, 68: 2, 69: 2,
                  **{t: 1 for t in range(10, 33, 2)}, **{t: 1 for t in range(35, 66, 2)}}
    with ExitStack() as ctx:
        def sb(name, shape, dt=F32):
            return ctx.enter_context(nc.sbuf_tensor(name, shape, dt))

        counts = ("xn_made xn_turned xn_cols qkv_psum rot v_made stacked q_turned q_cols k_turned k_cols "
                          "row_scores row_max max_turned max_rows shift_even shift_odd key_scores probs ctx_psum ctx_out "
                          "ctx_turned ctx_norm norm_steps s_psum s_made s_stored "
                          "picked rows_turned rows_cols hidden gate_in lin_in tanh_done lin_scaled mid acted "
                          "act_turned act_cols y_psum y_made y_stored").split()
        s = sems(nc, ctx, ["weights_in", "experts_in", "parts", "set", "bias_steps", "gathered_even", "gathered_odd",
                          "scattered", "tokens_back", "tokens_f", "tokens_turned", "blocks_known"] + counts)
        gathered = [s["gathered_even"], s["gathered_odd"]]
        w_qkv, w_o, cos, sin = m["w_qkv"], m["w_o"], m["cos"], m["sin"]
        shift_in = [s["shift_even"], s["shift_odd"]]
        w1 = sb("w1", [P, KC, E * 2 * I])
        w2 = sb("w2", [P, KC, E * D])
        pick = sb("pick", [P, E * P], BF16)
        bias = sb("bias", [P, 2 * I + D], BF16)
        xn = sb("xn", [P, QT, D])
        xnT = sb("xnT", [P, KC, T])
        t1 = sb("rot_a", [P, ROT])
        t2 = sb("rot_b", [P, ROT])
        qT = sb("qT", [P, HJ, T], F32R)
        kT = sb("kT", [P, 2, 4, T], F32R)
        v = sb("v", [P, QT, G0, 32])
        nmax = sb("nmax", [P, QT, H0])
        nmaxT = sb("nmaxT", [H0, 3 * P], F32R)
        shared = sb("shared", [P, 3072])
        qs = shared[:, 0:2048].rearrange("p (i n) -> p i n", i=QT)
        ks = shared[:, 2048:2560].rearrange("p (i n) -> p i n", i=QT)
        p0 = shared[:, 0:2048].rearrange("p (u j q) -> p u j q", u=2, j=4)
        p1 = shared[:, 2048:3072].rearrange("p (u j q) -> p u j q", u=2, j=4)
        ctx_sb = sb("ctx_sb", [P, QT, 4 * P])
        rec = sb("rec", [P, 4, 4])
        cx = sb("cx", [P, QT, D])
        s_sb = sb("s_sb", [P, QT, D])
        rows_in = sb("rows_in", [P, 2, D])
        rows_no = sb("rows_no", [P, 2], U32)
        carrier = sb("carrier0", [P, 2])
        rowsT = sb("rowsT", [P, KC * P])
        gate = sb("gate", [P, I])
        lin = sb("lin", [P, I])
        tanh = sb("tanh", [P, I])
        actd = sb("actd", [P, I])
        actT = sb("actT", [P, KC * P])
        y = sb("y", [P, D])
        back = sb("back", [BLOCKS, P], U32)
        back_f = sb("back_f", [BLOCKS, P])
        block = ctx.enter_context(nc.Block())


        @block.sync
        def _(sp):
            for name in counts:
                sp.sem_inc(s[name], 1)
            sp.dma_start(pick[:], a["pick"].rearrange("p e m -> p (e m)")).then_inc(s["weights_in"], 16)
            sp.wait_ge(s["set"], 1)
            for part in range(3):
                sp.dma_start(w2[32 * part:32 * part + E, 0, 0:768], a["b12"]).then_inc(s["weights_in"], 16)
            for k in range(KC):
                sp.dma_start(w1[:, k, :], a["w1"][k * P:(k + 1) * P, :]).then_inc(s["experts_in"], 16)
            sp.wait_ge(s["parts"], 6)
            for k in range(KC):
                sp.dma_start(w2[:, k, :], a["w2"][k * P:(k + 1) * P, :]).then_inc(s["experts_in"], 16)

            def batch(b, first, pairs, blocks):
                def attention():
                    def send_shift(g):
                        sp.wait_ge(s["key_scores"], 1 + KEY_FILLS * b + 3 * max(g - 1, 0))
                        if g == 0:
                            sp.wait_ge(s["max_rows"], 1 + 2 * b + 2)
                        sp.dma_start(m["shift"][0:1, g % 2, :, :].bitcast(F32),
                                     nmaxT[4 * g:4 * g + 4, :].bitcast(F32)).then_inc(shift_in[g % 2], 16)

                    for _ in range(33):
                        yield
                    send_shift(0)
                    send_shift(1)
                    yield
                    for g in range(G0):
                        if 1 <= g < G0 - 1:
                            send_shift(g + 1)
                        for _ in range(4):
                            yield
                    for _ in range(4):
                        yield
                    sp.wait_ge(s["s_made"], 1 + b + 1)
                    sp.dma_start(s_rows.rearrange("(n p) d -> p n d", p=P)[:, bass.ds(b * QT, QT), :],
                                 s_sb[:]).then_inc(s["s_stored"], 16)
                    yield

                def experts():
                    yield
                    for k in range(blocks + 1 if blocks else 0):
                        if k < blocks:
                            yield
                        if k >= 1:
                            yield
                        if k < blocks:
                            yield
                        if k >= 1:
                            sp.wait_ge(s["y_made"], 1 + first + k)
                            sp.dma_start(y_rows[bass.ds((first + k - 1) * P, P), :], y[:]).then_inc(s["y_stored"], 16)
                            yield

                weave(attention(), experts(), EXPERTS_AT)

            batches(sp, batch)
            sp.wait_ge(s["s_made"], 1 + B)
            sp.dma_start(s_rows.rearrange("(n p) d -> p n d", p=P)[:, NT:NT + QT, :], s_sb[:]).then_inc(s["s_stored"], 16)
            sp.wait_ge(s["s_stored"], 1 + 16 * (B + 1))
            sp.wait_ge(s["y_stored"], 1 + 16 * BLOCKS)

        @block.gpsimd
        def _(pool):
            def gather(n, u):
                nc.gpsimd.tensor_copy(rows_no[:, u:u + 1], m["block_tokens"][:, bass.ds(n, 1)]).then_inc(s["picked"], 1)
                pool.wait_ge(s["picked"], 1 + 2 * n + 2)
                nc.gpsimd.tensor_tensor(carrier[:, 1:2], carrier[:, 0:1], carrier[:, 0:1], ALU.add).then_inc(s["picked"], 1)
                nc.gpsimd.indirect_dma_start(rows_in[:, u, :], None, t_rows,
                                             bass.IndirectOffsetOnAxis(rows_no[:, u:u + 1], 0)).then_inc(gathered[u], 16)

            pool.memset(carrier[:], 0.0).then_inc(s["picked"], 1)
            pool.wait_ge(s["picked"], 1 + 1)
            for n in range(NT):
                for k in range(TOPK):
                    pool.indirect_dma_start(tokens, bass.IndirectOffsetOnAxis(m["slots"][:, n, k:k + 1], 0),
                                            m["token_no"][:, n:n + 1], None).then_inc(s["scattered"], 16)
            pool.wait_ge(s["scattered"], 16 * NT * TOPK)
            pool.dma_start(back[:], tokens.rearrange("(n p) o -> n (p o)", p=P)).then_inc(s["tokens_back"], 16)
            pool.wait_ge(s["blocks_known"], 1)
            gather(0, 0)
            gather(1, 1)

            def batch(first, pairs, blocks, ahead):
                for k in range(blocks):
                    if k + 2 < blocks + ahead:
                        pool.wait_ge(s["rows_turned"], 1 + (first + k) + 1)
                        pool.wait_ge(gathered[k % 2], 16 * (pairs + k // 2 + 1))
                        gather(first + k + 2, k % 2)

            with pool.Fori(0, B - 2) as b:
                batch(b * BPB, b * (BPB // 2), BPB, 2)
            done = (B - 2) * BPB
            batch(done, done // 2, BLOCKS - done, 0)
            pool.wait_ge(gathered[0], 16 * ((BLOCKS + 1) // 2))
            pool.wait_ge(gathered[1], 16 * (BLOCKS // 2))

        @block.tensor
        def _(pe):
            pe.wait_ge(s["weights_in"], 16 * 4)
            def batch(b, first, pairs, blocks):
                def attention():
                    yield
                    pe.wait_ge(s["xn_made"], 1 + QT * b + QT)
                    pe.wait_ge(s["s_made"], 1 + b)
                    for k in range(KC):
                        for i in range(QT):
                            ins = pe.transpose(MISC[:, (k * QT + i) * P:(k * QT + i + 1) * P],
                                               xn[:, i, k * P:(k + 1) * P], m["ident"][:])
                    ins.then_inc(s["xn_turned"], 1)
                    yield
                    pe.wait_ge(s["xn_cols"], 1 + b + 1)
                    pe.wait_ge(s["ctx_out"], 1 + 4 * b)
                    for i in range(QT):
                        for k in range(KC):
                            ins = pe.matmul(C[i][:, 0:QKV], xnT[:, k, i * P:(i + 1) * P], w_qkv[:, k, :],
                                            start=(k == 0), stop=(k == KC - 1))
                        ins.then_inc(s["qkv_psum"], 1)
                    yield
                    yield
                    pe.wait_ge(s["probs"], 1 + KEY_FILLS * b)
                    for f in range(4):
                        if f == 0:
                            pe.wait_ge(s["stacked"], 1 + 2 * b + 2)
                        for c in range(2):
                            for i in range(QT):
                                ins = pe.transpose(RING[f][:, (c * QT + i) * P:(c * QT + i + 1) * P],
                                                   qs[:, i, (2 * f + c) * P:(2 * f + c + 1) * P], m["ident"][:])
                        ins.then_inc(s["q_turned"], 1)
                        yield
                    pe.wait_ge(s["xn_cols"], 1 + b + 1)
                    for h in range(2):
                        for i in range(QT):
                            ins = pe.transpose(MISC[:, (h * QT + i) * P:(h * QT + i + 1) * P],
                                               ks[:, i, h * P:(h + 1) * P], m["ident"][:])
                    ins.then_inc(s["k_turned"], 1)
                    yield
                    pe.wait_ge(s["k_cols"], 1 + 4 * b + 4)
                    pe.wait_ge(s["q_cols"], 1 + 4 * b + 4)
                    for f in range(ROW_FILLS):
                        hj, u = f // 3, f % 3
                        if f >= 4:
                            pe.wait_ge(s["row_max"], 1 + ROW_FILLS * b + f - 3)
                        o = RING[f % 4]
                        if u == 0:
                            pe.matmul(o[:], qT[:, hj, 0:P], kT[:, hj // 4, :, 0:P], start=True, stop=False)
                            ins = pe.matmul(o[:], m["ident_bf"][:], m["row_mask"][:].unsqueeze(1).broadcast_to([P, 4, P]),
                                            start=False, stop=True)
                        else:
                            pe.matmul(o[:], qT[:, hj, P:T], kT[:, hj // 4, 2 * u - 2:2 * u, :], start=True, stop=False)
                            ins = pe.matmul(o[:].rearrange("p (g t) -> p g t", g=2)[:, :, P:T], m["ident_bf"][:],
                                            m["row_mask"][:].unsqueeze(1).broadcast_to([P, 2, P]), start=False, stop=True)
                        ins.then_inc(s["row_scores"], 1)
                        yield
                    pe.wait_ge(s["row_max"], 1 + ROW_FILLS * b + ROW_FILLS)
                    for i in range(QT):
                        ins = pe.transpose(MISC[0:H0, i * P:(i + 1) * P], nmax[:, i, :], m["ident"][:])
                    ins.then_inc(s["max_turned"], 1)
                    yield

                    def context(g):
                        h, o = g // 4, 32 * (g % 4)
                        pe.wait_ge(s["probs"], 1 + KEY_FILLS * b + 3 * g + 3)
                        if g == 4:
                            pe.wait_ge(s["ctx_out"], 1 + 4 * b + 2)
                        pe.matmul(C[0][o:o + 32, :], v[:, 0, g, :], p0[:, g % 2, :, 0:P], start=True, stop=True)
                        pe.matmul(C[1][o:o + 32, :], v[:, 0, g, :], p0[:, g % 2, :, P:T], start=True, stop=False)
                        pe.matmul(C[1][o:o + 32, :], v[:, 1, g, :], p1[:, g % 2, :, :],
                                  start=False, stop=True).then_inc(s["ctx_psum"], 1)

                    def turn_context(n):
                        pe.wait_ge(s["ctx_out"], 1 + 4 * b + 2 * (n // 2) + 2)
                        if n == 0:
                            pe.wait_ge(s["max_rows"], 1 + 2 * b + 2)
                        else:
                            pe.wait_ge(s["ctx_norm"], 1 + 4 * b + n)
                        for j in range(4):
                            ins = pe.transpose(MISC[:, j * P:(j + 1) * P], ctx_sb[:, n % 2, j * P:(j + 1) * P], m["ident"][:])
                        ins.then_inc(s["ctx_turned"], 1)

                    for g in range(G0):
                        pe.wait_ge(shift_in[g % 2], 1 + 16 * (G0 // 2 * b + g // 2 + 1))
                        for u in range(3):
                            f = 3 * g + u
                            if f >= 2:
                                pe.wait_ge(s["probs"], 1 + KEY_FILLS * b + f - 1)
                            o = S[f % 2]
                            h = g // 4
                            if u < 2:
                                pe.matmul(o[:], kT[:, h, g % 4, 0:P], qT[:, 4 * h + 2 * u:4 * h + 2 * u + 2, :],
                                          start=True, stop=False)
                                ins = pe.matmul(o[:], m["step"][:], m["shift"][:, g % 2, 2 * u:2 * u + 2, 0:T],
                                                start=False, stop=True)
                            else:
                                pe.matmul(o[:], kT[:, h, g % 4, P:T], qT[:, 4 * h:4 * h + 4, P:T],
                                          start=True, stop=False)
                                ins = pe.matmul(o[:], m["step"][:], m["shift"][:, g % 2, :, T:3 * P],
                                                start=False, stop=True)
                            ins.then_inc(s["key_scores"], 1)
                            yield
                        if g >= 1:
                            context(g - 1)
                        if g == 5:
                            turn_context(0)
                        if g == 6:
                            turn_context(1)
                        yield
                    context(G0 - 1)
                    yield
                    turn_context(2)
                    yield
                    turn_context(3)
                    yield
                    pe.wait_ge(s["ctx_norm"], 1 + 4 * b + 4)
                    for r in range(QT):
                        for i in range(QT):
                            ins = pe.matmul(MISC[:, r * D:(r + 1) * D], cx[:, i, r * P:(r + 1) * P], w_o[:, i, :],
                                            start=(i == 0), stop=(i == QT - 1))
                    ins.then_inc(s["s_psum"], 1)
                    if blocks == 0:
                        pe.wait_ge(s["tokens_f"], 1)
                        pe.transpose(TB[:, 0:BLOCKS], back_f[:], m["ident"][0:BLOCKS, 0:BLOCKS]).then_inc(s["tokens_turned"], 1)
                    yield

                def experts():
                    def turn_rows(k):
                        n = first + k
                        pe.wait_ge(gathered[k % 2], 16 * (pairs + k // 2 + 1))
                        pe.wait_ge(s["rows_cols"], 1 + n)
                        for c in range(KC):
                            ins = pe.transpose(TB[:, c * P:(c + 1) * P], rows_in[:, k % 2, c * P:(c + 1) * P], m["ident"][:])
                        ins.then_inc(s["rows_turned"], 1)

                    if blocks:
                        turn_rows(0)
                    yield
                    for k in range(blocks + 1 if blocks else 0):
                        n = first + k
                        if k < blocks:
                            if k == 0:
                                pe.wait_ge(s["experts_in"], 64)
                            e = pe.value_load(m["block_expert"][0:1, bass.ds(n, 1)], min_val=0, max_val=E - 1)
                            expert[k % 2] = e
                            pe.wait_ge(s["rows_cols"], 1 + n + 1)
                            pe.wait_ge(s["lin_in"], 1 + n)
                            pe.matmul(HB[:], pick[:, bass.ds(e * P, P)], bias[:, 0:2 * I], start=True, stop=False)
                            for c in range(KC):
                                ins = pe.matmul(HB[:], rowsT[:, c * P:(c + 1) * P], w1[:, c, bass.ds(e * 2 * I, 2 * I)],
                                                start=False, stop=(c == KC - 1))
                            ins.then_inc(s["hidden"], 1)
                            yield
                        if k >= 1:
                            pe.wait_ge(s["acted"], 1 + n)
                            pe.wait_ge(s["y_made"], 1 + n - 1)
                            for c in range(KC):
                                ins = pe.transpose(YB[:, D + c * P:D + (c + 1) * P], actd[:, c * P:(c + 1) * P], m["ident"][:])
                            ins.then_inc(s["act_turned"], 1)
                            yield
                        if k < blocks:
                            if k + 1 < blocks:
                                turn_rows(k + 1)
                            yield
                        if k >= 1:
                            e = expert[(k - 1) % 2]
                            pe.wait_ge(s["act_cols"], 1 + n)
                            pe.matmul(YB[:, 0:D], pick[:, bass.ds(e * P, P)], bias[:, 2 * I:], start=True, stop=False)
                            for c in range(KC):
                                ins = pe.matmul(YB[:, 0:D], actT[:, c * P:(c + 1) * P], w2[:, c, bass.ds(e * D, D)],
                                                start=False, stop=(c == KC - 1))
                            ins.then_inc(s["y_psum"], 1)
                            yield

                expert = [None, None]
                weave(attention(), experts(), EXPERTS_AT)

            batches(pe, batch)

        @block.scalar
        def _(act):
            def batch(b, first, pairs, blocks):
                def attention():
                    yield
                    act.wait_ge(s["xn_turned"], 1 + b + 1)
                    act.activation(xnT[:].rearrange("p k t -> p (k t)"), MISC[:], ACT.Copy).then_inc(s["xn_cols"], 1)
                    yield
                    yield
                    yield
                    for f in range(4):
                        act.wait_ge(s["q_turned"], 1 + 4 * b + f + 1)
                        act.activation(qT[:, 2 * f:2 * f + 2, :].rearrange("p c t -> p (c t)"), RING[f][:],
                                       ACT.Copy).then_inc(s["q_cols"], 1)
                        yield
                    for _ in range(1 + ROW_FILLS + 1):
                        yield
                    for g in range(G0):
                        for u in range(3):
                            f = 3 * g + u
                            act.wait_ge(s["key_scores"], 1 + KEY_FILLS * b + f + 1)
                            if u == 0 and g >= 2:
                                act.wait_ge(s["ctx_psum"], 1 + G0 * b + g - 1)
                            if u < 2:
                                dst = p0[:, g % 2, 2 * u:2 * u + 2, :].rearrange("p j q -> p (j q)")
                            else:
                                dst = p1[:, g % 2, :, :].rearrange("p j q -> p (j q)")
                            act.activation(dst, S[f % 2][:], ACT.Exp, scale=float(HD0) ** -0.5).then_inc(s["probs"], 1)
                            yield
                        if g == 4:
                            evacuate(0)
                        yield
                    evacuate(1)
                    yield
                    yield
                    yield
                    act.wait_ge(s["s_psum"], 1 + b + 1)
                    act.wait_ge(s["s_stored"], 1 + 16 * b)
                    act.activation(s_sb[:].rearrange("p i d -> p (i d)"), MISC[:], ACT.Copy).then_inc(s["s_made"], 1)
                    yield

                def evacuate(h):
                    act.wait_ge(s["ctx_psum"], 1 + G0 * b + 4 * h + 4)
                    act.wait_ge(s["ctx_turned"], 1 + 4 * b + 2 * h)
                    for i in range(QT):
                        act.activation(ctx_sb[:, i, :], C[i][:], ACT.Copy).then_inc(s["ctx_out"], 1)

                def experts():
                    def copy_rows(k):
                        n = first + k
                        act.wait_ge(s["rows_turned"], 1 + n + 1)
                        act.wait_ge(s["hidden"], 1 + n)
                        act.activation(rowsT[:], TB[:, 0:KC * P], ACT.Copy).then_inc(s["rows_cols"], 1)

                    if blocks:
                        copy_rows(0)
                    yield
                    for k in range(blocks + 1 if blocks else 0):
                        n = first + k
                        if k < blocks:
                            act.wait_ge(s["gate_in"], 1 + n + 1)
                            act.wait_ge(s["mid"], 1 + n)
                            act.activation(tanh[:], gate[:], ACT.Tanh, scale=ALPHA / 2).then_inc(s["tanh_done"], 1)
                            yield
                        if k >= 1:
                            act.wait_ge(s["act_turned"], 1 + n)
                            act.wait_ge(s["y_psum"], 1 + n - 1)
                            act.activation(actT[:], YB[:, D:D + KC * P], ACT.Copy).then_inc(s["act_cols"], 1)
                            yield
                        if k < blocks:
                            if k + 1 < blocks:
                                copy_rows(k + 1)
                            yield
                        if k >= 1:
                            act.wait_ge(s["y_psum"], 1 + n)
                            act.wait_ge(s["y_stored"], 1 + 16 * (n - 1))
                            act.activation(y[:], YB[:, 0:D], ACT.Copy).then_inc(s["y_made"], 1)
                            yield

                weave(attention(), experts(), EXPERTS_AT)

            batches(act, batch)

        @block.vector
        def _(dve):
            V = nc.vector
            V.memset(w2[:, 0, 0:768], 0.0).then_inc(s["set"], 1)
            V.memset(kT[:].rearrange("p h g t -> p (h g t)").bitcast(F32), 0.0).then_inc(s["parts"], 1)
            V.memset(v[:], 0.0).then_inc(s["parts"], 1)
            dve.wait_ge(s["parts"], 2)
            V.memset(v[:, :, :, HD0:HD0 + 1], 1.0).then_inc(s["parts"], 1)
            def split_bias():
                dve.wait_ge(s["weights_in"], 16 * 4)
                b12, left, half = w2[:, 0, 0:768], w2[:, 0, 768:1536], w2[:, 0, 1536:1920].bitcast(BF16)
                V.tensor_copy(bias[:], b12).then_inc(s["parts"], 1)
                dve.wait_ge(s["parts"], 4)
                V.tensor_tensor(left, b12, bias[:], ALU.subtract).then_inc(s["bias_steps"], 1)
                dve.wait_ge(s["bias_steps"], 1)
                V.tensor_copy(half, left).then_inc(s["bias_steps"], 1)
                dve.wait_ge(s["bias_steps"], 2)
                V.tensor_copy(bias[32:64, :], half[32:64, :]).then_inc(s["parts"], 1)
                V.tensor_tensor(bias[64:96, :], left[64:96, :], half[64:96, :], ALU.subtract).then_inc(s["parts"], 1)

            STEPS = 5 * QT + 4
            def batch(b, first, pairs, blocks):
                c = Chain(dve, s["norm_steps"], 1 + b * STEPS)

                def rotate(i):
                    dve.wait_ge(s["qkv_psum"], 1 + QT * b + i + 1)
                    if i == 0:
                        dve.wait_ge(s["ctx_psum"], 1 + G0 * b)
                    V.tensor_copy(v[:, i, :, 0:HD0],
                                  C[i][:, ROT:QKV].rearrange("p (g d) -> p g d", d=HD0)).then_inc(s["v_made"], 1)
                    qk = C[i][:, 0:ROT].rearrange("p (h d) -> p h d", d=HD0)
                    t1v = t1[:].rearrange("p (h d) -> p h d", d=HD0)
                    t2v = t2[:].rearrange("p (h d) -> p h d", d=HD0)
                    n, hd = ROT // HD0, HD0 // 2
                    c.then(V.tensor_tensor(t1v, qk, cos[:, i:i + 1, :].broadcast_to([P, n, HD0]), ALU.mult))
                    c.then(V.tensor_tensor(t2v[:, :, 0:hd], qk[:, :, hd:], sin[:, i:i + 1, 0:hd].broadcast_to([P, n, hd]), ALU.mult))
                    c.link(V.tensor_tensor(t2v[:, :, hd:], qk[:, :, 0:hd], sin[:, i:i + 1, hd:].broadcast_to([P, n, hd]), ALU.mult))
                    c.link(V.tensor_tensor(t1[:], t1[:], t2[:], ALU.add))
                    q = t1[:, 0:D].rearrange("p (n o d) -> p n o d", o=1, d=HD0).broadcast_to([P, 32, 2, HD0])
                    k = t1[:, D:ROT].rearrange("p (n o d) -> p n o d", o=1, d=HD0).broadcast_to([P, 8, 2, HD0])
                    q4 = qs[:, i, :].rearrange("p (n r c d) -> p n r c d", r=2, c=2, d=HD0)
                    k4 = ks[:, i, :].rearrange("p (n r c d) -> p n r c d", r=2, c=2, d=HD0)
                    V.tensor_copy(q4[:, :, 0, :, :].bitcast(F32R), q).then_inc(s["v_made"], 1)
                    c.link(V.tensor_copy(k4[:, :, :, 0, :].bitcast(F32R), k))
                    dve.wait_ge(s["v_made"], 1 + 4 * b + 2 * i + 2)
                    V.tensor_tensor(k4[:, :, :, 1, :].bitcast(F32R), k, k4[:, :, :, 0, :], ALU.subtract).then_inc(s["rot"], 1)
                    V.tensor_tensor(q4[:, :, 1, :, :].bitcast(F32R), q, q4[:, :, 0, :, :],
                                    ALU.subtract).then_inc(s["stacked"], 1)
                    dve.wait_ge(s["stacked"], 1 + 2 * b + i + 1)
                    dve.wait_ge(s["rot"], 1 + 2 * b + i + 1)

                def normalise(n):
                    h, i = n // 2, n % 2
                    dve.wait_ge(s["ctx_turned"], 1 + 4 * b + n + 1)
                    o = MISC[:].rearrange("p (j g r) -> p j g r", j=4, g=4)
                    c.link(V.reciprocal(rec[:], o[:, :, :, HD0]))
                    dst = cx[:, i, h * P:(h + 1) * P].rearrange("p (g j d) -> p j g d", g=4, j=4)
                    V.tensor_tensor(dst, o[:, :, :, 0:HD0], rec[:].unsqueeze(3).broadcast_to([P, 4, 4, HD0]),
                                    ALU.mult).then_inc(s["ctx_norm"], 1)

                first_batch = blocks == 0

                def attention():
                    dve.wait_ge(s["xn_turned"], 1 + b)
                    for i in range(QT):
                        n = b * QT + i
                        V.tensor_scalar(xn[:, i, :], x[:, bass.ds(n, 1), :].rearrange("p o d -> p (o d)"),
                                        mr[:, 0, bass.ds(n, 1)], mr[:, 1, bass.ds(n, 1)],
                                        ALU.subtract, ALU.mult).then_inc(s["xn_made"], 1)
                    yield
                    yield
                    rotate(0)
                    yield
                    rotate(1)
                    if first_batch:
                        split_bias()
                    yield
                    for _ in range(4):
                        yield
                    dve.wait_ge(s["k_turned"], 1 + b + 1)
                    for g in range(4):
                        r = slice(32 * g, 32 * g + 32)
                        V.tensor_copy(kT[r, :, g, :], MISC[r, :].rearrange("p (h t) -> p h t", h=2)).then_inc(s["k_cols"], 1)
                    yield
                    for f in range(ROW_FILLS):
                        hj, u = f // 3, f % 3
                        h, j = hj // 4, hj % 4
                        o = RING[f % 4]
                        dve.wait_ge(s["row_scores"], 1 + ROW_FILLS * b + f + 1)
                        heads = nmax[:].rearrange("p i (h g j) -> p i h g j", h=2, g=4)
                        if u == 0:
                            dst, src = heads[:, 0, h, :, j], o[:].rearrange("p (g t) -> p g t", g=4)
                        else:
                            dst, src = heads[:, 1, h, 2 * u - 2:2 * u, j], o[:].rearrange("p (g t) -> p g t", g=2)
                        V.tensor_reduce(dst, src, AX.X, ALU.max, negate=True).then_inc(s["row_max"], 1)
                        yield
                    dve.wait_ge(s["max_turned"], 1 + b + 1)
                    for u in range(2):
                        dve.wait_ge(shift_in[u], 1 + 16 * (G0 // 2) * b)
                    V.tensor_copy(nmaxT[:, 0:T], MISC[0:H0, 0:T]).then_inc(s["max_rows"], 1)
                    V.tensor_copy(nmaxT[:, T:], MISC[0:H0, P:T]).then_inc(s["max_rows"], 1)
                    yield
                    for g in range(G0):
                        for _ in range(3):
                            yield
                        if g == 5:
                            normalise(0)
                        if g == 6:
                            normalise(1)
                        yield
                    yield
                    normalise(2)
                    yield
                    normalise(3)
                    yield
                    if first_batch:
                        dve.wait_ge(s["tokens_back"], 16)
                        V.tensor_copy(back_f[:], back[:]).then_inc(s["tokens_f"], 1)
                        dve.wait_ge(s["tokens_turned"], 1)
                        V.tensor_copy(m["block_tokens"][:], TB[:, 0:BLOCKS]).then_inc(s["blocks_known"], 1)
                    yield

                def experts():
                    yield
                    for k in range(blocks + 1 if blocks else 0):
                        n = first + k
                        if k < blocks:
                            dve.wait_ge(s["hidden"], 1 + n + 1)
                            dve.wait_ge(s["acted"], 1 + n)
                            V.tensor_scalar(gate[:], HB[:, 0:I], LIMIT, None, ALU.min).then_inc(s["gate_in"], 1)
                            V.tensor_scalar(lin[:], HB[:, I:2 * I], LIMIT, -LIMIT, ALU.min, ALU.max).then_inc(s["lin_in"], 1)
                            dve.wait_ge(s["lin_in"], 1 + n + 1)
                            V.tensor_scalar(lin[:], lin[:], 1.0, 0.5, ALU.add, ALU.mult).then_inc(s["lin_scaled"], 1)
                            yield
                        if k >= 1:
                            yield
                        if k < blocks:
                            dve.wait_ge(s["tanh_done"], 1 + n + 1)
                            dve.wait_ge(s["act_turned"], 1 + n)
                            V.scalar_tensor_tensor(out=actd[:], in0=tanh[:], scalar=1.0, in1=gate[:],
                                                   op0=ALU.add, op1=ALU.mult).then_inc(s["mid"], 1)
                            dve.wait_ge(s["mid"], 1 + n + 1)
                            dve.wait_ge(s["lin_scaled"], 1 + n + 1)
                            V.tensor_tensor(actd[:], actd[:], lin[:], ALU.mult).then_inc(s["acted"], 1)
                            yield
                        if k >= 1:
                            yield

                weave(attention(), experts(), EXPERTS_AT)
                assert c.n == STEPS, c.n

            batches(dve, batch)


def beside(attention, head, at):
    for tick, _ in enumerate(attention):
        if tick in at:
            next(head, None)
        yield
    assert next(head, None) is None


def layer1(nc, a, m, y_rows, s_rows, out):
    x, mr, bank = m["x"], m["mean_rstd"], m["bank"]
    S, C, MISC, HIDDEN, DOWN = bank[0:2], bank[2:4], bank[4], bank[5:7], bank[7]
    RING = bank[0:4]
    PAIRS, GROUPS = H1 // 2, H1 // 4
    HEAD_AT = {28: 0, 32: 1, 35: 2, 38: 3}
    FFN_AT = {3: 1, 4: 1, 9: 1, 20: 1, 26: 2, 43: 1, 44: 1}
    ROW_FILLS, KEY_FILLS = GROUPS + PAIRS, 3 * GROUPS
    CHOICES = QT * TOPK
    with ExitStack() as ctx:
        def sb(name, shape, dt=F32):
            return ctx.enter_context(nc.sbuf_tensor(name, shape, dt))

        counts = ("s_in picked1 head_steps steps1 f_made f_tanh x_made xn_made1 xn_turned1 xn_cols1 qk_psum v_psum "
                          "v_cols stacked1 q_turned1 q_cols1 k_turned1 k_low k_high row_scores1 row_max1 max_turned1 "
                          "max_rows1 shift_even1 shift_odd1 key_scores1 probs1 ctx_psum1 ctx_out1 ctx_turned1 ctx_norm1 "
                          "cx_turned cx_cols s_psum1 s_made1 "
                          "hid_psum hid_tanh hid_mid hid_made down_psum down_made out_tanh out_mid out_made stored").split()
        s = sems(nc, ctx, ["attn_in", "ffn_in", "cleared", "cast", "scales", "scales_in", "rows_in1"] + counts)
        shift_in = [s["shift_even1"], s["shift_odd1"]]
        w_qkv = sb("w_qkv1", [P, KC, 3 * D])
        w_o = sb("w_o1", [P, KC, D])
        raw = sb("raw", [P, KC, HID], I32)
        w_gate = sb("w_gate1", [P, KC, HID])
        w_up = sb("w_up1", [P, KC, HID])
        w_down = sb("w_down1", [P, HC, D])
        s_gate = sb("s_gate", [P, HC])
        s_up = sb("s_up", [P, HC])
        s_both = sb("s_both", [P, HC])
        s_down = sb("s_down", [P, D])
        s0 = sb("s0", [P, QT, D])
        rows_no = sb("rows_no1", [P, CHOICES], U32)
        rows = sb("rows1", [P, CHOICES, D])
        f = sb("f", [P, QT, D])
        ft = sb("ft", [P, QT, D])
        stats = sb("stats1", [P, QT, 6])
        mv = sb("mv", [P, 2, QT])
        ve = sb("ve1", [P, QT])
        carrier = sb("carrier", [P, 2])
        ready = sb("ready", [P, 2])
        w2 = sb("w_2", [P, QT])
        xn = sb("xn1", [P, QT, D])
        xnT = sb("xnT1", [P, KC, T])
        qs = sb("qs1", [P, QT, 4 * D])
        ks = sb("ks1", [P, QT, 4 * D])
        qT = sb("qT1", [P, PAIRS, T], F32R)
        kT = sb("kT1", [P, PAIRS, 2, T], F32R)
        v = sb("v1", [P, QT, H1, 32])
        nmax = sb("nmax1", [P, QT, H1])
        nmaxT = sb("nmaxT1", [H1, 3 * P], F32R)
        p0 = sb("p0_1", [P, 2, 4, T])
        p1 = sb("p1_1", [P, 2, 4, P])
        ctx_sb = sb("ctx_sb1", [P, 2, T])
        rec = sb("rec1", [P, QT, 4])
        cx = sb("cx1", [P, QT, D])
        cxT = sb("cxT1", [P, KC, T])
        s1 = sb("s1", [P, QT, D])
        htanh = sb("htanh", [P, 2, T])
        hmid = sb("hmid", [P, T])
        hid = sb("hid", [P, 2, T])
        down = sb("down", [P, QT, D])
        dtanh = sb("dtanh", [P, QT, D])
        dout = sb("dout", [P, QT, D])
        block = ctx.enter_context(nc.Block())


        @block.sync
        def _(sp):
            for name in counts:
                sp.sem_inc(s[name], 1)
            sv = s_rows.rearrange("(n p) d -> p n d", p=P)
            ov = out.rearrange("b (i p) d -> p (b i) d", p=P)
            sp.dma_start(s0[:], sv[:, 0:QT, :]).then_inc(s["s_in"], 16)
            sp.dma_start(w_qkv[:], a["wqkv1"].rearrange("(c p) n -> p c n", p=P)).then_inc(s["attn_in"], 16)
            sp.dma_start(w_o[:], a["wo1"].rearrange("(c p) n -> p c n", p=P)).then_inc(s["attn_in"], 16)
            full = HID // P
            for name, dst in (("s_gate", s_gate), ("s_up", s_up)):
                sp.dma_start(dst[:, 0:full], a[name]).then_inc(s["scales_in"], 16)
                sp.dma_start(dst[0:ROWS[-1], full:], a[name + "_rest"]).then_inc(s["scales_in"], 16)
            sp.dma_start(s_down[:], a["s_down"].partition_broadcast(P)).then_inc(s["scales_in"], 16)
            sp.dma_start(raw[:], a["w_gate"].rearrange("(c p) n -> p c n", p=P)).then_inc(s["ffn_in"], 16)
            sp.wait_ge(s["cast"], 1)
            sp.dma_start(raw[:], a["w_up"].rearrange("(c p) n -> p c n", p=P)).then_inc(s["ffn_in"], 16)
            sp.wait_ge(s["cast"], 2)
            rd = raw[:].rearrange("p c n -> p (c n)")
            for c in range(HC - 1):
                sp.dma_start(rd[:, c * D:(c + 1) * D], a["w_down"][c * P:(c + 1) * P, :]).then_inc(s["ffn_in"], 16)
            sp.wait_ge(s["cast"], 3)
            sp.dma_start(rd[0:ROWS[-1], 0:D], a["w_down"][(HC - 1) * P:, :]).then_inc(s["ffn_in"], 16)

            def next_rows(b):
                sp.wait_ge(s["x_made"], 1 + QT * b + QT)
                sp.dma_start(s0[:], sv[:, bass.ds(b * QT + QT, QT), :]).then_inc(s["s_in"], 16)

            def batch(b, last):
                def attention():
                    def send_shift(g):
                        sp.wait_ge(s["key_scores1"], 1 + KEY_FILLS * b + 3 * max(g - 1, 0))
                        if g == 0:
                            sp.wait_ge(s["max_rows1"], 1 + 2 * b + 2)
                        sp.dma_start(m["shift"][0:1, g % 2, :, :].bitcast(F32),
                                     nmaxT[4 * g:4 * g + 4, :].bitcast(F32)).then_inc(shift_in[g % 2], 16)

                    for _ in range(26):
                        yield
                    send_shift(0)
                    send_shift(1)
                    yield
                    for g in range(GROUPS):
                        if 1 <= g < GROUPS - 1:
                            send_shift(g + 1)
                        for _ in range(4):
                            yield
                    for _ in range(4):
                        yield
                    if not last:
                        next_rows(b + 1)
                    yield
                    sp.wait_ge(s["out_made"], 1 + QT * b + QT)
                    sp.dma_start(ov[:, bass.ds(b * QT, QT), :], dout[:]).then_inc(s["stored"], 16)
                    yield

                for _ in attention():
                    pass

            next_rows(0)
            with sp.Fori(0, B - 1) as b:
                batch(b, False)
            batch(B - 1, True)
            sp.wait_ge(s["stored"], 1 + 16 * B)
            sp.wait_ge(s["s_in"], 1 + 16 * (B + 1))

        @block.gpsimd
        def _(pool):
            pool.memset(ready[:], 0.0).then_inc(s["picked1"], 1)
            pool.wait_ge(s["picked1"], 1 + 1)

            def gather_rows(b):
                nc.gpsimd.tensor_copy(rows_no[:], m["slots"][:, bass.ds(b * QT, QT), :].rearrange("p i k -> p (i k)")
                                      ).then_inc(s["picked1"], 1)
                pool.wait_ge(s["picked1"], 1 + 2 * b + 2)
                nc.gpsimd.tensor_tensor(ready[:, 1:2], ready[:, 0:1], ready[:, 0:1], ALU.add).then_inc(s["picked1"], 1)
                for c in range(CHOICES):
                    nc.gpsimd.indirect_dma_start(rows[:, c, :], None, y_rows,
                                                 bass.IndirectOffsetOnAxis(rows_no[:, c:c + 1], 0)).then_inc(s["rows_in1"], 16)
                pool.wait_ge(s["rows_in1"], 16 * CHOICES * (b + 1))

            gather_rows(0)
            full = HID // P
            pool.wait_ge(s["ffn_in"], 16)
            nc.gpsimd.tensor_scalar(w_gate[:], raw[:], -128.0, None, ALU.add).then_inc(s["cast"], 1)
            pool.wait_ge(s["ffn_in"], 16 * 2)
            nc.gpsimd.tensor_scalar(w_up[:], raw[:], -128.0, None, ALU.add).then_inc(s["cast"], 1)
            rd = raw[:].rearrange("p c n -> p (c n)")
            pool.wait_ge(s["ffn_in"], 16 * (2 + full))
            nc.gpsimd.tensor_scalar(w_down[:, 0:full, :].rearrange("p c n -> p (c n)"), rd[:, 0:full * D], -128.0, None,
                                    ALU.add).then_inc(s["cast"], 1)
            pool.wait_ge(s["ffn_in"], 16 * (3 + full))
            nc.gpsimd.tensor_scalar(w_down[0:ROWS[-1], full, :], rd[0:ROWS[-1], 0:D], -128.0, None,
                                    ALU.add).then_inc(s["cast"], 1)
            with pool.Fori(1, B) as b:
                pool.wait_ge(s["f_made"], 1 + QT * b)
                gather_rows(b)

        @block.tensor
        def _(pe):
            pe.wait_ge(s["attn_in"], 32)
            pe.wait_ge(s["cleared"], 3)
            def batch(b, last):
                def attention():
                    yield
                    yield
                    pe.wait_ge(s["xn_made1"], 1 + QT * b + QT)
                    pe.wait_ge(s["s_made1"], 1 + b)
                    for k in range(KC):
                        for i in range(QT):
                            ins = pe.transpose(MISC[:, (k * QT + i) * P:(k * QT + i + 1) * P],
                                               xn[:, i, k * P:(k + 1) * P], m["ident"][:])
                    ins.then_inc(s["xn_turned1"], 1)
                    yield
                    pe.wait_ge(s["xn_cols1"], 1 + b + 1)
                    pe.wait_ge(s["ctx_out1"], 1 + GROUPS * b)
                    for i in range(QT):
                        for k in range(KC):
                            ins = pe.matmul(C[i][:], xnT[:, k, i * P:(i + 1) * P], w_qkv[:, k, 0:2 * D],
                                            start=(k == 0), stop=(k == KC - 1))
                        ins.then_inc(s["qk_psum"], 1)
                    for i in range(QT):
                        for k in range(KC):
                            ins = pe.matmul(MISC[:, i * D:(i + 1) * D], xnT[:, k, i * P:(i + 1) * P], w_qkv[:, k, 2 * D:],
                                            start=(k == 0), stop=(k == KC - 1))
                    ins.then_inc(s["v_psum"], 1)
                    yield
                    yield
                    yield
                    pe.wait_ge(s["probs1"], 1 + KEY_FILLS * b)
                    for f_ in range(8):
                        src = qs if f_ < 4 else ks
                        if f_ == 0:
                            pe.wait_ge(s["stacked1"], 1 + 2 * QT * b + 2 * QT)
                        if f_ >= 4:
                            pe.wait_ge(s["q_cols1"], 1 + 4 * b + f_ - 3)
                        for c in range(2):
                            for i in range(QT):
                                j = 2 * (f_ % 4) + c
                                ins = pe.transpose(RING[f_ % 4][:, (c * QT + i) * P:(c * QT + i + 1) * P],
                                                   src[:, i, j * P:(j + 1) * P], m["ident"][:])
                        ins.then_inc(s["q_turned1" if f_ < 4 else "k_turned1"], 1)
                        yield
                    pe.wait_ge(s["k_low"], 1 + 4 * b + 4)
                    pe.wait_ge(s["k_high"], 1 + 4 * b + 4)
                    for f_ in range(ROW_FILLS):
                        if f_ >= 4:
                            pe.wait_ge(s["row_max1"], 1 + ROW_FILLS * b + f_ - 3)
                        o = RING[f_ % 4]
                        if f_ < GROUPS:
                            for c in range(2):
                                j = 2 * f_ + c
                                pe.matmul(o[:, c * T:(c + 1) * T], qT[:, j, 0:P], kT[:, j, :, 0:P], start=True, stop=False)
                                ins = pe.matmul(o[:, c * T:(c + 1) * T], m["ident_bf"][:],
                                                m["row_mask"][:].unsqueeze(1).broadcast_to([P, 2, P]), start=False, stop=True)
                        else:
                            j = f_ - GROUPS
                            pe.matmul(o[:], qT[:, j, P:T], kT[:, j, :, :], start=True, stop=False)
                            ins = pe.matmul(o[:].rearrange("p (g t) -> p g t", g=2)[:, :, P:T], m["ident_bf"][:],
                                            m["row_mask"][:].unsqueeze(1).broadcast_to([P, 2, P]), start=False, stop=True)
                        ins.then_inc(s["row_scores1"], 1)
                        yield
                    pe.wait_ge(s["row_max1"], 1 + ROW_FILLS * b + ROW_FILLS)
                    pe.wait_ge(s["v_cols"], 1 + b + 1)
                    for i in range(QT):
                        ins = pe.transpose(MISC[0:H1, i * P:(i + 1) * P], nmax[:, i, :], m["ident"][:])
                    ins.then_inc(s["max_turned1"], 1)
                    yield

                    def context(g):
                        pe.wait_ge(s["probs1"], 1 + KEY_FILLS * b + 3 * g + 3)
                        if g >= 2:
                            pe.wait_ge(s["ctx_out1"], 1 + GROUPS * b + g - 1)
                        for j in range(4):
                            o, h = C[g % 2][32 * j:32 * j + 32, :], 4 * g + j
                            pe.matmul(o[:, 0:T], v[:, 0, h, :], p0[:, g % 2, j, :], start=True, stop=False)
                            ins = pe.matmul(o[:, P:T], v[:, 1, h, :], p1[:, g % 2, j, :], start=False, stop=True)
                        ins.then_inc(s["ctx_psum1"], 1)

                    def turn_context(g):
                        pe.wait_ge(s["ctx_out1"], 1 + GROUPS * b + g + 1)
                        if g == 0:
                            pe.wait_ge(s["max_rows1"], 1 + 2 * b + 2)
                        else:
                            pe.wait_ge(s["ctx_norm1"], 1 + GROUPS * b + g)
                        for i in range(QT):
                            ins = pe.transpose(MISC[:, i * P:(i + 1) * P], ctx_sb[:, g % 2, i * P:(i + 1) * P], m["ident"][:])
                        ins.then_inc(s["ctx_turned1"], 1)

                    for g in range(GROUPS):
                        pe.wait_ge(shift_in[g % 2], 1 + 16 * (GROUPS // 2 * b + g // 2 + 1))
                        for u in range(3):
                            f_ = 3 * g + u
                            if f_ >= 2:
                                pe.wait_ge(s["probs1"], 1 + KEY_FILLS * b + f_ - 1)
                            o = S[f_ % 2]
                            if u < 2:
                                j = 2 * g + u
                                for c in range(2):
                                    pe.matmul(o[:, c * T:(c + 1) * T], kT[:, j, c, 0:P], qT[:, j, :],
                                              start=(c == 0), stop=False, skip_group_check=True)
                                ins = pe.matmul(o[:], m["step"][:], m["shift"][:, g % 2, 2 * u:2 * u + 2, 0:T],
                                                start=False, stop=True, skip_group_check=True)
                            else:
                                for c in range(4):
                                    j = 2 * g + c // 2
                                    pe.matmul(o[:, c * P:(c + 1) * P], kT[:, j, c % 2, P:T], qT[:, j, P:T],
                                              start=(c == 0), stop=False, skip_group_check=True)
                                ins = pe.matmul(o[:], m["step"][:], m["shift"][:, g % 2, :, T:3 * P],
                                                start=False, stop=True, skip_group_check=True)
                            ins.then_inc(s["key_scores1"], 1)
                            yield
                        if g >= 1:
                            context(g - 1)
                        if g >= 2:
                            turn_context(g - 2)
                        yield
                    context(GROUPS - 1)
                    turn_context(GROUPS - 2)
                    yield
                    turn_context(GROUPS - 1)
                    yield
                    pe.wait_ge(s["ctx_norm1"], 1 + GROUPS * b + GROUPS)
                    for k in range(KC):
                        for i in range(QT):
                            ins = pe.transpose(MISC[:, (k * QT + i) * P:(k * QT + i + 1) * P],
                                               cx[:, i, k * P:(k + 1) * P], m["ident"][:])
                    ins.then_inc(s["cx_turned"], 1)
                    yield
                    pe.wait_ge(s["cx_cols"], 1 + b + 1)
                    for i in range(QT):
                        for k in range(KC):
                            ins = pe.matmul(MISC[:, i * D:(i + 1) * D], cxT[:, k, i * P:(i + 1) * P], w_o[:, k, :],
                                            start=(k == 0), stop=(k == KC - 1))
                    ins.then_inc(s["s_psum1"], 1)
                    yield
                    yield

                def feed_forward():
                    for c in range(HC + 2):
                        if c < HC:
                            r = ROWS[c]
                            if c == 0:
                                pe.wait_ge(s["xn_cols1"], 1 + b + 1)
                                pe.wait_ge(s["cast"], 4)
                            pe.wait_ge(s["hid_made"], 1 + HC * b + max(c - 1, 0))
                            for n, w in enumerate((w_gate, w_up)):
                                for k in range(KC):
                                    ins = pe.matmul(HIDDEN[c % 2][0:r, n * T:(n + 1) * T], w[:, k, c * P:c * P + r],
                                                    xnT[:, k, :], start=(k == 0), stop=(k == KC - 1))
                            ins.then_inc(s["hid_psum"], 1)
                        if c >= 2:
                            d_ = c - 2
                            r = ROWS[d_]
                            pe.wait_ge(s["hid_made"], 1 + HC * b + d_ + 1)
                            if d_ == 0:
                                pe.wait_ge(s["down_made"], 1 + QT * b)
                            for i in range(QT):
                                ins = pe.matmul(DOWN[:, i * D:(i + 1) * D], hid[0:r, d_ % 2, i * P:(i + 1) * P],
                                                w_down[0:r, d_, :], start=(d_ == 0 and i == 0),
                                                stop=(d_ == HC - 1 and i == QT - 1), skip_group_check=True)
                            ins.then_inc(s["down_psum"], 1)
                        yield

                weave(attention(), feed_forward(), FFN_AT)

            with pe.Fori(0, B - 1) as b:
                batch(b, False)
            batch(B - 1, True)

        @block.scalar
        def _(act):
            def head(b):
                yield
                for i in range(QT):
                    act.wait_ge(s["f_made"], 1 + QT * b + i + 1)
                    act.activation(ft[:, i, :], f[:, i, :], ACT.Tanh, scale=0.5).then_inc(s["f_tanh"], 1)
                yield

            def batch(b, last):
                def attention():
                    yield
                    yield
                    act.wait_ge(s["xn_turned1"], 1 + b + 1)
                    act.activation(xnT[:].rearrange("p k t -> p (k t)"), MISC[:], ACT.Copy).then_inc(s["xn_cols1"], 1)
                    yield
                    act.wait_ge(s["v_psum"], 1 + b + 1)
                    act.activation(v[:, :, :, 0:HD1], MISC[:].rearrange("p (i h d) -> p i h d", i=QT, d=HD1),
                                   ACT.Copy).then_inc(s["v_cols"], 1)
                    yield
                    yield
                    yield
                    for f_ in range(4):
                        act.wait_ge(s["q_turned1"], 1 + 4 * b + f_ + 1)
                        act.activation(qT[:, 2 * f_:2 * f_ + 2, :].rearrange("p c t -> p (c t)"), RING[f_ % 4][:],
                                       ACT.Copy).then_inc(s["q_cols1"], 1)
                        yield
                    for f_ in range(4):
                        act.wait_ge(s["k_turned1"], 1 + 4 * b + f_ + 1)
                        act.activation(kT[0:64, 2 * f_:2 * f_ + 2, 0, :], RING[f_ % 4][0:64, :].rearrange("p (c t) -> p c t", c=2),
                                       ACT.Copy).then_inc(s["k_low"], 1)
                        yield
                    for _ in range(ROW_FILLS + 1):
                        yield

                    def evacuate(g):
                        act.wait_ge(s["ctx_psum1"], 1 + GROUPS * b + g + 1)
                        act.wait_ge(s["ctx_turned1"], 1 + GROUPS * b + max(g - 1, 0))
                        act.activation(ctx_sb[:, g % 2, :], C[g % 2][:, 0:T], ACT.Copy).then_inc(s["ctx_out1"], 1)

                    for g in range(GROUPS):
                        for u in range(3):
                            f_ = 3 * g + u
                            act.wait_ge(s["key_scores1"], 1 + KEY_FILLS * b + f_ + 1)
                            if u == 0 and g >= 2:
                                act.wait_ge(s["ctx_psum1"], 1 + GROUPS * b + g - 1)
                            dst = (p0[:, g % 2, 2 * u:2 * u + 2, :] if u < 2 else p1[:, g % 2, :, :])
                            act.activation(dst.rearrange("p j q -> p (j q)"), S[f_ % 2][:], ACT.Exp,
                                           scale=float(HD1) ** -0.5).then_inc(s["probs1"], 1)
                            yield
                        if g >= 1:
                            evacuate(g - 1)
                        yield
                    evacuate(GROUPS - 1)
                    yield
                    yield
                    act.wait_ge(s["cx_turned"], 1 + b + 1)
                    act.activation(cxT[:].rearrange("p k t -> p (k t)"), MISC[:], ACT.Copy).then_inc(s["cx_cols"], 1)
                    yield
                    act.wait_ge(s["s_psum1"], 1 + b + 1)
                    act.wait_ge(s["out_mid"], 1 + 2 * QT * b)
                    act.activation(s1[:].rearrange("p i d -> p (i d)"), MISC[:], ACT.Copy).then_inc(s["s_made1"], 1)
                    yield
                    for i in range(QT):
                        act.wait_ge(s["down_made"], 1 + QT * b + i + 1)
                        act.activation(dtanh[:, i, :], down[:, i, :], ACT.Tanh, scale=0.5).then_inc(s["out_tanh"], 1)
                    yield

                def feed_forward():
                    for c in range(HC):
                        r = ROWS[c]
                        if c == 0:
                            act.wait_ge(s["scales"], 4)
                        act.wait_ge(s["hid_psum"], 1 + HC * b + c + 1)
                        act.wait_ge(s["hid_mid"], 1 + HC * b + max(c - 1, 0))
                        act.activation(htanh[0:r, c % 2, :], HIDDEN[c % 2][0:r, 0:T], ACT.Tanh,
                                       scale=s_gate[0:r, c:c + 1]).then_inc(s["hid_tanh"], 1)
                        yield
                    yield
                    yield

                weave(attention() if last else beside(attention(), head(b + 1), HEAD_AT), feed_forward(), FFN_AT)

            for _ in head(0):
                pass
            with act.Fori(0, B - 1) as b:
                batch(b, False)
            batch(B - 1, True)

        @block.vector
        def _(dve):
            V = nc.vector
            V.memset(kT[:].rearrange("p h g t -> p (h g t)").bitcast(F32), 0.0).then_inc(s["cleared"], 1)
            V.memset(v[:], 0.0).then_inc(s["cleared"], 1)
            dve.wait_ge(s["cleared"], 2)
            V.memset(v[:, :, :, HD1:HD1 + 1], 1.0).then_inc(s["cleared"], 1)
            HEAD = QT * (TOPK + 2 + 2) + 3 + RSQRT_STEPS
            STEPS = 2 * QT + GROUPS
            def head(b):
                c = Chain(dve, s["head_steps"], 1 + b * HEAD)
                xs = [x[:, bass.ds(b * QT + i, 1), :].rearrange("p o d -> p (o d)") for i in range(QT)]
                dve.wait_ge(s["rows_in1"], 16 * CHOICES * (b + 1))
                dve.wait_ge(s["s_in"], 1 + 16 * (b + 1))
                for i in range(QT):
                    n = b * QT + i
                    c.then(V.tensor_scalar(f[:, i, :], xs[i], mr[:, 0, bass.ds(n, 1)], mr[:, 1, bass.ds(n, 1)],
                                           ALU.subtract, ALU.mult))
                for k in range(TOPK):
                    c.wait()
                    for i in range(QT):
                        ins = V.scalar_tensor_tensor(out=f[:, i, :], in0=rows[:, i * TOPK + k, :],
                                                     scalar=m["gates"][:, bass.ds(b * QT + i, 1), k], in1=f[:, i, :],
                                                     op0=ALU.mult, op1=ALU.add)
                        if k < TOPK - 1:
                            c.then(ins)
                        else:
                            ins.then_inc(s["f_made"], 1)
                yield
                for i in range(QT):
                    dve.wait_ge(s["f_tanh"], 1 + QT * b + i + 1)
                    c.then(V.scalar_tensor_tensor(out=ft[:, i, :], in0=ft[:, i, :], scalar=1.0, in1=f[:, i, :],
                                                  op0=ALU.add, op1=ALU.mult))
                c.wait()
                for i in range(QT):
                    c.then(V.scalar_tensor_tensor(out=ft[:, i, :], in0=ft[:, i, :], scalar=0.5, in1=s0[:, i, :],
                                                  op0=ALU.mult, op1=ALU.mult))
                c.wait()
                for i in range(QT):
                    V.tensor_tensor(xs[i], xs[i], ft[:, i, :], ALU.add).then_inc(s["x_made"], 1)
                yield
                dve.wait_ge(s["x_made"], 1 + QT * b + QT)
                c.then(V.memset(carrier[:, 0:1], 0.0))
                for i in range(QT):
                    c.then(V.bn_stats(stats[:, i, :], xs[i]))
                c.wait()
                c.then(V.memset(carrier[:, 1:2], 0.0))
                for i in range(QT):
                    c.then(V.bn_aggr(mv[:, :, i], stats[:, i, :]))
                c.wait()
                c.link(V.tensor_scalar(ve[:], mv[:, 1, :], EPS, None, ALU.add))
                yield
                rsqrt(nc, c, ve[:], mv[:, 1, :], w2[:])
                dve.wait_ge(s["xn_turned1"], 1 + b)
                for i in range(QT):
                    V.tensor_scalar(xn[:, i, :], xs[i], mv[:, 0, i:i + 1], mv[:, 1, i:i + 1],
                                    ALU.subtract, ALU.mult).then_inc(s["xn_made1"], 1)
                assert c.n == HEAD, c.n
            def batch(b, last):
                c = Chain(dve, s["steps1"], 1 + b * STEPS)
                xs = [x[:, bass.ds(b * QT + i, 1), :].rearrange("p o d -> p (o d)") for i in range(QT)]

                def normalise(g):
                    dve.wait_ge(s["ctx_turned1"], 1 + GROUPS * b + g + 1)
                    o = MISC[:, 0:T].rearrange("p (i j r) -> p i j r", i=QT, j=4)
                    c.link(V.reciprocal(rec[:], o[:, :, :, HD1]))
                    V.tensor_tensor(cx[:, :, 64 * g:64 * g + 64].rearrange("p i (j d) -> p i j d", j=4), o[:, :, :, 0:HD1],
                                    rec[:].unsqueeze(3).broadcast_to([P, QT, 4, HD1]), ALU.mult).then_inc(s["ctx_norm1"], 1)

                def attention():
                    for _ in range(4):
                        yield
                    for i in range(QT):
                        dve.wait_ge(s["qk_psum"], 1 + QT * b + i + 1)
                        q = C[i][:, 0:D].rearrange("p (n o d) -> p n o d", o=1, d=HD1).broadcast_to([P, H1, 2, HD1])
                        k = C[i][:, D:2 * D].rearrange("p (n o d) -> p n o d", o=1, d=HD1).broadcast_to([P, H1, 2, HD1])
                        q4 = qs[:, i, :].rearrange("p (n r c d) -> p n r c d", r=2, c=2, d=HD1)
                        k4 = ks[:, i, :].rearrange("p (n r c d) -> p n r c d", r=2, c=2, d=HD1)
                        c.then(V.tensor_copy(q4[:, :, 0, :, :].bitcast(F32R), q))
                        c.link(V.tensor_copy(k4[:, :, :, 0, :].bitcast(F32R), k))
                        V.tensor_tensor(q4[:, :, 1, :, :].bitcast(F32R), q, q4[:, :, 0, :, :],
                                        ALU.subtract).then_inc(s["stacked1"], 1)
                        V.tensor_tensor(k4[:, :, :, 1, :].bitcast(F32R), k, k4[:, :, :, 0, :],
                                        ALU.subtract).then_inc(s["stacked1"], 1)
                        yield
                    for _ in range(4):
                        yield
                    for f_ in range(4):
                        dve.wait_ge(s["k_turned1"], 1 + 4 * b + f_ + 1)
                        V.tensor_copy(kT[64:P, 2 * f_:2 * f_ + 2, 1, :],
                                      RING[f_ % 4][64:P, :].rearrange("p (c t) -> p c t", c=2)).then_inc(s["k_high"], 1)
                        yield
                    for f_ in range(ROW_FILLS):
                        dve.wait_ge(s["row_scores1"], 1 + ROW_FILLS * b + f_ + 1)
                        o = RING[f_ % 4]
                        if f_ < GROUPS:
                            dst, src = nmax[:, 0, 4 * f_:4 * f_ + 4], o[:].rearrange("p (g t) -> p g t", g=4)
                        else:
                            j = f_ - GROUPS
                            dst, src = nmax[:, 1, 2 * j:2 * j + 2], o[:].rearrange("p (g t) -> p g t", g=2)
                        V.tensor_reduce(dst, src, AX.X, ALU.max, negate=True).then_inc(s["row_max1"], 1)
                        yield
                    dve.wait_ge(s["max_turned1"], 1 + b + 1)
                    for u in range(2):
                        dve.wait_ge(shift_in[u], 1 + 16 * (GROUPS // 2) * b)
                    V.tensor_copy(nmaxT[:, 0:T], MISC[0:H1, 0:T]).then_inc(s["max_rows1"], 1)
                    V.tensor_copy(nmaxT[:, T:], MISC[0:H1, P:T]).then_inc(s["max_rows1"], 1)
                    yield
                    for g in range(GROUPS):
                        for _ in range(3):
                            yield
                        if g >= 2:
                            normalise(g - 2)
                        yield
                    normalise(GROUPS - 2)
                    yield
                    normalise(GROUPS - 1)
                    yield
                    yield
                    yield
                    for i in range(QT):
                        if i == 0:
                            dve.wait_ge(s["down_psum"], 1 + HC * b + HC)
                        V.tensor_tensor(down[:, i, :], DOWN[:, i * D:(i + 1) * D], s_down[:], ALU.mult).then_inc(s["down_made"], 1)
                    yield
                    for i in range(QT):
                        dve.wait_ge(s["out_tanh"], 1 + QT * b + i + 1)
                        V.scalar_tensor_tensor(out=dtanh[:, i, :], in0=dtanh[:, i, :], scalar=1.0, in1=down[:, i, :],
                                               op0=ALU.add, op1=ALU.mult).then_inc(s["out_mid"], 1)
                    dve.wait_ge(s["s_made1"], 1 + b + 1)
                    dve.wait_ge(s["out_mid"], 1 + 2 * QT * b + QT)
                    for i in range(QT):
                        V.scalar_tensor_tensor(out=dtanh[:, i, :], in0=dtanh[:, i, :], scalar=0.5, in1=s1[:, i, :],
                                               op0=ALU.mult, op1=ALU.mult).then_inc(s["out_mid"], 1)
                    dve.wait_ge(s["out_mid"], 1 + 2 * QT * b + 2 * QT)
                    dve.wait_ge(s["stored"], 1 + 16 * b)
                    for i in range(QT):
                        V.tensor_tensor(dout[:, i, :], xs[i], dtanh[:, i, :], ALU.add).then_inc(s["out_made"], 1)
                    yield

                def feed_forward():
                    yield
                    for c_ in range(HC):
                        r = ROWS[c_]
                        HB = HIDDEN[c_ % 2]
                        dve.wait_ge(s["hid_tanh"], 1 + HC * b + c_ + 1)
                        dve.wait_ge(s["hid_made"], 1 + HC * b + c_)
                        V.scalar_tensor_tensor(out=hmid[0:r, :], in0=htanh[0:r, c_ % 2, :], scalar=1.0, in1=HB[0:r, 0:T],
                                               op0=ALU.add, op1=ALU.mult).then_inc(s["hid_mid"], 1)
                        dve.wait_ge(s["hid_mid"], 1 + HC * b + c_ + 1)
                        if c_ >= 2:
                            dve.wait_ge(s["down_psum"], 1 + HC * b + c_ - 1)
                        else:
                            dve.wait_ge(s["down_psum"], 1 + HC * b)
                        V.scalar_tensor_tensor(out=hid[0:r, c_ % 2, :], in0=HB[0:r, T:2 * T], scalar=s_both[0:r, c_:c_ + 1],
                                               in1=hmid[0:r, :], op0=ALU.mult, op1=ALU.mult).then_inc(s["hid_made"], 1)
                        yield
                    yield

                weave(attention() if last else beside(attention(), head(b + 1), HEAD_AT), feed_forward(), FFN_AT)
                assert c.n == STEPS, (c.n, STEPS)

            for _ in head(0):
                pass
            full = HID // P
            dve.wait_ge(s["scales_in"], 16 * 5)
            V.scalar_tensor_tensor(out=s_both[:, 0:full], in0=s_gate[:, 0:full], scalar=0.5, in1=s_up[:, 0:full],
                                   op0=ALU.mult, op1=ALU.mult).then_inc(s["scales"], 1)
            V.scalar_tensor_tensor(out=s_both[0:ROWS[-1], full:], in0=s_gate[0:ROWS[-1], full:], scalar=0.5,
                                   in1=s_up[0:ROWS[-1], full:], op0=ALU.mult, op1=ALU.mult).then_inc(s["scales"], 1)
            dve.wait_ge(s["scales"], 2)
            V.tensor_scalar(s_gate[:, 0:full], s_gate[:, 0:full], 0.5, None, ALU.mult).then_inc(s["scales"], 1)
            V.tensor_scalar(s_gate[0:ROWS[-1], full:], s_gate[0:ROWS[-1], full:], 0.5, None, ALU.mult).then_inc(s["scales"], 1)
            with dve.Fori(0, B - 1) as b:
                batch(b, False)
            batch(B - 1, True)


def constants():
    bf16 = mybir.dt.np(BF16)
    r, c = np.arange(P)[:, None], np.arange(P)[None, :]
    step = np.where((r == 0) | (r - 1 < c), 1.0, 0.0).astype(np.float32)
    beyond = np.where((r > 0) & (r - 1 >= c), -BIG, 0.0).astype(np.float32)
    half = HD0 // 2
    freq = (1.0 / 10000.0 ** (np.arange(half, dtype=np.float32) * 2.0 / HD0)).astype(np.float32)
    ang = np.arange(T, dtype=np.float32)[:, None] * freq[None, :]
    cos, sin = np.cos(ang).astype(np.float32), np.sin(ang).astype(np.float32)
    e = np.arange(E)
    pick = np.zeros((P, E, P), np.float32)
    for part in range(3):
        for n in range(E):
            pick[32 * part + n, n, :] = 1.0
    return {
        "ident": np.eye(P, dtype=np.float32), "ident_bf": np.eye(P).astype(bf16),
        "row_mask": np.where(c > r, -BIG, 0.0).astype(bf16),
        "step": step, "shift": np.concatenate([beyond, 0 * beyond, beyond], 1),
        "before": np.where(r < c, 1.0, 0.0).astype(bf16),
        "multiples": np.broadcast_to(np.arange(NT, dtype=np.float32) * P, (P, NT)).copy(),
        "upto": np.broadcast_to((e[None, :] <= e[:, None]).astype(np.float32), (P, E, E)).copy(),
        "block_no": np.arange(BLOCKS, dtype=np.float32)[None],
        "token_no": (np.arange(NT)[None] * P + np.arange(P)[:, None]).astype(np.uint32),
        "pick": pick.astype(bf16),
        "cos": np.concatenate([cos, cos], 1).reshape(QT, P, HD0).transpose(1, 0, 2).copy(),
        "sin": np.concatenate([-sin, sin], 1).reshape(QT, P, HD0).transpose(1, 0, 2).copy(),
    }


def layout(inputs):
    g = {k: np.asarray(v) for k, v in inputs.items()}
    wq = g["L0_attn_Wq"].reshape(D, 2, 4, 4, HD0).transpose(0, 1, 3, 2, 4).reshape(D, D)
    full = HID // P * P
    w1 = g["L0_ffn_w1"]
    return {
        "x": g["L0_attn_x"],
        "wqkv0": np.concatenate([wq, g["L0_attn_Wk"], g["L0_attn_Wv"]], 1),
        "wo0": g["L0_attn_Wo"],
        "norm_w": g["L0_ffn_norm_w"][None], "gate_w": g["L0_ffn_gate_w"].T, "gate_b": g["L0_ffn_gate_b"][None],
        "w1": w1.reshape(E, I, 2, D).transpose(3, 0, 2, 1).reshape(D, E * 2 * I),
        "w2": g["L0_ffn_w2"].transpose(2, 0, 1).reshape(I, E * D),
        "b12": np.concatenate([g["L0_ffn_b1"].reshape(E, I, 2).transpose(0, 2, 1).reshape(E, 2 * I),
                               g["L0_ffn_b2"]], 1),
        "wqkv1": np.concatenate([g["L1_attn_wq"].T, g["L1_attn_wk"].T, g["L1_attn_wv"].T], 1),
        "wo1": g["L1_attn_wo"].T,
        "w_gate": g["L1_ffn_wq_gate"].T, "w_up": g["L1_ffn_wq_up"].T, "w_down": g["L1_ffn_wq_down"].T,
        **{name + end: part for name in ("s_gate", "s_up") for end, part in (
            ("", g["L1_ffn_" + name][:full].reshape(-1, P).T), ("_rest", g["L1_ffn_" + name][full:, None]))},
        "s_down": g["L1_ffn_s_down"][None],
    }


def kernel(**inputs):
    import concourse.bacc as bacc
    from concourse.bass_utils import run_bass_kernel_spmd

    nc = bacc.Bacc("TRN2", target_bir_lowering=False, num_devices=1)
    arrays, a = {}, {}
    for name, v in {**layout(inputs), **constants()}.items():
        v = np.ascontiguousarray(v)
        arrays[f"in_{name}"] = v
        a[name] = nc.dram_tensor(f"in_{name}", v.shape, mybir.dt.from_np(v.dtype), kind="ExternalInput").ap()
    out = nc.dram_tensor("out_x", [B, T, D], F32, kind="ExternalOutput").ap()
    build(nc, a, out)
    r = run_bass_kernel_spmd(nc, [arrays], core_ids=[0])
    return r.results[0]["out_x"]
```

```python
from contextlib import ExitStack

import numpy as np

import concourse.bass as bass
from concourse import mybir

ALU = mybir.AluOpType
ACT = mybir.ActivationFunctionType
AX = mybir.AxisListType
F32 = mybir.dt.float32
F32R = mybir.dt.float32r
BF16 = mybir.dt.bfloat16
I32 = mybir.dt.int32
U32 = mybir.dt.uint32

P = 128
B, T, D = 8, 256, 256
QT = T // P
KC = D // P
NT = B * QT
H0, G0, HD0 = 32, 8, 8
H1, HD1 = 16, 16
E, TOPK, I = 16, 4, 256
BLOCKS = NT * TOPK + E - 1
BPB = 12
HID = 704
HC = (HID + P - 1) // P
ROWS = [min(P, HID - c * P) for c in range(HC)]
EPS = 1e-5
BIG = float(2.0 ** 100)
ALPHA, LIMIT = 1.702, 7.0
NOT_A_LOGIT = -3.0e38
CHOSEN = 3.0e38


def build(nc, a, out):
    tokens = nc.dram_tensor("expert_tokens", [BLOCKS * P, 1], U32).ap()
    t_rows = nc.dram_tensor("normed_rows", [NT * P, D], F32).ap()
    y_rows = nc.dram_tensor("expert_rows", [BLOCKS * P, D], F32).ap()
    s_rows = nc.dram_tensor("attention_rows", [(NT + QT) * P, D], F32).ap()
    with ExitStack() as ctx:
        def sb(name, shape, dt=F32):
            return ctx.enter_context(nc.sbuf_tensor(name, shape, dt))

        m = {}
        m["x"] = sb("x", [P, NT, D])
        m["mean_rstd"] = sb("mean_rstd", [P, 3, NT])
        m["ident"] = sb("ident", [P, P])
        m["ident_bf"] = sb("ident_bf", [P, P], BF16)
        m["row_mask"] = sb("row_mask", [P, P], BF16)
        m["step"] = sb("step", [P, P], F32R)
        m["shift"] = sb("shift", [P, 2, 4, 3 * P], F32R)
        m["slots"] = sb("slots", [P, NT + QT, TOPK], U32)
        m["gates"] = sb("gates", [P, NT, TOPK])
        m["block_expert"] = sb("block_expert", [1, BLOCKS], I32)
        m["block_tokens"] = sb("block_tokens", [P, BLOCKS], U32)
        m["token_no"] = sb("token_no", [P, NT], U32)
        m["w_qkv"] = sb("w_qkv", [P, KC, D + 2 * G0 * HD0])
        m["w_o"] = sb("w_o", [P, QT, D])
        m["cos"] = sb("cos", [P, QT, HD0])
        m["sin"] = sb("sin", [P, QT, HD0])
        m["logits"] = sb("logits", [P, NT, E + 4])
        m["top"] = sb("top", [P, NT, 8])
        m["chosen"] = sb("chosen", [P, NT, E])
        m["row_of"] = sb("row_of", [P, NT, E])
        m["row_list"] = sb("row_list", [P, NT, 8])
        m["last_block"] = sb("last_block", [P, E])
        m["block_no"] = sb("block_no", [1, BLOCKS])
        m["kT"] = sb("kT", [P, 2, 4, T], F32R)
        m["v"] = sb("v", [P, QT, G0, 32])
        m["large"] = sb("large", [P, KC * E * 2 * I])
        m["bank"] = [ctx.enter_context(nc.psum_tensor(f"bank{i}", [P, 512], F32)) for i in range(8)]
        route(nc, a, m, tokens, t_rows)
        layer0(nc, a, m, tokens, t_rows, y_rows, s_rows)
        layer1(nc, a, m, y_rows, s_rows, out)


def sems(nc, ctx, names):
    return {n: ctx.enter_context(nc.semaphore(n)) for n in names}


class Chain:

    def __init__(self, eng, sem, base=0):
        self.eng, self.sem, self.base, self.n = eng, sem, base, 0

    def then(self, ins):
        self.n += 1
        ins.then_inc(self.sem, 1)
        return ins

    def wait(self):
        self.eng.wait_ge(self.sem, self.base + self.n)

    def link(self, ins):
        self.then(ins)
        self.wait()


def layer1_data(m):
    parts, at = {}, 0
    for name, rows, columns in (("rows", QT * TOPK, D), ("s0", QT, D), ("w_qkv", KC, 3 * D), ("w_o", KC, D),
                                ("raw", KC, HID), ("w_gate", KC, HID), ("w_up", KC, HID), ("w_down", HC, D),
                                ("qs", QT, 4 * D), ("ks", QT, 4 * D), ("f", QT, D), ("ft", QT, D)):
        parts[name] = m["large"][:, at:at + rows * columns].rearrange("p (r c) -> p r c", r=rows)
        at += rows * columns
    assert at <= KC * E * 2 * I
    parts["raw"] = parts["raw"].bitcast(I32)
    return parts


RSQRT_STEPS = 11


def rsqrt(nc, c, v, y, w):
    c.link(nc.vector.tensor_single_scalar(w.bitcast(I32), v.bitcast(I32), 1, ALU.logical_shift_right))
    c.link(nc.vector.tensor_scalar(y.bitcast(I32), w.bitcast(I32), -1.0, float(0x5F3759DF), ALU.mult, ALU.add))
    for _ in range(3):
        c.link(nc.vector.tensor_tensor(w, y, y, ALU.mult))
        c.link(nc.vector.scalar_tensor_tensor(out=w, in0=w, scalar=-0.5, in1=v, op0=ALU.mult, op1=ALU.mult))
        c.link(nc.vector.scalar_tensor_tensor(out=y, in0=w, scalar=1.5, in1=y, op0=ALU.add, op1=ALU.mult))


def route(nc, a, m, tokens, t_rows):
    x, mr, bank = m["x"], m["mean_rstd"], m["bank"]
    CH = 4
    with ExitStack() as ctx:
        def sb(name, shape, dt=F32):
            return ctx.enter_context(nc.sbuf_tensor(name, shape, dt))

        x_in = [ctx.enter_context(nc.semaphore(f"x_in{c}")) for c in range(NT // CH)]
        s = sems(nc, ctx, "consts_in cleared vec t_made stored_even stored_odd t_turned t_cols logit_psum "
                          "mask_bf counted attention_in "
                          "pool_set dma_zero".split())
        stored = [s["stored_even"], s["stored_odd"]]
        stats = sb("stats", [P, NT, 6])
        ve = sb("ve", [P, 2, NT])
        w16 = sb("w16", [P, 2, NT])
        norm_w = sb("norm_w", [P, D])
        gate_w = sb("gate_w", [P, KC, E])
        gate_b = sb("gate_b", [P, E])
        xn = sb("xn_r", [P, QT, D])
        t = sb("t_r", [P, 2, QT, D])
        tT = sb("tT_r", [P, 2, KC, QT * P])
        lg, top, mk, where, best, end = (m[n] for n in ("logits", "top", "chosen", "row_of", "row_list", "last_block"))
        marks = sb("marks", [P, NT, 8])
        repl = sb("repl", [P, NT, E + 4])
        mk_bf = sb("mk_bf", [P, NT, E], BF16)
        cmp = sb("cmp", [P, E, NT])
        need = sb("need", [P, E])
        start = sb("start", [P, E])
        before = sb("before", [P, P], BF16)
        ones = sb("ones", [P, P], BF16)
        multiples = sb("multiples", [P, NT])
        upto = sb("upto", [P, E, E])
        step_f = sb("step_f", [P, P])
        shift_f = sb("shift_f", [P, 3 * P])
        zeros = sb("zeros", [BLOCKS, P], U32)

        block = ctx.enter_context(nc.Block())

        xv = a["x"].rearrange("b (i p) d -> p (b i) d", p=P)

        @block.sync
        def _(sp):
            for name in ("t_made", "t_cols", "vec", "stored_even", "stored_odd"):
                sp.sem_inc(s[name], 1)
            sp.sem_inc(s["t_turned"], 1 + 1)
            for c in range(0, NT // CH, 2):
                sp.dma_start(x[:, c * CH:(c + 1) * CH, :], xv[:, c * CH:(c + 1) * CH, :]).then_inc(x_in[c], 16)
            constants = ((m["ident"][:], a["ident"]), (m["ident_bf"][:], a["ident_bf"]),
                         (gate_w[:], a["gate_w"].rearrange("(c p) e -> p c e", p=P)),
                         (gate_b[:], a["gate_b"].partition_broadcast(P)),
                         (norm_w[:], a["norm_w"].partition_broadcast(P)),
                         (m["row_mask"][:], a["row_mask"]), (step_f[:], a["step"]),
                         (shift_f[:], a["shift"]), (before[:], a["before"]),
                         (multiples[:], a["multiples"]), (upto[:], a["upto"]),
                         (m["block_no"][:], a["block_no"]), (m["token_no"][:], a["token_no"]))
            assert len(constants) == CONSTS
            for dst, src in constants:
                sp.dma_start(dst, src).then_inc(s["consts_in"], 16)
            for dst, src in ((m["w_qkv"][:], a["wqkv0"].rearrange("(c p) n -> p c n", p=P)),
                             (m["w_o"][:], a["wo0"].rearrange("(c p) n -> p c n", p=P)),
                             (m["cos"][:], a["cos"]), (m["sin"][:], a["sin"])):
                sp.dma_start(dst, src).then_inc(s["attention_in"], 16)
            sp.wait_ge(s["pool_set"], 1)
            sp.dma_start(tokens.rearrange("(n p) o -> n (p o)", p=P), zeros[:]).then_inc(s["dma_zero"], 16)
            with sp.Fori(0, B // 2) as pair:
                for u in range(2):
                    b = pair * 2 + u
                    sp.wait_ge(s["t_made"], 1 + QT * b + QT)
                    sp.dma_start(t_rows.rearrange("(i p) d -> p i d", p=P)[:, bass.ds(b * QT, QT), :],
                                 t[:, u]).then_inc(stored[u], 16)
            for u in range(2):
                sp.wait_ge(stored[u], 1 + 16 * (B // 2))
            sp.wait_ge(s["dma_zero"], 16)
            sp.wait_ge(s["attention_in"], 16 * 4)

        @block.gpsimd
        def _(pool):
            pool.memset(zeros[:], 0).then_inc(s["pool_set"], 1)
            nc.gpsimd.memset(m["kT"][:].rearrange("p h g t -> p (h g t)").bitcast(F32), 0.0)
            nc.gpsimd.memset(m["v"][:], 0.0).then_inc(s["cleared"], 1)
            pool.wait_ge(s["cleared"], 1)
            nc.gpsimd.memset(m["v"][:, :, :, HD0:HD0 + 1], 1.0)
            pool.wait_ge(s["consts_in"], 16 * CONSTS)
            nc.gpsimd.tensor_copy(m["step"][:], step_f[:])
            for n in range(2):
                for j in range(4):
                    nc.gpsimd.tensor_copy(m["shift"][:, n, j, :], shift_f[:])

        @block.tensor
        def _(pe):
            pe.wait_ge(s["consts_in"], 16 * CONSTS)
            with pe.Fori(0, B // 2) as pair:
                for u in range(2):
                    b = pair * 2 + u
                    pe.wait_ge(s["t_made"], 1 + QT * b + QT)
                    for k in range(KC):
                        for i in range(QT):
                            ins = pe.transpose(bank[u][:, (k * QT + i) * P:(k * QT + i + 1) * P],
                                               t[:, u, i, k * P:(k + 1) * P], m["ident"][:])
                    ins.then_inc(s["t_turned"], 1)
                for u in range(2):
                    b = pair * 2 + u
                    pe.wait_ge(s["t_cols"], 1 + b + 1)
                    for i in range(QT):
                        for k in range(KC):
                            ins = pe.matmul(bank[4][:, bass.ds((b * QT + i) * E, E)], tT[:, u, k, i * P:(i + 1) * P],
                                            gate_w[:, k, :], start=(k == 0), stop=(k == KC - 1))
                    ins.then_inc(s["logit_psum"], 1)
            pe.wait_ge(s["mask_bf"], 1)
            marks_of = mk_bf[:].rearrange("p n e -> p (n e)")
            pe.matmul(bank[2][:, 0:NT * E], before[:], marks_of, start=True, stop=True)
            for n in range(1, NT):
                pe.matmul(bank[2][:, n * E:NT * E], ones[:], marks_of[:, 0:(NT - n) * E],
                          start=False, stop=True, skip_group_check=True)
            for n in range(NT):
                ins = pe.matmul(bank[3][:, 0:E], ones[:], mk_bf[:, n, :], start=(n == 0), stop=(n == NT - 1))
            ins.then_inc(s["counted"], 1)

        @block.scalar
        def _(act):
            for c in range(1, NT // CH, 2):
                act.dma_start(x[:, c * CH:(c + 1) * CH, :], xv[:, c * CH:(c + 1) * CH, :]).then_inc(x_in[c], 16)
            with act.Fori(0, B // 2) as pair:
                for u in range(2):
                    b = pair * 2 + u
                    act.wait_ge(s["t_turned"], 1 + b + 2)
                    act.activation(tT[:, u].rearrange("p k t -> p (k t)"), bank[u][:], ACT.Copy).then_inc(s["t_cols"], 1)

        @block.vector
        def _(dve):
            c = Chain(dve, s["vec"], 1)
            c.then(dve.memset(ones[:], 1.0))
            c.then(dve.memset(lg[:, :, E:], NOT_A_LOGIT))
            c.then(dve.memset(marks[:, :, TOPK:], NOT_A_LOGIT))
            c.then(dve.memset(m["slots"][:, NT:, :], 0))
            for n in range(NT):
                if n % CH == 0:
                    dve.wait_ge(x_in[n // CH], 16)
                c.then(dve.bn_stats(stats[:, n, :], x[:, n, :]))
            c.wait()
            for n in range(NT):
                c.then(dve.bn_aggr(mr[:, 0:2, n], stats[:, n, :]))
            c.wait()
            c.link(dve.tensor_scalar(ve[:, 0, :], mr[:, 1, :], EPS, None, ALU.add))
            c.link(dve.reciprocal(w16[:, 0, :], ve[:, 0, :]))
            c.link(dve.tensor_tensor(ve[:, 1, :], w16[:, 0, :], mr[:, 1, :], ALU.mult))
            c.link(dve.tensor_scalar(ve[:, 1, :], ve[:, 1, :], EPS, None, ALU.add))
            rsqrt(nc, c, ve[:], mr[:, 1:3, :], w16[:])
            dve.wait_ge(s["consts_in"], 16 * CONSTS)
            base = c.n
            with dve.Fori(0, B // 2) as pair:
                for u in range(2):
                    b = pair * 2 + u
                    dve.wait_ge(s["t_turned"], 1 + b)
                    dve.wait_ge(stored[u], 1 + 16 * pair)
                    for i in range(QT):
                        n = b * QT + i
                        dve.tensor_scalar(xn[:, i, :], x[:, bass.ds(n, 1), :].rearrange("p o d -> p (o d)"),
                                          mr[:, 0, bass.ds(n, 1)], mr[:, 1, bass.ds(n, 1)],
                                          ALU.subtract, ALU.mult).then_inc(s["vec"], 1)
                    dve.wait_ge(s["vec"], 1 + b * QT + (base + QT))
                    for i in range(QT):
                        dve.scalar_tensor_tensor(out=t[:, u, i, :], in0=xn[:, i, :], scalar=mr[:, 2, bass.ds(b * QT + i, 1)],
                                                 in1=norm_w[:], op0=ALU.mult, op1=ALU.mult).then_inc(s["t_made"], 1)
                    dve.wait_ge(s["t_made"], 1 + QT * b + QT)
            c.n += B * QT
            dve.wait_ge(s["logit_psum"], B)
            c.link(dve.tensor_tensor(lg[:, :, 0:E], bank[4][:, 0:NT * E].rearrange("p (i e) -> p i e", e=E),
                                     gate_b[:].unsqueeze(1).broadcast_to([P, NT, E]), ALU.add))
            for n in range(NT):
                c.then(dve.max(top[:, n, :], lg[:, n, 0:E]))
            c.wait()
            c.link(dve.tensor_copy(marks[:, :, 0:TOPK], top[:, :, 0:TOPK]))
            for n in range(NT):
                c.then(dve.match_replace(repl[:, n, :], marks[:, n, :], lg[:, n, :], CHOSEN))
            c.wait()
            c.link(dve.tensor_tensor(mk[:], repl[:, :, 0:E], lg[:, :, 0:E], ALU.not_equal))
            dve.tensor_copy(mk_bf[:], mk[:]).then_inc(s["mask_bf"], 1)
            dve.wait_ge(s["counted"], 1)
            c.link(dve.tensor_tensor(cmp[:], bank[3][:, 0:E].unsqueeze(2).broadcast_to([P, E, NT]),
                                     multiples[:].unsqueeze(1).broadcast_to([P, E, NT]), ALU.is_gt))
            c.link(dve.tensor_reduce(need[:], cmp[:], AX.X, ALU.add))
            c.link(dve.tensor_tensor(cmp[:], need[:].unsqueeze(1).broadcast_to([P, E, E]), upto[:], ALU.mult))
            c.link(dve.tensor_reduce(end[:], cmp[:], AX.X, ALU.add))
            c.link(dve.tensor_tensor(start[:], end[:], need[:], ALU.subtract))
            c.link(dve.tensor_scalar(start[:], start[:], float(P), 1.0, ALU.mult, ALU.add))
            c.link(dve.tensor_tensor(where[:], bank[2][:, 0:NT * E].rearrange("p (n e) -> p n e", e=E), start[:].unsqueeze(1).broadcast_to([P, NT, E]), ALU.add))
            c.link(dve.tensor_tensor(where[:], where[:], mk[:], ALU.mult))
            for n in range(NT):
                c.then(dve.max(best[:, n, :], where[:, n, :]))
            c.wait()
            dve.tensor_scalar(m["slots"][:, 0:NT, :], best[:, :, 0:TOPK], -1.0, None, ALU.add).then_inc(s["counted"], 2)


CONSTS = 13


def weave(attention, other, steps):
    tick, attending, beside = 0, True, True
    while attending or beside:
        if attending:
            attending = next(attention, "end") != "end"
        for _ in range(steps.get(tick, 0) if attending else 1):
            beside = beside and next(other, "end") != "end"
        tick += 1


def batches(eng, batch):
    batch(0, 0, 0, 0)
    with eng.Fori(1, B - 1) as b:
        batch(b, b * BPB - BPB, b * (BPB // 2) - BPB // 2, BPB)
    done = (B - 2) * BPB
    batch(B - 1, done, done // 2, BLOCKS - done)


def layer0(nc, a, m, tokens, t_rows, y_rows, s_rows):
    x, mr, bank = m["x"], m["mean_rstd"], m["bank"]
    S, C, MISC, HB, TB, YB = bank[0:2], bank[2:4], bank[4], bank[5], bank[6], bank[7]
    RING = bank[0:4]
    HJ = H0 // 4
    QKV = D + 2 * G0 * HD0
    ROT = D + G0 * HD0
    ROW_FILLS, KEY_FILLS = 3 * HJ, 3 * G0
    EXPERTS_AT = {1: 1, 2: 2, 3: 3, 4: 1, 5: 2, 6: 1, 7: 1, 8: 2, 10: 1, 13: 1, 14: 1, 20: 1, 21: 1, 22: 1,
                  24: 1, 26: 2, 28: 1, 30: 1, 32: 2, 33: 3, 34: 1, 40: 2, 43: 1, 45: 1, 50: 1, 52: 1, 55: 2, 57: 1,
                  59: 1, 63: 2, 65: 1, 66: 3, 67: 1, 68: 1, 69: 1}
    with ExitStack() as ctx:
        def sb(name, shape, dt=F32):
            return ctx.enter_context(nc.sbuf_tensor(name, shape, dt))

        counts = ("xn_made xn_turned xn_cols qkv_psum rot v_made stacked q_turned q_cols k_turned k_cols "
                          "row_scores row_max max_turned max_rows shift_even shift_odd key_scores probs ctx_psum ctx_out "
                          "ctx_turned ctx_norm norm_steps s_psum s_made s_stored "
                          "picked rows_turned rows_cols hidden gate_in lin_in tanh_done lin_scaled mid acted "
                          "act_turned act_cols y_psum y_made y_stored").split()
        s = sems(nc, ctx, ["weights_in", "experts_in", "parts", "set", "bias_steps", "gate_steps", "exp_in", "exp_out", "experts_known", "gathered_even", "gathered_odd",
                          "scattered", "layer1_in", "tokens_back", "tokens_f", "tokens_turned", "blocks_known"] + counts)
        gathered = [s["gathered_even"], s["gathered_odd"]]
        w_qkv, w_o, cos, sin = m["w_qkv"], m["w_o"], m["cos"], m["sin"]
        shift_in = [s["shift_even"], s["shift_odd"]]
        w1 = m["large"][:].rearrange("p (k n) -> p k n", k=KC)
        w2 = sb("w2", [P, KC, E * D])
        pick = sb("pick", [P, E * P], BF16)
        bias = sb("bias", [P, 2 * I + D], BF16)
        xn = sb("xn", [P, QT, D])
        xnT = sb("xnT", [P, KC, T])
        t1 = sb("rot_a", [P, ROT])
        t2 = sb("rot_b", [P, ROT])
        qT = sb("qT", [P, HJ, T], F32R)
        kT, v = m["kT"], m["v"]
        gates_of = sb("gates_of", [P, NT, E])
        scratch = sb("scratch", [P, NT, E])
        sums = sb("sums", [P, NT])
        ended = sb("ended", [1, BLOCKS, E])
        expert_no = sb("expert_no", [1, BLOCKS])
        nmax = sb("nmax", [P, QT, H0])
        nmaxT = sb("nmaxT", [H0, 3 * P], F32R)
        shared = sb("shared", [P, 3072])
        qs = shared[:, 0:2048].rearrange("p (i n) -> p i n", i=QT)
        ks = shared[:, 2048:2560].rearrange("p (i n) -> p i n", i=QT)
        p0 = shared[:, 0:2048].rearrange("p (u j q) -> p u j q", u=2, j=4)
        p1 = shared[:, 2048:3072].rearrange("p (u j q) -> p u j q", u=2, j=4)
        ctx_sb = sb("ctx_sb", [P, QT, 4 * P])
        rec = sb("rec", [P, 4, 4])
        cx = sb("cx", [P, QT, D])
        s_sb = sb("s_sb", [P, QT, D])
        rows_in = sb("rows_in", [P, 2, D])
        rows_no = sb("rows_no", [P, 2], U32)
        carrier = sb("carrier0", [P, 2])
        rowsT = sb("rowsT", [P, KC * P])
        gate = sb("gate", [P, I])
        lin = sb("lin", [P, I])
        tanh = sb("tanh", [P, I])
        actd = sb("actd", [P, I])
        actT = sb("actT", [P, KC * P])
        y = sb("y", [P, D])
        back = sb("back", [BLOCKS, P], U32)
        back_f = sb("back_f", [BLOCKS, P])
        block = ctx.enter_context(nc.Block())


        @block.sync
        def _(sp):
            for name in counts:
                sp.sem_inc(s[name], 1)
            sp.dma_start(pick[:], a["pick"].rearrange("p e m -> p (e m)")).then_inc(s["weights_in"], 16)
            sp.wait_ge(s["set"], 1)
            for part in range(3):
                sp.dma_start(w2[32 * part:32 * part + E, 0, 0:768], a["b12"]).then_inc(s["weights_in"], 16)
            for k in range(KC):
                sp.dma_start(w1[:, k, :], a["w1"][k * P:(k + 1) * P, :]).then_inc(s["experts_in"], 16)
            sp.wait_ge(s["parts"], 3)
            for k in range(KC):
                sp.dma_start(w2[:, k, :], a["w2"][k * P:(k + 1) * P, :]).then_inc(s["experts_in"], 16)

            def batch(b, first, pairs, blocks):
                def attention():
                    def send_shift(g):
                        sp.wait_ge(s["key_scores"], 1 + KEY_FILLS * b + 3 * max(g - 1, 0))
                        if g == 0:
                            sp.wait_ge(s["max_rows"], 1 + 2 * b + 2)
                        sp.dma_start(m["shift"][0:1, g % 2, :, :].bitcast(F32),
                                     nmaxT[4 * g:4 * g + 4, :].bitcast(F32)).then_inc(shift_in[g % 2], 16)

                    for _ in range(33):
                        yield
                    send_shift(0)
                    send_shift(1)
                    yield
                    for g in range(G0):
                        if 1 <= g < G0 - 1:
                            send_shift(g + 1)
                        for _ in range(4):
                            yield
                    for _ in range(4):
                        yield
                    sp.wait_ge(s["s_made"], 1 + b + 1)
                    sp.dma_start(s_rows.rearrange("(n p) d -> p n d", p=P)[:, bass.ds(b * QT, QT), :],
                                 s_sb[:]).then_inc(s["s_stored"], 16)
                    yield

                def experts():
                    yield
                    for k in range(blocks + 1 if blocks else 0):
                        if k < blocks:
                            yield
                        if k >= 1:
                            yield
                        if k < blocks:
                            yield
                        if k >= 1:
                            sp.wait_ge(s["y_made"], 1 + first + k)
                            sp.dma_start(y_rows[bass.ds((first + k - 1) * P, P), :], y[:]).then_inc(s["y_stored"], 16)
                            yield

                weave(attention(), experts(), EXPERTS_AT)

            batches(sp, batch)
            sp.wait_ge(s["s_made"], 1 + B)
            sp.dma_start(s_rows.rearrange("(n p) d -> p n d", p=P)[:, NT:NT + QT, :], s_sb[:]).then_inc(s["s_stored"], 16)
            sp.wait_ge(s["s_stored"], 1 + 16 * (B + 1))
            sp.wait_ge(s["y_stored"], 1 + 16 * BLOCKS)

        @block.gpsimd
        def _(pool):
            def gather(n, u):
                nc.gpsimd.tensor_copy(rows_no[:, u:u + 1], m["block_tokens"][:, bass.ds(n, 1)]).then_inc(s["picked"], 1)
                pool.wait_ge(s["picked"], 1 + 2 * n + 2)
                nc.gpsimd.tensor_tensor(carrier[:, 1:2], carrier[:, 0:1], carrier[:, 0:1], ALU.add).then_inc(s["picked"], 1)
                nc.gpsimd.indirect_dma_start(rows_in[:, u, :], None, t_rows,
                                             bass.IndirectOffsetOnAxis(rows_no[:, u:u + 1], 0)).then_inc(gathered[u], 16)

            pool.memset(w2[:, 0, 0:768], 0.0).then_inc(s["set"], 1)
            pool.memset(carrier[:], 0.0).then_inc(s["picked"], 1)
            pool.wait_ge(s["picked"], 1 + 1)
            for n in range(NT):
                for k in range(TOPK):
                    pool.indirect_dma_start(tokens, bass.IndirectOffsetOnAxis(m["slots"][:, n, k:k + 1], 0),
                                            m["token_no"][:, n:n + 1], None).then_inc(s["scattered"], 16)
            pool.wait_ge(s["scattered"], 16 * NT * TOPK)
            pool.dma_start(back[:], tokens.rearrange("(n p) o -> n (p o)", p=P)).then_inc(s["tokens_back"], 16)
            pool.wait_ge(s["blocks_known"], 1)
            gather(0, 0)
            gather(1, 1)

            def batch(first, pairs, blocks, ahead):
                for k in range(blocks):
                    if k + 2 < blocks + ahead:
                        pool.wait_ge(s["rows_turned"], 1 + (first + k) + 1)
                        pool.wait_ge(gathered[k % 2], 16 * (pairs + k // 2 + 1))
                        gather(first + k + 2, k % 2)

            with pool.Fori(0, B - 2) as b:
                batch(b * BPB, b * (BPB // 2), BPB, 2)
            done = (B - 2) * BPB
            batch(done, done // 2, BLOCKS - done, 0)
            pool.wait_ge(gathered[0], 16 * ((BLOCKS + 1) // 2))
            pool.wait_ge(gathered[1], 16 * (BLOCKS // 2))
            pool.wait_ge(s["y_stored"], 1 + 16 * BLOCKS)
            coming = layer1_data(m)
            for i in range(QT):
                for k in range(TOPK):
                    pool.indirect_dma_start(coming["rows"][:, i * TOPK + k, :], None, y_rows,
                                            bass.IndirectOffsetOnAxis(m["slots"][:, i, k:k + 1], 0)).then_inc(s["layer1_in"], 16)
            for dst, src in (("w_qkv", "wqkv1"), ("w_o", "wo1"), ("raw", "w_gate")):
                pool.dma_start(coming[dst], a[src].rearrange("(c p) n -> p c n", p=P)).then_inc(s["layer1_in"], 16)
            pool.wait_ge(s["layer1_in"], 16 * (QT * TOPK + 3))

        @block.tensor
        def _(pe):
            pe.wait_ge(s["weights_in"], 16 * 4)
            def batch(b, first, pairs, blocks):
                def attention():
                    yield
                    pe.wait_ge(s["xn_made"], 1 + QT * b + QT)
                    pe.wait_ge(s["s_made"], 1 + b)
                    for k in range(KC):
                        for i in range(QT):
                            ins = pe.transpose(MISC[:, (k * QT + i) * P:(k * QT + i + 1) * P],
                                               xn[:, i, k * P:(k + 1) * P], m["ident"][:])
                    ins.then_inc(s["xn_turned"], 1)
                    yield
                    pe.wait_ge(s["xn_cols"], 1 + b + 1)
                    pe.wait_ge(s["ctx_out"], 1 + 4 * b)
                    for i in range(QT):
                        for k in range(KC):
                            ins = pe.matmul(C[i][:, 0:QKV], xnT[:, k, i * P:(i + 1) * P], w_qkv[:, k, :],
                                            start=(k == 0), stop=(k == KC - 1))
                        ins.then_inc(s["qkv_psum"], 1)
                    yield
                    yield
                    pe.wait_ge(s["probs"], 1 + KEY_FILLS * b)
                    for f in range(4):
                        if f == 0:
                            pe.wait_ge(s["stacked"], 1 + 2 * b + 2)
                        for c in range(2):
                            for i in range(QT):
                                ins = pe.transpose(RING[f][:, (c * QT + i) * P:(c * QT + i + 1) * P],
                                                   qs[:, i, (2 * f + c) * P:(2 * f + c + 1) * P], m["ident"][:])
                        ins.then_inc(s["q_turned"], 1)
                        yield
                    pe.wait_ge(s["xn_cols"], 1 + b + 1)
                    for h in range(2):
                        for i in range(QT):
                            ins = pe.transpose(MISC[:, (h * QT + i) * P:(h * QT + i + 1) * P],
                                               ks[:, i, h * P:(h + 1) * P], m["ident"][:])
                    ins.then_inc(s["k_turned"], 1)
                    yield
                    pe.wait_ge(s["k_cols"], 1 + 4 * b + 4)
                    pe.wait_ge(s["q_cols"], 1 + 4 * b + 4)
                    for f in range(ROW_FILLS):
                        hj, u = f // 3, f % 3
                        if f >= 4:
                            pe.wait_ge(s["row_max"], 1 + ROW_FILLS * b + f - 3)
                        o = RING[f % 4]
                        if u == 0:
                            pe.matmul(o[:], qT[:, hj, 0:P], kT[:, hj // 4, :, 0:P], start=True, stop=False)
                            ins = pe.matmul(o[:], m["ident_bf"][:], m["row_mask"][:].unsqueeze(1).broadcast_to([P, 4, P]),
                                            start=False, stop=True)
                        else:
                            pe.matmul(o[:], qT[:, hj, P:T], kT[:, hj // 4, 2 * u - 2:2 * u, :], start=True, stop=False)
                            ins = pe.matmul(o[:].rearrange("p (g t) -> p g t", g=2)[:, :, P:T], m["ident_bf"][:],
                                            m["row_mask"][:].unsqueeze(1).broadcast_to([P, 2, P]), start=False, stop=True)
                        ins.then_inc(s["row_scores"], 1)
                        yield
                    pe.wait_ge(s["row_max"], 1 + ROW_FILLS * b + ROW_FILLS)
                    for i in range(QT):
                        ins = pe.transpose(MISC[0:H0, i * P:(i + 1) * P], nmax[:, i, :], m["ident"][:])
                    ins.then_inc(s["max_turned"], 1)
                    yield

                    def context(g):
                        h, o = g // 4, 32 * (g % 4)
                        pe.wait_ge(s["probs"], 1 + KEY_FILLS * b + 3 * g + 3)
                        if g == 4:
                            pe.wait_ge(s["ctx_out"], 1 + 4 * b + 2)
                        pe.matmul(C[0][o:o + 32, :], v[:, 0, g, :], p0[:, g % 2, :, 0:P], start=True, stop=True)
                        pe.matmul(C[1][o:o + 32, :], v[:, 0, g, :], p0[:, g % 2, :, P:T], start=True, stop=False)
                        pe.matmul(C[1][o:o + 32, :], v[:, 1, g, :], p1[:, g % 2, :, :],
                                  start=False, stop=True).then_inc(s["ctx_psum"], 1)

                    def turn_context(n):
                        pe.wait_ge(s["ctx_out"], 1 + 4 * b + 2 * (n // 2) + 2)
                        if n == 0:
                            pe.wait_ge(s["max_rows"], 1 + 2 * b + 2)
                        else:
                            pe.wait_ge(s["ctx_norm"], 1 + 4 * b + n)
                        for j in range(4):
                            ins = pe.transpose(MISC[:, j * P:(j + 1) * P], ctx_sb[:, n % 2, j * P:(j + 1) * P], m["ident"][:])
                        ins.then_inc(s["ctx_turned"], 1)

                    for g in range(G0):
                        pe.wait_ge(shift_in[g % 2], 1 + 16 * (G0 // 2 * b + g // 2 + 1))
                        for u in range(3):
                            f = 3 * g + u
                            if f >= 2:
                                pe.wait_ge(s["probs"], 1 + KEY_FILLS * b + f - 1)
                            o = S[f % 2]
                            h = g // 4
                            if u < 2:
                                pe.matmul(o[:], kT[:, h, g % 4, 0:P], qT[:, 4 * h + 2 * u:4 * h + 2 * u + 2, :],
                                          start=True, stop=False)
                                ins = pe.matmul(o[:], m["step"][:], m["shift"][:, g % 2, 2 * u:2 * u + 2, 0:T],
                                                start=False, stop=True)
                            else:
                                pe.matmul(o[:], kT[:, h, g % 4, P:T], qT[:, 4 * h:4 * h + 4, P:T],
                                          start=True, stop=False)
                                ins = pe.matmul(o[:], m["step"][:], m["shift"][:, g % 2, :, T:3 * P],
                                                start=False, stop=True)
                            ins.then_inc(s["key_scores"], 1)
                            yield
                        if g >= 1:
                            context(g - 1)
                        if g == 5:
                            turn_context(0)
                        if g == 6:
                            turn_context(1)
                        yield
                    context(G0 - 1)
                    yield
                    turn_context(2)
                    yield
                    turn_context(3)
                    yield
                    pe.wait_ge(s["ctx_norm"], 1 + 4 * b + 4)
                    for r in range(QT):
                        for i in range(QT):
                            ins = pe.matmul(MISC[:, r * D:(r + 1) * D], cx[:, i, r * P:(r + 1) * P], w_o[:, i, :],
                                            start=(i == 0), stop=(i == QT - 1))
                    ins.then_inc(s["s_psum"], 1)
                    if blocks == 0:
                        pe.wait_ge(s["tokens_f"], 1)
                        pe.transpose(TB[:, 0:BLOCKS], back_f[:], m["ident"][0:BLOCKS, 0:BLOCKS]).then_inc(s["tokens_turned"], 1)
                    yield

                def experts():
                    def turn_rows(k):
                        n = first + k
                        pe.wait_ge(gathered[k % 2], 16 * (pairs + k // 2 + 1))
                        pe.wait_ge(s["rows_cols"], 1 + n)
                        for c in range(KC):
                            ins = pe.transpose(TB[:, c * P:(c + 1) * P], rows_in[:, k % 2, c * P:(c + 1) * P], m["ident"][:])
                        ins.then_inc(s["rows_turned"], 1)

                    if blocks:
                        turn_rows(0)
                    yield
                    for k in range(blocks + 1 if blocks else 0):
                        n = first + k
                        if k < blocks:
                            if k == 0:
                                pe.wait_ge(s["experts_in"], 64)
                                pe.wait_ge(s["experts_known"], 1)
                            e = pe.value_load(m["block_expert"][0:1, bass.ds(n, 1)], min_val=0, max_val=E - 1)
                            expert[k % 2] = e
                            pe.wait_ge(s["rows_cols"], 1 + n + 1)
                            pe.wait_ge(s["lin_in"], 1 + n)
                            pe.matmul(HB[:], pick[:, bass.ds(e * P, P)], bias[:, 0:2 * I], start=True, stop=False)
                            for c in range(KC):
                                ins = pe.matmul(HB[:], rowsT[:, c * P:(c + 1) * P], w1[:, c, bass.ds(e * 2 * I, 2 * I)],
                                                start=False, stop=(c == KC - 1))
                            ins.then_inc(s["hidden"], 1)
                            yield
                        if k >= 1:
                            pe.wait_ge(s["acted"], 1 + n)
                            pe.wait_ge(s["y_made"], 1 + n - 1)
                            for c in range(KC):
                                ins = pe.transpose(YB[:, D + c * P:D + (c + 1) * P], actd[:, c * P:(c + 1) * P], m["ident"][:])
                            ins.then_inc(s["act_turned"], 1)
                            yield
                        if k < blocks:
                            if k + 1 < blocks:
                                turn_rows(k + 1)
                            yield
                        if k >= 1:
                            e = expert[(k - 1) % 2]
                            pe.wait_ge(s["act_cols"], 1 + n)
                            pe.matmul(YB[:, 0:D], pick[:, bass.ds(e * P, P)], bias[:, 2 * I:], start=True, stop=False)
                            for c in range(KC):
                                ins = pe.matmul(YB[:, 0:D], actT[:, c * P:(c + 1) * P], w2[:, c, bass.ds(e * D, D)],
                                                start=False, stop=(c == KC - 1))
                            ins.then_inc(s["y_psum"], 1)
                            yield

                expert = [None, None]
                weave(attention(), experts(), EXPERTS_AT)

            batches(pe, batch)

        @block.scalar
        def _(act):
            def batch(b, first, pairs, blocks):
                def attention():
                    yield
                    act.wait_ge(s["xn_turned"], 1 + b + 1)
                    act.activation(xnT[:].rearrange("p k t -> p (k t)"), MISC[:], ACT.Copy).then_inc(s["xn_cols"], 1)
                    yield
                    yield
                    yield
                    for f in range(4):
                        act.wait_ge(s["q_turned"], 1 + 4 * b + f + 1)
                        act.activation(qT[:, 2 * f:2 * f + 2, :].rearrange("p c t -> p (c t)"), RING[f][:],
                                       ACT.Copy).then_inc(s["q_cols"], 1)
                        yield
                    if blocks == 0:
                        act.wait_ge(s["exp_in"], 1)
                        act.activation(scratch[:], scratch[:], ACT.Exp).then_inc(s["exp_out"], 1)
                    act.wait_ge(s["k_turned"], 1 + b + 1)
                    for g in range(2):
                        r = slice(32 * g, 32 * g + 32)
                        act.activation(kT[r, :, g, :], MISC[r, :].rearrange("p (h t) -> p h t", h=2),
                                       ACT.Copy).then_inc(s["k_cols"], 1)
                    yield
                    for _ in range(ROW_FILLS + 1):
                        yield
                    for g in range(G0):
                        for u in range(3):
                            f = 3 * g + u
                            act.wait_ge(s["key_scores"], 1 + KEY_FILLS * b + f + 1)
                            if u == 0 and g >= 2:
                                act.wait_ge(s["ctx_psum"], 1 + G0 * b + g - 1)
                            if u < 2:
                                dst = p0[:, g % 2, 2 * u:2 * u + 2, :].rearrange("p j q -> p (j q)")
                            else:
                                dst = p1[:, g % 2, :, :].rearrange("p j q -> p (j q)")
                            act.activation(dst, S[f % 2][:], ACT.Exp, scale=float(HD0) ** -0.5).then_inc(s["probs"], 1)
                            yield
                        if g == 4:
                            evacuate(0)
                        yield
                    evacuate(1)
                    yield
                    yield
                    yield
                    act.wait_ge(s["s_psum"], 1 + b + 1)
                    act.wait_ge(s["s_stored"], 1 + 16 * b)
                    act.activation(s_sb[:].rearrange("p i d -> p (i d)"), MISC[:], ACT.Copy).then_inc(s["s_made"], 1)
                    yield

                def evacuate(h):
                    act.wait_ge(s["ctx_psum"], 1 + G0 * b + 4 * h + 4)
                    act.wait_ge(s["ctx_turned"], 1 + 4 * b + 2 * h)
                    for i in range(QT):
                        act.activation(ctx_sb[:, i, :], C[i][:], ACT.Copy).then_inc(s["ctx_out"], 1)

                def experts():
                    def copy_rows(k):
                        n = first + k
                        act.wait_ge(s["rows_turned"], 1 + n + 1)
                        act.wait_ge(s["hidden"], 1 + n)
                        act.activation(rowsT[:], TB[:, 0:KC * P], ACT.Copy).then_inc(s["rows_cols"], 1)

                    if blocks:
                        copy_rows(0)
                    yield
                    for k in range(blocks + 1 if blocks else 0):
                        n = first + k
                        if k < blocks:
                            act.wait_ge(s["gate_in"], 1 + n + 1)
                            act.wait_ge(s["mid"], 1 + n)
                            act.activation(tanh[:], gate[:], ACT.Tanh, scale=ALPHA / 2).then_inc(s["tanh_done"], 1)
                            yield
                        if k >= 1:
                            act.wait_ge(s["act_turned"], 1 + n)
                            act.wait_ge(s["y_psum"], 1 + n - 1)
                            act.activation(actT[:], YB[:, D:D + KC * P], ACT.Copy).then_inc(s["act_cols"], 1)
                            yield
                        if k < blocks:
                            if k + 1 < blocks:
                                copy_rows(k + 1)
                            yield
                        if k >= 1:
                            act.wait_ge(s["y_psum"], 1 + n)
                            act.wait_ge(s["y_stored"], 1 + 16 * (n - 1))
                            act.activation(y[:], YB[:, 0:D], ACT.Copy).then_inc(s["y_made"], 1)
                            yield

                weave(attention(), experts(), EXPERTS_AT)

            batches(act, batch)

        @block.vector
        def _(dve):
            V = nc.vector
            def split_bias():
                dve.wait_ge(s["weights_in"], 16 * 4)
                b12, left, half = w2[:, 0, 0:768], w2[:, 0, 768:1536], w2[:, 0, 1536:1920].bitcast(BF16)
                V.tensor_copy(bias[:], b12).then_inc(s["parts"], 1)
                dve.wait_ge(s["parts"], 1)
                V.tensor_tensor(left, b12, bias[:], ALU.subtract).then_inc(s["bias_steps"], 1)
                dve.wait_ge(s["bias_steps"], 1)
                V.tensor_copy(half, left).then_inc(s["bias_steps"], 1)
                dve.wait_ge(s["bias_steps"], 2)
                V.tensor_copy(bias[32:64, :], half[32:64, :]).then_inc(s["parts"], 1)
                V.tensor_tensor(bias[64:96, :], left[64:96, :], half[64:96, :], ALU.subtract).then_inc(s["parts"], 1)

            def softmax():
                V.tensor_tensor(scratch[:], m["logits"][:, :, 0:E], m["top"][:, :, 0:1].broadcast_to([P, NT, E]),
                                ALU.subtract).then_inc(s["exp_in"], 1)

            def gates():
                c = Chain(dve, s["gate_steps"])
                where, best, end = m["row_of"], m["row_list"], m["last_block"]
                dve.wait_ge(s["exp_out"], 1)
                c.link(V.tensor_tensor(gates_of[:], scratch[:], m["chosen"][:], ALU.mult))
                c.link(V.tensor_reduce(sums[:], gates_of[:], AX.X, ALU.add))
                c.link(V.reciprocal(sums[:], sums[:]))
                c.link(V.tensor_tensor(gates_of[:], gates_of[:], sums[:].unsqueeze(2).broadcast_to([P, NT, E]), ALU.mult))
                for k in range(TOPK):
                    c.link(V.tensor_tensor(scratch[:], where[:], best[:, :, k:k + 1].broadcast_to([P, NT, E]), ALU.is_equal))
                    c.link(V.tensor_tensor(scratch[:], scratch[:], gates_of[:], ALU.mult))
                    c.link(V.tensor_reduce(m["gates"][:, :, k], scratch[:], AX.X, ALU.add))
                c.link(V.tensor_tensor(ended[:], end[0:1, :].unsqueeze(1).broadcast_to([1, BLOCKS, E]),
                                       m["block_no"][:].unsqueeze(2).broadcast_to([1, BLOCKS, E]), ALU.is_le))
                c.link(V.tensor_reduce(expert_no[:], ended[:], AX.X, ALU.add))
                V.tensor_scalar(m["block_expert"][:], expert_no[:], float(E - 1), None, ALU.min).then_inc(s["experts_known"], 1)

            STEPS = 5 * QT + 4
            def batch(b, first, pairs, blocks):
                c = Chain(dve, s["norm_steps"], 1 + b * STEPS)

                def rotate(i):
                    dve.wait_ge(s["qkv_psum"], 1 + QT * b + i + 1)
                    if i == 0:
                        dve.wait_ge(s["ctx_psum"], 1 + G0 * b)
                    V.tensor_copy(v[:, i, :, 0:HD0],
                                  C[i][:, ROT:QKV].rearrange("p (g d) -> p g d", d=HD0)).then_inc(s["v_made"], 1)
                    qk = C[i][:, 0:ROT].rearrange("p (h d) -> p h d", d=HD0)
                    t1v = t1[:].rearrange("p (h d) -> p h d", d=HD0)
                    t2v = t2[:].rearrange("p (h d) -> p h d", d=HD0)
                    n, hd = ROT // HD0, HD0 // 2
                    c.then(V.tensor_tensor(t1v, qk, cos[:, i:i + 1, :].broadcast_to([P, n, HD0]), ALU.mult))
                    c.then(V.tensor_tensor(t2v[:, :, 0:hd], qk[:, :, hd:], sin[:, i:i + 1, 0:hd].broadcast_to([P, n, hd]), ALU.mult))
                    c.link(V.tensor_tensor(t2v[:, :, hd:], qk[:, :, 0:hd], sin[:, i:i + 1, hd:].broadcast_to([P, n, hd]), ALU.mult))
                    c.link(V.tensor_tensor(t1[:], t1[:], t2[:], ALU.add))
                    q = t1[:, 0:D].rearrange("p (n o d) -> p n o d", o=1, d=HD0).broadcast_to([P, 32, 2, HD0])
                    k = t1[:, D:ROT].rearrange("p (n o d) -> p n o d", o=1, d=HD0).broadcast_to([P, 8, 2, HD0])
                    q4 = qs[:, i, :].rearrange("p (n r c d) -> p n r c d", r=2, c=2, d=HD0)
                    k4 = ks[:, i, :].rearrange("p (n r c d) -> p n r c d", r=2, c=2, d=HD0)
                    V.tensor_copy(q4[:, :, 0, :, :].bitcast(F32R), q).then_inc(s["v_made"], 1)
                    c.link(V.tensor_copy(k4[:, :, :, 0, :].bitcast(F32R), k))
                    dve.wait_ge(s["v_made"], 1 + 4 * b + 2 * i + 2)
                    V.tensor_tensor(k4[:, :, :, 1, :].bitcast(F32R), k, k4[:, :, :, 0, :], ALU.subtract).then_inc(s["rot"], 1)
                    V.tensor_tensor(q4[:, :, 1, :, :].bitcast(F32R), q, q4[:, :, 0, :, :],
                                    ALU.subtract).then_inc(s["stacked"], 1)
                    dve.wait_ge(s["stacked"], 1 + 2 * b + i + 1)
                    dve.wait_ge(s["rot"], 1 + 2 * b + i + 1)

                def normalise(n):
                    h, i = n // 2, n % 2
                    dve.wait_ge(s["ctx_turned"], 1 + 4 * b + n + 1)
                    o = MISC[:].rearrange("p (j g r) -> p j g r", j=4, g=4)
                    c.link(V.reciprocal(rec[:], o[:, :, :, HD0]))
                    dst = cx[:, i, h * P:(h + 1) * P].rearrange("p (g j d) -> p j g d", g=4, j=4)
                    V.tensor_tensor(dst, o[:, :, :, 0:HD0], rec[:].unsqueeze(3).broadcast_to([P, 4, 4, HD0]),
                                    ALU.mult).then_inc(s["ctx_norm"], 1)

                first_batch = blocks == 0

                def attention():
                    dve.wait_ge(s["xn_turned"], 1 + b)
                    for i in range(QT):
                        n = b * QT + i
                        V.tensor_scalar(xn[:, i, :], x[:, bass.ds(n, 1), :].rearrange("p o d -> p (o d)"),
                                        mr[:, 0, bass.ds(n, 1)], mr[:, 1, bass.ds(n, 1)],
                                        ALU.subtract, ALU.mult).then_inc(s["xn_made"], 1)
                    yield
                    yield
                    rotate(0)
                    yield
                    rotate(1)
                    if first_batch:
                        split_bias()
                        softmax()
                    yield
                    for _ in range(4):
                        yield
                    dve.wait_ge(s["k_turned"], 1 + b + 1)
                    for g in range(2, 4):
                        r = slice(32 * g, 32 * g + 32)
                        V.tensor_copy(kT[r, :, g, :], MISC[r, :].rearrange("p (h t) -> p h t", h=2)).then_inc(s["k_cols"], 1)
                    yield
                    for f in range(ROW_FILLS):
                        hj, u = f // 3, f % 3
                        h, j = hj // 4, hj % 4
                        o = RING[f % 4]
                        dve.wait_ge(s["row_scores"], 1 + ROW_FILLS * b + f + 1)
                        heads = nmax[:].rearrange("p i (h g j) -> p i h g j", h=2, g=4)
                        if u == 0:
                            dst, src = heads[:, 0, h, :, j], o[:].rearrange("p (g t) -> p g t", g=4)
                        else:
                            dst, src = heads[:, 1, h, 2 * u - 2:2 * u, j], o[:].rearrange("p (g t) -> p g t", g=2)
                        V.tensor_reduce(dst, src, AX.X, ALU.max, negate=True).then_inc(s["row_max"], 1)
                        yield
                    dve.wait_ge(s["max_turned"], 1 + b + 1)
                    for u in range(2):
                        dve.wait_ge(shift_in[u], 1 + 16 * (G0 // 2) * b)
                    V.tensor_copy(nmaxT[:, 0:T], MISC[0:H0, 0:T]).then_inc(s["max_rows"], 1)
                    V.tensor_copy(nmaxT[:, T:], MISC[0:H0, P:T]).then_inc(s["max_rows"], 1)
                    yield
                    for g in range(G0):
                        for _ in range(3):
                            yield
                        if g == 0 and first_batch:
                            gates()
                        if g == 5:
                            normalise(0)
                        if g == 6:
                            normalise(1)
                        yield
                    yield
                    normalise(2)
                    yield
                    normalise(3)
                    yield
                    if first_batch:
                        dve.wait_ge(s["tokens_back"], 16)
                        V.tensor_copy(back_f[:], back[:]).then_inc(s["tokens_f"], 1)
                        dve.wait_ge(s["tokens_turned"], 1)
                        V.tensor_copy(m["block_tokens"][:], TB[:, 0:BLOCKS]).then_inc(s["blocks_known"], 1)
                    yield

                def experts():
                    yield
                    for k in range(blocks + 1 if blocks else 0):
                        n = first + k
                        if k < blocks:
                            dve.wait_ge(s["hidden"], 1 + n + 1)
                            dve.wait_ge(s["acted"], 1 + n)
                            V.tensor_scalar(gate[:], HB[:, 0:I], LIMIT, None, ALU.min).then_inc(s["gate_in"], 1)
                            V.tensor_scalar(lin[:], HB[:, I:2 * I], LIMIT, -LIMIT, ALU.min, ALU.max).then_inc(s["lin_in"], 1)
                            dve.wait_ge(s["lin_in"], 1 + n + 1)
                            V.tensor_scalar(lin[:], lin[:], 1.0, 0.5, ALU.add, ALU.mult).then_inc(s["lin_scaled"], 1)
                            yield
                        if k >= 1:
                            yield
                        if k < blocks:
                            dve.wait_ge(s["tanh_done"], 1 + n + 1)
                            dve.wait_ge(s["act_turned"], 1 + n)
                            V.scalar_tensor_tensor(out=actd[:], in0=tanh[:], scalar=1.0, in1=gate[:],
                                                   op0=ALU.add, op1=ALU.mult).then_inc(s["mid"], 1)
                            dve.wait_ge(s["mid"], 1 + n + 1)
                            dve.wait_ge(s["lin_scaled"], 1 + n + 1)
                            V.tensor_tensor(actd[:], actd[:], lin[:], ALU.mult).then_inc(s["acted"], 1)
                            yield
                        if k >= 1:
                            yield

                weave(attention(), experts(), EXPERTS_AT)
                assert c.n == STEPS, c.n

            batches(dve, batch)


def beside(attention, head, at):
    for tick, _ in enumerate(attention):
        if tick in at:
            next(head, None)
        yield
    assert next(head, None) is None


def layer1(nc, a, m, y_rows, s_rows, out):
    x, mr, bank = m["x"], m["mean_rstd"], m["bank"]
    S, C, MISC, HIDDEN, DOWN = bank[0:2], bank[2:4], bank[4], bank[5:7], bank[7]
    RING = bank[0:4]
    PAIRS, GROUPS = H1 // 2, H1 // 4
    HEAD_AT = {28: 0, 32: 1, 35: 2, 38: 3}
    FFN_AT = {3: 1, 4: 2, 5: 1, 9: 2, 12: 1, 13: 1, 22: 1, 24: 1, 25: 1, 26: 2, 39: 1, 42: 1, 43: 1, 44: 1,
              45: 1}
    ROW_FILLS, KEY_FILLS = GROUPS + PAIRS, 3 * GROUPS
    CHOICES = QT * TOPK
    with ExitStack() as ctx:
        def sb(name, shape, dt=F32):
            return ctx.enter_context(nc.sbuf_tensor(name, shape, dt))

        counts = ("s_in picked1 head_steps steps1 f_made f_tanh x_made xn_made1 xn_turned1 xn_cols1 qk_psum v_psum "
                          "v_cols high_parts stacked1 q_turned1 q_cols1 k_turned1 k_low k_high row_scores1 row_max1 max_turned1 "
                          "max_rows1 shift_even1 shift_odd1 key_scores1 probs1 ctx_psum1 ctx_out1 ctx_turned1 ctx_norm1 "
                          "cx_turned cx_cols s_psum1 s_made1 "
                          "hid_psum hid_tanh hid_mid hid_made down_psum down_made out_tanh out_mid out_made stored").split()
        s = sems(nc, ctx, ["counts_set", "ffn_in", "cleared", "cast", "scales", "scales_in", "rows_in1"] + counts)
        shift_in = [s["shift_even1"], s["shift_odd1"]]
        data = layer1_data(m)
        w_qkv, w_o, raw, w_gate, w_up, w_down, s0, rows, f, ft, qs, ks = (
            data[n] for n in "w_qkv w_o raw w_gate w_up w_down s0 rows f ft qs ks".split())
        s_gate = sb("s_gate", [P, HC])
        s_up = sb("s_up", [P, HC])
        s_both = sb("s_both", [P, HC])
        s_down = sb("s_down", [P, D])
        rows_no = sb("rows_no1", [P, CHOICES], U32)
        stats = sb("stats1", [P, QT, 6])
        mv = sb("mv", [P, 2, QT])
        ve = sb("ve1", [P, QT])
        carrier = sb("carrier", [P, 2])
        ready = sb("ready", [P, 2])
        w2 = sb("w_2", [P, QT])
        xn = sb("xn1", [P, QT, D])
        xnT = sb("xnT1", [P, KC, T])
        qT = sb("qT1", [P, PAIRS, T], F32R)
        kT = sb("kT1", [P, PAIRS, 2, T], F32R)
        v = sb("v1", [P, QT, H1, 32])
        nmax = sb("nmax1", [P, QT, H1])
        nmaxT = sb("nmaxT1", [H1, 3 * P], F32R)
        p0 = sb("p0_1", [P, 2, 4, T])
        p1 = sb("p1_1", [P, 2, 4, P])
        ctx_sb = sb("ctx_sb1", [P, 2, T])
        rec = sb("rec1", [P, QT, 4])
        cx = sb("cx1", [P, QT, D])
        cxT = sb("cxT1", [P, KC, T])
        s1 = sb("s1", [P, QT, D])
        htanh = sb("htanh", [P, 2, T])
        hmid = sb("hmid", [P, T])
        hid = sb("hid", [P, 2, T])
        down = sb("down", [P, QT, D])
        dtanh = sb("dtanh", [P, QT, D])
        dout = sb("dout", [P, QT, D])
        block = ctx.enter_context(nc.Block())


        @block.sync
        def _(sp):
            for name in counts:
                sp.sem_inc(s[name], 1)
            sp.sem_inc(s["counts_set"], 1)
            sv = s_rows.rearrange("(n p) d -> p n d", p=P)
            ov = out.rearrange("b (i p) d -> p (b i) d", p=P)
            sp.dma_start(s0[:], sv[:, 0:QT, :]).then_inc(s["s_in"], 16)
            full = HID // P
            for name, dst in (("s_gate", s_gate), ("s_up", s_up)):
                sp.dma_start(dst[:, 0:full], a[name]).then_inc(s["scales_in"], 16)
                sp.dma_start(dst[0:ROWS[-1], full:], a[name + "_rest"]).then_inc(s["scales_in"], 16)
            sp.dma_start(s_down[:], a["s_down"].partition_broadcast(P)).then_inc(s["scales_in"], 16)
            sp.wait_ge(s["cast"], 1)
            sp.dma_start(raw[:], a["w_up"].rearrange("(c p) n -> p c n", p=P)).then_inc(s["ffn_in"], 16)
            sp.wait_ge(s["cast"], 2)
            rd = raw[:].rearrange("p c n -> p (c n)")
            for c in range(HC - 1):
                sp.dma_start(rd[:, c * D:(c + 1) * D], a["w_down"][c * P:(c + 1) * P, :]).then_inc(s["ffn_in"], 16)
            sp.wait_ge(s["cast"], 3)
            sp.dma_start(rd[0:ROWS[-1], 0:D], a["w_down"][(HC - 1) * P:, :]).then_inc(s["ffn_in"], 16)

            def next_rows(b):
                sp.wait_ge(s["x_made"], 1 + QT * b + QT)
                sp.dma_start(s0[:], sv[:, bass.ds(b * QT + QT, QT), :]).then_inc(s["s_in"], 16)

            def batch(b, last):
                def attention():
                    def send_shift(g):
                        sp.wait_ge(s["key_scores1"], 1 + KEY_FILLS * b + 3 * max(g - 1, 0))
                        if g == 0:
                            sp.wait_ge(s["max_rows1"], 1 + 2 * b + 2)
                        sp.dma_start(m["shift"][0:1, g % 2, :, :].bitcast(F32),
                                     nmaxT[4 * g:4 * g + 4, :].bitcast(F32)).then_inc(shift_in[g % 2], 16)

                    for _ in range(26):
                        yield
                    send_shift(0)
                    send_shift(1)
                    yield
                    for g in range(GROUPS):
                        if 1 <= g < GROUPS - 1:
                            send_shift(g + 1)
                        for _ in range(4):
                            yield
                    for _ in range(4):
                        yield
                    if not last:
                        next_rows(b + 1)
                    yield
                    sp.wait_ge(s["out_made"], 1 + QT * b + QT)
                    sp.dma_start(ov[:, bass.ds(b * QT, QT), :], dout[:]).then_inc(s["stored"], 16)
                    yield

                for _ in attention():
                    pass

            next_rows(0)
            with sp.Fori(0, B - 1) as b:
                batch(b, False)
            batch(B - 1, True)
            sp.wait_ge(s["stored"], 1 + 16 * B)
            sp.wait_ge(s["s_in"], 1 + 16 * (B + 1))

        @block.gpsimd
        def _(pool):
            pool.memset(ready[:], 0.0).then_inc(s["picked1"], 1)
            pool.wait_ge(s["picked1"], 1 + 1)

            def gather_rows(b):
                nc.gpsimd.tensor_copy(rows_no[:], m["slots"][:, bass.ds(b * QT, QT), :].rearrange("p i k -> p (i k)")
                                      ).then_inc(s["picked1"], 1)
                pool.wait_ge(s["picked1"], 1 + 2 * b)
                nc.gpsimd.tensor_tensor(ready[:, 1:2], ready[:, 0:1], ready[:, 0:1], ALU.add).then_inc(s["picked1"], 1)
                for c in range(CHOICES):
                    nc.gpsimd.indirect_dma_start(rows[:, c, :], None, y_rows,
                                                 bass.IndirectOffsetOnAxis(rows_no[:, c:c + 1], 0)).then_inc(s["rows_in1"], 16)
                pool.wait_ge(s["rows_in1"], 16 * CHOICES * b)

            pool.memset(kT[:].rearrange("p h g t -> p (h g t)").bitcast(F32), 0.0).then_inc(s["cleared"], 1)
            pool.memset(v[:], 0.0).then_inc(s["cleared"], 1)
            pool.wait_ge(s["cleared"], 2)
            pool.memset(v[:, :, :, HD1:HD1 + 1], 1.0).then_inc(s["cleared"], 1)
            full = HID // P
            nc.gpsimd.tensor_scalar(w_gate[:], raw[:], -128.0, None, ALU.add).then_inc(s["cast"], 1)
            pool.wait_ge(s["ffn_in"], 16)
            nc.gpsimd.tensor_scalar(w_up[:], raw[:], -128.0, None, ALU.add).then_inc(s["cast"], 1)
            rd = raw[:].rearrange("p c n -> p (c n)")
            pool.wait_ge(s["ffn_in"], 16 * (1 + full))
            nc.gpsimd.tensor_scalar(w_down[:, 0:full, :].rearrange("p c n -> p (c n)"), rd[:, 0:full * D], -128.0, None,
                                    ALU.add).then_inc(s["cast"], 1)
            pool.wait_ge(s["ffn_in"], 16 * (2 + full))
            nc.gpsimd.tensor_scalar(w_down[0:ROWS[-1], full, :], rd[0:ROWS[-1], 0:D], -128.0, None,
                                    ALU.add).then_inc(s["cast"], 1)
            with pool.Fori(1, B) as b:
                pool.wait_ge(s["f_made"], 1 + QT * b)
                gather_rows(b)

        @block.tensor
        def _(pe):
            pe.wait_ge(s["cleared"], 3)
            def batch(b, last):
                def attention():
                    yield
                    yield
                    pe.wait_ge(s["xn_made1"], 1 + QT * b + QT)
                    pe.wait_ge(s["s_made1"], 1 + b)
                    for k in range(KC):
                        for i in range(QT):
                            ins = pe.transpose(MISC[:, (k * QT + i) * P:(k * QT + i + 1) * P],
                                               xn[:, i, k * P:(k + 1) * P], m["ident"][:])
                    ins.then_inc(s["xn_turned1"], 1)
                    yield
                    pe.wait_ge(s["xn_cols1"], 1 + b + 1)
                    pe.wait_ge(s["ctx_out1"], 1 + GROUPS * b)
                    for i in range(QT):
                        for k in range(KC):
                            ins = pe.matmul(C[i][:], xnT[:, k, i * P:(i + 1) * P], w_qkv[:, k, 0:2 * D],
                                            start=(k == 0), stop=(k == KC - 1))
                        ins.then_inc(s["qk_psum"], 1)
                    for i in range(QT):
                        for k in range(KC):
                            ins = pe.matmul(MISC[:, i * D:(i + 1) * D], xnT[:, k, i * P:(i + 1) * P], w_qkv[:, k, 2 * D:],
                                            start=(k == 0), stop=(k == KC - 1))
                    ins.then_inc(s["v_psum"], 1)
                    yield
                    yield
                    yield
                    pe.wait_ge(s["probs1"], 1 + KEY_FILLS * b)
                    for f_ in range(8):
                        src = qs if f_ < 4 else ks
                        if f_ == 0:
                            pe.wait_ge(s["stacked1"], 1 + 2 * QT * b + 2 * QT)
                        if f_ >= 4:
                            pe.wait_ge(s["q_cols1"], 1 + 4 * b + f_ - 3)
                        for c in range(2):
                            for i in range(QT):
                                j = 2 * (f_ % 4) + c
                                ins = pe.transpose(RING[f_ % 4][:, (c * QT + i) * P:(c * QT + i + 1) * P],
                                                   src[:, i, j * P:(j + 1) * P], m["ident"][:])
                        ins.then_inc(s["q_turned1" if f_ < 4 else "k_turned1"], 1)
                        yield
                    pe.wait_ge(s["k_low"], 1 + 4 * b + 4)
                    pe.wait_ge(s["k_high"], 1 + 4 * b + 4)
                    for f_ in range(ROW_FILLS):
                        if f_ >= 4:
                            pe.wait_ge(s["row_max1"], 1 + ROW_FILLS * b + f_ - 3)
                        o = RING[f_ % 4]
                        if f_ < GROUPS:
                            for c in range(2):
                                j = 2 * f_ + c
                                pe.matmul(o[:, c * T:(c + 1) * T], qT[:, j, 0:P], kT[:, j, :, 0:P], start=True, stop=False)
                                ins = pe.matmul(o[:, c * T:(c + 1) * T], m["ident_bf"][:],
                                                m["row_mask"][:].unsqueeze(1).broadcast_to([P, 2, P]), start=False, stop=True)
                        else:
                            j = f_ - GROUPS
                            pe.matmul(o[:], qT[:, j, P:T], kT[:, j, :, :], start=True, stop=False)
                            ins = pe.matmul(o[:].rearrange("p (g t) -> p g t", g=2)[:, :, P:T], m["ident_bf"][:],
                                            m["row_mask"][:].unsqueeze(1).broadcast_to([P, 2, P]), start=False, stop=True)
                        ins.then_inc(s["row_scores1"], 1)
                        yield
                    pe.wait_ge(s["row_max1"], 1 + ROW_FILLS * b + ROW_FILLS)
                    pe.wait_ge(s["v_cols"], 1 + b + 1)
                    for i in range(QT):
                        ins = pe.transpose(MISC[0:H1, i * P:(i + 1) * P], nmax[:, i, :], m["ident"][:])
                    ins.then_inc(s["max_turned1"], 1)
                    yield

                    def context(g):
                        pe.wait_ge(s["probs1"], 1 + KEY_FILLS * b + 3 * g + 3)
                        if g >= 2:
                            pe.wait_ge(s["ctx_out1"], 1 + GROUPS * b + g - 1)
                        for j in range(4):
                            o, h = C[g % 2][32 * j:32 * j + 32, :], 4 * g + j
                            pe.matmul(o[:, 0:T], v[:, 0, h, :], p0[:, g % 2, j, :], start=True, stop=False)
                            ins = pe.matmul(o[:, P:T], v[:, 1, h, :], p1[:, g % 2, j, :], start=False, stop=True)
                        ins.then_inc(s["ctx_psum1"], 1)

                    def turn_context(g):
                        pe.wait_ge(s["ctx_out1"], 1 + GROUPS * b + g + 1)
                        if g == 0:
                            pe.wait_ge(s["max_rows1"], 1 + 2 * b + 2)
                        else:
                            pe.wait_ge(s["ctx_norm1"], 1 + GROUPS * b + g)
                        for i in range(QT):
                            ins = pe.transpose(MISC[:, i * P:(i + 1) * P], ctx_sb[:, g % 2, i * P:(i + 1) * P], m["ident"][:])
                        ins.then_inc(s["ctx_turned1"], 1)

                    for g in range(GROUPS):
                        pe.wait_ge(shift_in[g % 2], 1 + 16 * (GROUPS // 2 * b + g // 2 + 1))
                        for u in range(3):
                            f_ = 3 * g + u
                            if f_ >= 2:
                                pe.wait_ge(s["probs1"], 1 + KEY_FILLS * b + f_ - 1)
                            o = S[f_ % 2]
                            if u < 2:
                                j = 2 * g + u
                                for c in range(2):
                                    pe.matmul(o[:, c * T:(c + 1) * T], kT[:, j, c, 0:P], qT[:, j, :],
                                              start=(c == 0), stop=False, skip_group_check=True)
                                ins = pe.matmul(o[:], m["step"][:], m["shift"][:, g % 2, 2 * u:2 * u + 2, 0:T],
                                                start=False, stop=True, skip_group_check=True)
                            else:
                                for c in range(4):
                                    j = 2 * g + c // 2
                                    pe.matmul(o[:, c * P:(c + 1) * P], kT[:, j, c % 2, P:T], qT[:, j, P:T],
                                              start=(c == 0), stop=False, skip_group_check=True)
                                ins = pe.matmul(o[:], m["step"][:], m["shift"][:, g % 2, :, T:3 * P],
                                                start=False, stop=True, skip_group_check=True)
                            ins.then_inc(s["key_scores1"], 1)
                            yield
                        if g >= 1:
                            context(g - 1)
                        if g >= 2:
                            turn_context(g - 2)
                        yield
                    context(GROUPS - 1)
                    turn_context(GROUPS - 2)
                    yield
                    turn_context(GROUPS - 1)
                    yield
                    pe.wait_ge(s["ctx_norm1"], 1 + GROUPS * b + GROUPS)
                    for k in range(KC):
                        for i in range(QT):
                            ins = pe.transpose(MISC[:, (k * QT + i) * P:(k * QT + i + 1) * P],
                                               cx[:, i, k * P:(k + 1) * P], m["ident"][:])
                    ins.then_inc(s["cx_turned"], 1)
                    yield
                    pe.wait_ge(s["cx_cols"], 1 + b + 1)
                    for i in range(QT):
                        for k in range(KC):
                            ins = pe.matmul(MISC[:, i * D:(i + 1) * D], cxT[:, k, i * P:(i + 1) * P], w_o[:, k, :],
                                            start=(k == 0), stop=(k == KC - 1))
                    ins.then_inc(s["s_psum1"], 1)
                    yield
                    yield

                def feed_forward():
                    for c in range(HC + 2):
                        if c < HC:
                            r = ROWS[c]
                            if c == 0:
                                pe.wait_ge(s["xn_cols1"], 1 + b + 1)
                                pe.wait_ge(s["cast"], 4)
                            pe.wait_ge(s["hid_made"], 1 + HC * b + max(c - 1, 0))
                            for n, w in enumerate((w_gate, w_up)):
                                if n == 1:
                                    yield
                                for k in range(KC):
                                    ins = pe.matmul(HIDDEN[c % 2][0:r, n * T:(n + 1) * T], w[:, k, c * P:c * P + r],
                                                    xnT[:, k, :], start=(k == 0), stop=(k == KC - 1))
                            ins.then_inc(s["hid_psum"], 1)
                            yield
                        if c >= 2:
                            d_ = c - 2
                            r = ROWS[d_]
                            pe.wait_ge(s["hid_made"], 1 + HC * b + d_ + 1)
                            if d_ == 0:
                                pe.wait_ge(s["down_made"], 1 + QT * b)
                            for i in range(QT):
                                ins = pe.matmul(DOWN[:, i * D:(i + 1) * D], hid[0:r, d_ % 2, i * P:(i + 1) * P],
                                                w_down[0:r, d_, :], start=(d_ == 0 and i == 0),
                                                stop=(d_ == HC - 1 and i == QT - 1), skip_group_check=True)
                            ins.then_inc(s["down_psum"], 1)
                            yield

                weave(attention(), feed_forward(), FFN_AT)

            with pe.Fori(0, B - 1) as b:
                batch(b, False)
            batch(B - 1, True)

        @block.scalar
        def _(act):
            def head(b):
                yield
                for i in range(QT):
                    act.wait_ge(s["f_made"], 1 + QT * b + i + 1)
                    act.activation(ft[:, i, :], f[:, i, :], ACT.Tanh, scale=0.5).then_inc(s["f_tanh"], 1)
                yield

            def batch(b, last):
                def attention():
                    yield
                    yield
                    act.wait_ge(s["xn_turned1"], 1 + b + 1)
                    act.activation(xnT[:].rearrange("p k t -> p (k t)"), MISC[:], ACT.Copy).then_inc(s["xn_cols1"], 1)
                    yield
                    act.wait_ge(s["v_psum"], 1 + b + 1)
                    act.activation(v[:, :, :, 0:HD1], MISC[:].rearrange("p (i h d) -> p i h d", i=QT, d=HD1),
                                   ACT.Copy).then_inc(s["v_cols"], 1)
                    yield
                    act.wait_ge(s["qk_psum"], 1 + QT * b + 2)
                    act.wait_ge(s["q_turned1"], 1 + 4 * b)
                    act.wait_ge(s["k_turned1"], 1 + 4 * b)
                    parts = "p (n r c d) -> p n r c d"
                    for dst, columns in ((qs[:, 1, :].rearrange(parts, r=2, c=2, d=HD1)[:, :, 0, :, :], C[1][:, 0:D]),
                                         (ks[:, 1, :].rearrange(parts, r=2, c=2, d=HD1)[:, :, :, 0, :], C[1][:, D:2 * D])):
                        act.activation(dst.bitcast(F32R),
                                       columns.rearrange("p (n o d) -> p n o d", o=1, d=HD1).broadcast_to([P, H1, 2, HD1]),
                                       ACT.Copy).then_inc(s["high_parts"], 1)
                    yield
                    yield
                    for f_ in range(4):
                        act.wait_ge(s["q_turned1"], 1 + 4 * b + f_ + 1)
                        act.activation(qT[:, 2 * f_:2 * f_ + 2, :].rearrange("p c t -> p (c t)"), RING[f_ % 4][:],
                                       ACT.Copy).then_inc(s["q_cols1"], 1)
                        yield
                    for f_ in range(4):
                        act.wait_ge(s["k_turned1"], 1 + 4 * b + f_ + 1)
                        act.activation(kT[0:64, 2 * f_:2 * f_ + 2, 0, :], RING[f_ % 4][0:64, :].rearrange("p (c t) -> p c t", c=2),
                                       ACT.Copy).then_inc(s["k_low"], 1)
                        yield
                    for _ in range(ROW_FILLS + 1):
                        yield

                    def evacuate(g):
                        act.wait_ge(s["ctx_psum1"], 1 + GROUPS * b + g + 1)
                        act.wait_ge(s["ctx_turned1"], 1 + GROUPS * b + max(g - 1, 0))
                        act.activation(ctx_sb[:, g % 2, :], C[g % 2][:, 0:T], ACT.Copy).then_inc(s["ctx_out1"], 1)

                    for g in range(GROUPS):
                        for u in range(3):
                            f_ = 3 * g + u
                            act.wait_ge(s["key_scores1"], 1 + KEY_FILLS * b + f_ + 1)
                            if u == 0 and g >= 2:
                                act.wait_ge(s["ctx_psum1"], 1 + GROUPS * b + g - 1)
                            dst = (p0[:, g % 2, 2 * u:2 * u + 2, :] if u < 2 else p1[:, g % 2, :, :])
                            act.activation(dst.rearrange("p j q -> p (j q)"), S[f_ % 2][:], ACT.Exp,
                                           scale=float(HD1) ** -0.5).then_inc(s["probs1"], 1)
                            yield
                        if g >= 1:
                            evacuate(g - 1)
                        yield
                    evacuate(GROUPS - 1)
                    yield
                    yield
                    act.wait_ge(s["cx_turned"], 1 + b + 1)
                    act.activation(cxT[:].rearrange("p k t -> p (k t)"), MISC[:], ACT.Copy).then_inc(s["cx_cols"], 1)
                    yield
                    act.wait_ge(s["s_psum1"], 1 + b + 1)
                    act.wait_ge(s["out_mid"], 1 + 2 * QT * b)
                    act.activation(s1[:].rearrange("p i d -> p (i d)"), MISC[:], ACT.Copy).then_inc(s["s_made1"], 1)
                    yield
                    for i in range(QT):
                        act.wait_ge(s["down_made"], 1 + QT * b + i + 1)
                        act.activation(dtanh[:, i, :], down[:, i, :], ACT.Tanh, scale=0.5).then_inc(s["out_tanh"], 1)
                    yield

                def feed_forward():
                    for c in range(HC):
                        yield
                        r = ROWS[c]
                        if c == 0:
                            act.wait_ge(s["scales"], 4)
                        act.wait_ge(s["hid_psum"], 1 + HC * b + c + 1)
                        act.wait_ge(s["hid_mid"], 1 + HC * b + max(c - 1, 0))
                        act.activation(htanh[0:r, c % 2, :], HIDDEN[c % 2][0:r, 0:T], ACT.Tanh,
                                       scale=s_gate[0:r, c:c + 1]).then_inc(s["hid_tanh"], 1)
                        yield
                        if c >= 2:
                            yield
                    yield
                    yield

                weave(attention() if last else beside(attention(), head(b + 1), HEAD_AT), feed_forward(), FFN_AT)

            for _ in head(0):
                pass
            with act.Fori(0, B - 1) as b:
                batch(b, False)
            batch(B - 1, True)

        @block.vector
        def _(dve):
            V = nc.vector
            HEAD = QT * (TOPK + 2 + 2) + 3 + RSQRT_STEPS
            STEPS = 2 + GROUPS
            def head(b, first=False):
                c = Chain(dve, s["head_steps"], 1 + b * HEAD)
                xs = [x[:, bass.ds(b * QT + i, 1), :].rearrange("p o d -> p (o d)") for i in range(QT)]
                if first:
                    dve.wait_ge(s["counts_set"], 1)
                else:
                    dve.wait_ge(s["rows_in1"], 16 * CHOICES * b)
                for i in range(QT):
                    n = b * QT + i
                    c.then(V.tensor_scalar(f[:, i, :], xs[i], mr[:, 0, bass.ds(n, 1)], mr[:, 1, bass.ds(n, 1)],
                                           ALU.subtract, ALU.mult))
                for k in range(TOPK):
                    c.wait()
                    for i in range(QT):
                        ins = V.scalar_tensor_tensor(out=f[:, i, :], in0=rows[:, i * TOPK + k, :],
                                                     scalar=m["gates"][:, bass.ds(b * QT + i, 1), k], in1=f[:, i, :],
                                                     op0=ALU.mult, op1=ALU.add)
                        if k < TOPK - 1:
                            c.then(ins)
                        else:
                            ins.then_inc(s["f_made"], 1)
                yield
                dve.wait_ge(s["s_in"], 1 + 16 * (b + 1))
                for i in range(QT):
                    dve.wait_ge(s["f_tanh"], 1 + QT * b + i + 1)
                    c.then(V.scalar_tensor_tensor(out=ft[:, i, :], in0=ft[:, i, :], scalar=1.0, in1=f[:, i, :],
                                                  op0=ALU.add, op1=ALU.mult))
                c.wait()
                for i in range(QT):
                    c.then(V.scalar_tensor_tensor(out=ft[:, i, :], in0=ft[:, i, :], scalar=0.5, in1=s0[:, i, :],
                                                  op0=ALU.mult, op1=ALU.mult))
                c.wait()
                for i in range(QT):
                    V.tensor_tensor(xs[i], xs[i], ft[:, i, :], ALU.add).then_inc(s["x_made"], 1)
                yield
                dve.wait_ge(s["x_made"], 1 + QT * b + QT)
                c.then(V.memset(carrier[:, 0:1], 0.0))
                for i in range(QT):
                    c.then(V.bn_stats(stats[:, i, :], xs[i]))
                c.wait()
                c.then(V.memset(carrier[:, 1:2], 0.0))
                for i in range(QT):
                    c.then(V.bn_aggr(mv[:, :, i], stats[:, i, :]))
                c.wait()
                c.link(V.tensor_scalar(ve[:], mv[:, 1, :], EPS, None, ALU.add))
                yield
                rsqrt(nc, c, ve[:], mv[:, 1, :], w2[:])
                dve.wait_ge(s["xn_turned1"], 1 + b)
                for i in range(QT):
                    V.tensor_scalar(xn[:, i, :], xs[i], mv[:, 0, i:i + 1], mv[:, 1, i:i + 1],
                                    ALU.subtract, ALU.mult).then_inc(s["xn_made1"], 1)
                assert c.n == HEAD, c.n
            def batch(b, last):
                c = Chain(dve, s["steps1"], 1 + b * STEPS)
                xs = [x[:, bass.ds(b * QT + i, 1), :].rearrange("p o d -> p (o d)") for i in range(QT)]

                def normalise(g):
                    dve.wait_ge(s["ctx_turned1"], 1 + GROUPS * b + g + 1)
                    o = MISC[:, 0:T].rearrange("p (i j r) -> p i j r", i=QT, j=4)
                    c.link(V.reciprocal(rec[:], o[:, :, :, HD1]))
                    V.tensor_tensor(cx[:, :, 64 * g:64 * g + 64].rearrange("p i (j d) -> p i j d", j=4), o[:, :, :, 0:HD1],
                                    rec[:].unsqueeze(3).broadcast_to([P, QT, 4, HD1]), ALU.mult).then_inc(s["ctx_norm1"], 1)

                def attention():
                    for _ in range(4):
                        yield
                    for i in range(QT):
                        dve.wait_ge(s["qk_psum"], 1 + QT * b + i + 1)
                        q = C[i][:, 0:D].rearrange("p (n o d) -> p n o d", o=1, d=HD1).broadcast_to([P, H1, 2, HD1])
                        k = C[i][:, D:2 * D].rearrange("p (n o d) -> p n o d", o=1, d=HD1).broadcast_to([P, H1, 2, HD1])
                        q4 = qs[:, i, :].rearrange("p (n r c d) -> p n r c d", r=2, c=2, d=HD1)
                        k4 = ks[:, i, :].rearrange("p (n r c d) -> p n r c d", r=2, c=2, d=HD1)
                        if i == 0:
                            c.then(V.tensor_copy(q4[:, :, 0, :, :].bitcast(F32R), q))
                            c.link(V.tensor_copy(k4[:, :, :, 0, :].bitcast(F32R), k))
                        else:
                            dve.wait_ge(s["high_parts"], 1 + 2 * b + 2)
                        V.tensor_tensor(q4[:, :, 1, :, :].bitcast(F32R), q, q4[:, :, 0, :, :],
                                        ALU.subtract).then_inc(s["stacked1"], 1)
                        V.tensor_tensor(k4[:, :, :, 1, :].bitcast(F32R), k, k4[:, :, :, 0, :],
                                        ALU.subtract).then_inc(s["stacked1"], 1)
                        yield
                    for _ in range(4):
                        yield
                    for f_ in range(4):
                        dve.wait_ge(s["k_turned1"], 1 + 4 * b + f_ + 1)
                        V.tensor_copy(kT[64:P, 2 * f_:2 * f_ + 2, 1, :],
                                      RING[f_ % 4][64:P, :].rearrange("p (c t) -> p c t", c=2)).then_inc(s["k_high"], 1)
                        yield
                    for f_ in range(ROW_FILLS):
                        dve.wait_ge(s["row_scores1"], 1 + ROW_FILLS * b + f_ + 1)
                        o = RING[f_ % 4]
                        if f_ < GROUPS:
                            dst, src = nmax[:, 0, 4 * f_:4 * f_ + 4], o[:].rearrange("p (g t) -> p g t", g=4)
                        else:
                            j = f_ - GROUPS
                            dst, src = nmax[:, 1, 2 * j:2 * j + 2], o[:].rearrange("p (g t) -> p g t", g=2)
                        V.tensor_reduce(dst, src, AX.X, ALU.max, negate=True).then_inc(s["row_max1"], 1)
                        yield
                    dve.wait_ge(s["max_turned1"], 1 + b + 1)
                    for u in range(2):
                        dve.wait_ge(shift_in[u], 1 + 16 * (GROUPS // 2) * b)
                    V.tensor_copy(nmaxT[:, 0:T], MISC[0:H1, 0:T]).then_inc(s["max_rows1"], 1)
                    V.tensor_copy(nmaxT[:, T:], MISC[0:H1, P:T]).then_inc(s["max_rows1"], 1)
                    yield
                    for g in range(GROUPS):
                        for _ in range(3):
                            yield
                        if g >= 2:
                            normalise(g - 2)
                        yield
                    normalise(GROUPS - 2)
                    yield
                    normalise(GROUPS - 1)
                    yield
                    yield
                    yield
                    for i in range(QT):
                        if i == 0:
                            dve.wait_ge(s["down_psum"], 1 + HC * b + HC)
                        V.tensor_tensor(down[:, i, :], DOWN[:, i * D:(i + 1) * D], s_down[:], ALU.mult).then_inc(s["down_made"], 1)
                    yield
                    for i in range(QT):
                        dve.wait_ge(s["out_tanh"], 1 + QT * b + i + 1)
                        V.scalar_tensor_tensor(out=dtanh[:, i, :], in0=dtanh[:, i, :], scalar=1.0, in1=down[:, i, :],
                                               op0=ALU.add, op1=ALU.mult).then_inc(s["out_mid"], 1)
                    dve.wait_ge(s["s_made1"], 1 + b + 1)
                    dve.wait_ge(s["out_mid"], 1 + 2 * QT * b + QT)
                    for i in range(QT):
                        V.scalar_tensor_tensor(out=dtanh[:, i, :], in0=dtanh[:, i, :], scalar=0.5, in1=s1[:, i, :],
                                               op0=ALU.mult, op1=ALU.mult).then_inc(s["out_mid"], 1)
                    dve.wait_ge(s["out_mid"], 1 + 2 * QT * b + 2 * QT)
                    dve.wait_ge(s["stored"], 1 + 16 * b)
                    for i in range(QT):
                        V.tensor_tensor(dout[:, i, :], xs[i], dtanh[:, i, :], ALU.add).then_inc(s["out_made"], 1)
                    yield

                def feed_forward():
                    yield
                    yield
                    for c_ in range(HC):
                        if c_ + 1 < HC:
                            yield
                        r = ROWS[c_]
                        HB = HIDDEN[c_ % 2]
                        dve.wait_ge(s["hid_tanh"], 1 + HC * b + c_ + 1)
                        dve.wait_ge(s["hid_made"], 1 + HC * b + c_)
                        V.scalar_tensor_tensor(out=hmid[0:r, :], in0=htanh[0:r, c_ % 2, :], scalar=1.0, in1=HB[0:r, 0:T],
                                               op0=ALU.add, op1=ALU.mult).then_inc(s["hid_mid"], 1)
                        dve.wait_ge(s["hid_mid"], 1 + HC * b + c_ + 1)
                        if c_ >= 2:
                            dve.wait_ge(s["down_psum"], 1 + HC * b + c_ - 1)
                        else:
                            dve.wait_ge(s["down_psum"], 1 + HC * b)
                        V.scalar_tensor_tensor(out=hid[0:r, c_ % 2, :], in0=HB[0:r, T:2 * T], scalar=s_both[0:r, c_:c_ + 1],
                                               in1=hmid[0:r, :], op0=ALU.mult, op1=ALU.mult).then_inc(s["hid_made"], 1)
                        if c_ + 1 < HC:
                            yield
                        if c_ >= 1:
                            yield
                    yield

                weave(attention() if last else beside(attention(), head(b + 1), HEAD_AT), feed_forward(), FFN_AT)
                assert c.n == STEPS, (c.n, STEPS)

            for _ in head(0, first=True):
                pass
            full = HID // P
            dve.wait_ge(s["scales_in"], 16 * 5)
            V.scalar_tensor_tensor(out=s_both[:, 0:full], in0=s_gate[:, 0:full], scalar=0.5, in1=s_up[:, 0:full],
                                   op0=ALU.mult, op1=ALU.mult).then_inc(s["scales"], 1)
            V.scalar_tensor_tensor(out=s_both[0:ROWS[-1], full:], in0=s_gate[0:ROWS[-1], full:], scalar=0.5,
                                   in1=s_up[0:ROWS[-1], full:], op0=ALU.mult, op1=ALU.mult).then_inc(s["scales"], 1)
            dve.wait_ge(s["scales"], 2)
            V.tensor_scalar(s_gate[:, 0:full], s_gate[:, 0:full], 0.5, None, ALU.mult).then_inc(s["scales"], 1)
            V.tensor_scalar(s_gate[0:ROWS[-1], full:], s_gate[0:ROWS[-1], full:], 0.5, None, ALU.mult).then_inc(s["scales"], 1)
            with dve.Fori(0, B - 1) as b:
                batch(b, False)
            batch(B - 1, True)


def constants():
    bf16 = mybir.dt.np(BF16)
    r, c = np.arange(P)[:, None], np.arange(P)[None, :]
    step = np.where((r == 0) | (r - 1 < c), 1.0, 0.0).astype(np.float32)
    beyond = np.where((r > 0) & (r - 1 >= c), -BIG, 0.0).astype(np.float32)
    half = HD0 // 2
    freq = (1.0 / 10000.0 ** (np.arange(half, dtype=np.float32) * 2.0 / HD0)).astype(np.float32)
    ang = np.arange(T, dtype=np.float32)[:, None] * freq[None, :]
    cos, sin = np.cos(ang).astype(np.float32), np.sin(ang).astype(np.float32)
    e = np.arange(E)
    pick = np.zeros((P, E, P), np.float32)
    for part in range(3):
        for n in range(E):
            pick[32 * part + n, n, :] = 1.0
    return {
        "ident": np.eye(P, dtype=np.float32), "ident_bf": np.eye(P).astype(bf16),
        "row_mask": np.where(c > r, -BIG, 0.0).astype(bf16),
        "step": step, "shift": np.concatenate([beyond, 0 * beyond, beyond], 1),
        "before": np.where(r < c, 1.0, 0.0).astype(bf16),
        "multiples": np.broadcast_to(np.arange(NT, dtype=np.float32) * P, (P, NT)).copy(),
        "upto": np.broadcast_to((e[None, :] <= e[:, None]).astype(np.float32), (P, E, E)).copy(),
        "block_no": np.arange(BLOCKS, dtype=np.float32)[None],
        "token_no": (np.arange(NT)[None] * P + np.arange(P)[:, None]).astype(np.uint32),
        "pick": pick.astype(bf16),
        "cos": np.concatenate([cos, cos], 1).reshape(QT, P, HD0).transpose(1, 0, 2).copy(),
        "sin": np.concatenate([-sin, sin], 1).reshape(QT, P, HD0).transpose(1, 0, 2).copy(),
    }


def layout(inputs):
    g = {k: np.asarray(v) for k, v in inputs.items()}
    wq = g["L0_attn_Wq"].reshape(D, 2, 4, 4, HD0).transpose(0, 1, 3, 2, 4).reshape(D, D)
    full = HID // P * P
    w1 = g["L0_ffn_w1"]
    return {
        "x": g["L0_attn_x"],
        "wqkv0": np.concatenate([wq, g["L0_attn_Wk"], g["L0_attn_Wv"]], 1),
        "wo0": g["L0_attn_Wo"],
        "norm_w": g["L0_ffn_norm_w"][None], "gate_w": g["L0_ffn_gate_w"].T, "gate_b": g["L0_ffn_gate_b"][None],
        "w1": w1.reshape(E, I, 2, D).transpose(3, 0, 2, 1).reshape(D, E * 2 * I),
        "w2": g["L0_ffn_w2"].transpose(2, 0, 1).reshape(I, E * D),
        "b12": np.concatenate([g["L0_ffn_b1"].reshape(E, I, 2).transpose(0, 2, 1).reshape(E, 2 * I),
                               g["L0_ffn_b2"]], 1),
        "wqkv1": np.concatenate([g["L1_attn_wq"].T, g["L1_attn_wk"].T, g["L1_attn_wv"].T], 1),
        "wo1": g["L1_attn_wo"].T,
        "w_gate": g["L1_ffn_wq_gate"].T, "w_up": g["L1_ffn_wq_up"].T, "w_down": g["L1_ffn_wq_down"].T,
        **{name + end: part for name in ("s_gate", "s_up") for end, part in (
            ("", g["L1_ffn_" + name][:full].reshape(-1, P).T), ("_rest", g["L1_ffn_" + name][full:, None]))},
        "s_down": g["L1_ffn_s_down"][None],
    }


def kernel(**inputs):
    import concourse.bacc as bacc
    from concourse.bass_utils import run_bass_kernel_spmd

    nc = bacc.Bacc("TRN2", target_bir_lowering=False, num_devices=1)
    arrays, a = {}, {}
    for name, v in {**layout(inputs), **constants()}.items():
        v = np.ascontiguousarray(v)
        arrays[f"in_{name}"] = v
        a[name] = nc.dram_tensor(f"in_{name}", v.shape, mybir.dt.from_np(v.dtype), kind="ExternalInput").ap()
    out = nc.dram_tensor("out_x", [B, T, D], F32, kind="ExternalOutput").ap()
    build(nc, a, out)
    r = run_bass_kernel_spmd(nc, [arrays], core_ids=[0])
    return r.results[0]["out_x"]
```
